# Optimizing a Trainium2 kernel written in Bass

```python
import numpy as np
import jax
import jax.numpy as jnp

def _softmax(x, axis=-1):
    return jax.nn.softmax(x, axis=axis)

def _gelu(x):
    return jax.nn.gelu(x, approximate=True)

def _silu(x):
    return jax.nn.silu(x)

def _sigmoid(x):
    return jax.nn.sigmoid(x)

def _layernorm(x, axis=-1, eps=1e-05):
    m = jnp.mean(x, axis=axis, keepdims=True)
    v = jnp.var(x, axis=axis, keepdims=True)
    return (x - m) / jnp.sqrt(v + eps)

def _scatter_add(tgt, idx, src, axis=0):
    return tgt.at[idx].add(src)

def _segment_sum(src, seg, n):
    return jax.ops.segment_sum(src, seg, n)
kernel_name = 'mk_adaln_ffn_d2_seqx_r8_0a114b'

def setup_inputs(seed: int=0):
    np.random.seed(seed)
    _w = jnp.asarray

    def _rec_inputs():
        import jax
        import jax.numpy as jnp
        _rk = jax.random.key(seed)
        x = -0.000125 + 0.9999 * jax.random.normal(jax.random.fold_in(_rk, 1), (32, 32, 256), jnp.float32)
        _lenS = 32 - jax.random.randint(jax.random.fold_in(_rk, 7), (32,), 0, max(1, 32 // 4) + 1, jnp.int32)
        _lenS2 = 32 - jax.random.randint(jax.random.fold_in(_rk, 8), (32,), 0, max(1, 32 // 4) + 1, jnp.int32)
        cond_2048 = 0.000782532 + 0.100527 * jax.random.normal(jax.random.fold_in(_rk, 11), (32, 256), jnp.float32)
        return (x, cond_2048)
    x, cond_2048 = _rec_inputs()

    def _L0_cond_setup():
        import jax, jax.numpy as jnp
        import numpy as np
        key = jax.random.key(seed)
        k1, k2, k3 = jax.random.split(key, 3)
        B, L, D, K = (4, 512, 256, 4)
        x = jax.random.normal(k1, (B, L, D), dtype=jnp.float32)
        w = jax.random.normal(k2, (K, 1, D), dtype=jnp.float32) * 0.1
        b = jax.random.normal(k3, (D,), dtype=jnp.float32) * 0.1
        return {'x': x, 'w': w, 'b': b}
    _L0_cond_all = _L0_cond_setup()
    _L0_cond_in = {k: v for k, v in _L0_cond_all.items() if k in ('b',)}
    del _L0_cond_all

    def _L0_ffn_setup():
        import jax, jax.numpy as jnp
        import numpy as np
        ROPE_THETA = 1000000.0
        TOP_K = 2

        def rmsnorm(x, w, eps=1e-06):
            xf = x.astype(jnp.float32)
            n = jax.lax.rsqrt(jnp.mean(xf * xf, axis=-1, keepdims=True) + eps)
            return (xf * n).astype(x.dtype) * w

        def rope_tables(seq_len, head_dim):
            freqs = 1.0 / ROPE_THETA ** (jnp.arange(0, head_dim, 2, dtype=jnp.float32) / head_dim)
            t = jnp.arange(seq_len, dtype=jnp.float32)
            f = jnp.outer(t, freqs)
            return (jnp.cos(f), jnp.sin(f))

        def apply_rope(x, cos, sin):
            half = x.shape[-1] // 2
            x1, x2 = (x[..., :half], x[..., half:])
            c = cos[None, None]
            s = sin[None, None]
            return jnp.concatenate([x1 * c - x2 * s, x2 * c + x1 * s], axis=-1)
        key = jax.random.key(seed)
        ks = jax.random.split(key, 8)
        B, S, D = (2, 256, 256)
        Hq, Hkv, hd = (16, 4, 128)
        E, I = (8, 176)
        sc = 0.02
        return {'hidden': jax.random.normal(ks[0], (B, S, D), jnp.float32), 'attn_norm_w': jnp.ones((D,), jnp.float32), 'q_w': jax.random.normal(ks[1], (Hq * hd, D), jnp.float32) * sc, 'k_w': jax.random.normal(ks[2], (Hkv * hd, D), jnp.float32) * sc, 'v_w': jax.random.normal(ks[3], (Hkv * hd, D), jnp.float32) * sc, 'o_w': jax.random.normal(ks[4], (D, Hq * hd), jnp.float32) * sc, 'q_norm_w': jnp.ones((hd,), jnp.float32), 'k_norm_w': jnp.ones((hd,), jnp.float32), 'ffn_norm_w': jnp.ones((D,), jnp.float32), 'gate_w': jax.random.normal(ks[5], (E, D), jnp.float32) * sc, 'wg': jax.random.normal(ks[6], (E, I, D), jnp.float32) * sc, 'wu': jax.random.normal(ks[7], (E, I, D), jnp.float32) * sc, 'wd': jax.random.normal(jax.random.fold_in(key, 99), (E, D, I), jnp.float32) * sc}
    _L0_ffn_all = _L0_ffn_setup()
    _L0_ffn_in = {k: v for k, v in _L0_ffn_all.items() if k in ('attn_norm_w', 'q_w', 'k_w', 'v_w', 'o_w', 'q_norm_w', 'k_norm_w', 'ffn_norm_w', 'gate_w', 'wg', 'wu', 'wd')}
    del _L0_ffn_all

    def _L1_cond_setup():
        import jax, jax.numpy as jnp
        import numpy as np
        DIM = 256
        H = 16
        DH = 128
        INNER = H * DH
        MLP = 4 * DIM
        B, T = (2, 256)
        EPS = 1e-06

        def _ln(x):
            mu = jnp.mean(x, axis=-1, keepdims=True)
            var = jnp.var(x, axis=-1, keepdims=True)
            return (x - mu) * jax.lax.rsqrt(var + EPS)
        key = jax.random.key(seed)
        ks = jax.random.split(key, 12)
        s = 0.02
        return {'x': jax.random.normal(ks[0], (B, T, DIM), jnp.float32), 'timestep_embed': jax.random.normal(ks[1], (B, DIM), jnp.float32), 'ada_w': jax.random.normal(ks[2], (DIM, 6 * DIM), jnp.float32) * s, 'ada_b': jnp.zeros((6 * DIM,), jnp.float32), 'qkv_w': jax.random.normal(ks[3], (DIM, 3 * INNER), jnp.float32) * s, 'qkv_b': jnp.zeros((3 * INNER,), jnp.float32), 'out_w': jax.random.normal(ks[4], (INNER, DIM), jnp.float32) * s, 'out_b': jnp.zeros((DIM,), jnp.float32), 'ffn_w1': jax.random.normal(ks[5], (DIM, MLP), jnp.float32) * s, 'ffn_b1': jnp.zeros((MLP,), jnp.float32), 'ffn_w2': jax.random.normal(ks[6], (MLP, DIM), jnp.float32) * s, 'ffn_b2': jnp.zeros((DIM,), jnp.float32)}
    _L1_cond_all = _L1_cond_setup()
    _L1_cond_in = {k: v for k, v in _L1_cond_all.items() if k in ('ada_w', 'ada_b', 'qkv_w', 'qkv_b', 'out_w', 'out_b', 'ffn_w1', 'ffn_b1', 'ffn_w2', 'ffn_b2')}
    del _L1_cond_all

    def _L1_ffn_setup():
        import jax, jax.numpy as jnp
        import numpy as np
        RANK = 64
        SCALING = 1.0 / RANK
        TEMPERATURE = 1.0
        key = jax.random.key(seed)
        k_x, k_a, k_b, k_w = jax.random.split(key, 4)
        B_, S, D = (4, 256, 256)
        E, R, O = (8, RANK, 256)
        x = jax.random.normal(k_x, (B_, S, D), dtype=jnp.float32)
        A = jax.random.normal(k_a, (E, R, D), dtype=jnp.float32) * (1.0 / np.sqrt(D))
        Bw = jax.random.normal(k_b, (E, O, R), dtype=jnp.float32) * 0.02
        Wr = jax.random.normal(k_w, (E, D), dtype=jnp.float32) * (1.0 / np.sqrt(D))
        br = jnp.zeros((E,), dtype=jnp.float32)
        return {'x': x, 'A': A, 'B': Bw, 'Wr': Wr, 'br': br}
    _L1_ffn_all = _L1_ffn_setup()
    _L1_ffn_in = {k: v for k, v in _L1_ffn_all.items() if k in ('A', 'B', 'Wr', 'br')}
    del _L1_ffn_all
    return {'x': x, 'cond_2048': cond_2048, 'L0_cond_b': _L0_cond_in['b'], 'L0_ffn_attn_norm_w': _L0_ffn_in['attn_norm_w'], 'L0_ffn_q_w': _L0_ffn_in['q_w'], 'L0_ffn_k_w': _L0_ffn_in['k_w'], 'L0_ffn_v_w': _L0_ffn_in['v_w'], 'L0_ffn_o_w': _L0_ffn_in['o_w'], 'L0_ffn_q_norm_w': _L0_ffn_in['q_norm_w'], 'L0_ffn_k_norm_w': _L0_ffn_in['k_norm_w'], 'L0_ffn_ffn_norm_w': _L0_ffn_in['ffn_norm_w'], 'L0_ffn_gate_w': _L0_ffn_in['gate_w'], 'L0_ffn_wg': _L0_ffn_in['wg'], 'L0_ffn_wu': _L0_ffn_in['wu'], 'L0_ffn_wd': _L0_ffn_in['wd'], 'L1_cond_ada_w': _L1_cond_in['ada_w'], 'L1_cond_ada_b': _L1_cond_in['ada_b'], 'L1_cond_qkv_w': _L1_cond_in['qkv_w'], 'L1_cond_qkv_b': _L1_cond_in['qkv_b'], 'L1_cond_out_w': _L1_cond_in['out_w'], 'L1_cond_out_b': _L1_cond_in['out_b'], 'L1_cond_ffn_w1': _L1_cond_in['ffn_w1'], 'L1_cond_ffn_b1': _L1_cond_in['ffn_b1'], 'L1_cond_ffn_w2': _L1_cond_in['ffn_w2'], 'L1_cond_ffn_b2': _L1_cond_in['ffn_b2'], 'L1_ffn_A': _L1_ffn_in['A'], 'L1_ffn_B': _L1_ffn_in['B'], 'L1_ffn_Wr': _L1_ffn_in['Wr'], 'L1_ffn_br': _L1_ffn_in['br']}

def reference(x, cond_2048, L0_cond_b, L0_ffn_attn_norm_w, L0_ffn_q_w, L0_ffn_k_w, L0_ffn_v_w, L0_ffn_o_w, L0_ffn_q_norm_w, L0_ffn_k_norm_w, L0_ffn_ffn_norm_w, L0_ffn_gate_w, L0_ffn_wg, L0_ffn_wu, L0_ffn_wd, L1_cond_ada_w, L1_cond_ada_b, L1_cond_qkv_w, L1_cond_qkv_b, L1_cond_out_w, L1_cond_out_b, L1_cond_ffn_w1, L1_cond_ffn_b1, L1_cond_ffn_w2, L1_cond_ffn_b2, L1_ffn_A, L1_ffn_B, L1_ffn_Wr, L1_ffn_br):
    import jax
    import jax.numpy as jnp

    def _L0_cond_ref(x, w, b):
        import jax, jax.numpy as jnp
        import numpy as np
        'Depthwise causal conv1d, channel-last.\n            x: (B, L, D); w: (K, 1, D); b: (D,). Returns (B, L, D).\n            Matches torch: Conv1d(D, D, K, groups=D, padding=K-1)(x.T)[..., :L].T\n            which is exactly a causal conv (left pad K-1, trim to L).\n            '
        K = w.shape[0]
        D = x.shape[-1]
        y = jax.lax.conv_general_dilated(x, w, window_strides=(1,), padding=[(K - 1, 0)], feature_group_count=D, dimension_numbers=('NWC', 'WIO', 'NWC'))
        return y + b

    def _L0_ffn_ref(hidden, attn_norm_w, q_w, k_w, v_w, o_w, q_norm_w, k_norm_w, ffn_norm_w, gate_w, wg, wu, wd):
        import jax, jax.numpy as jnp
        import numpy as np
        ROPE_THETA = 1000000.0
        TOP_K = 2

        def rmsnorm(x, w, eps=1e-06):
            xf = x.astype(jnp.float32)
            n = jax.lax.rsqrt(jnp.mean(xf * xf, axis=-1, keepdims=True) + eps)
            return (xf * n).astype(x.dtype) * w

        def rope_tables(seq_len, head_dim):
            freqs = 1.0 / ROPE_THETA ** (jnp.arange(0, head_dim, 2, dtype=jnp.float32) / head_dim)
            t = jnp.arange(seq_len, dtype=jnp.float32)
            f = jnp.outer(t, freqs)
            return (jnp.cos(f), jnp.sin(f))

        def apply_rope(x, cos, sin):
            half = x.shape[-1] // 2
            x1, x2 = (x[..., :half], x[..., half:])
            c = cos[None, None]
            s = sin[None, None]
            return jnp.concatenate([x1 * c - x2 * s, x2 * c + x1 * s], axis=-1)
        B, S, D = hidden.shape
        hd = q_norm_w.shape[0]
        Hq = q_w.shape[0] // hd
        Hkv = k_w.shape[0] // hd
        n_rep = Hq // Hkv
        h = rmsnorm(hidden, attn_norm_w)
        q = (h @ q_w.T).reshape(B, S, Hq, hd)
        k = (h @ k_w.T).reshape(B, S, Hkv, hd)
        v = (h @ v_w.T).reshape(B, S, Hkv, hd)
        q = rmsnorm(q, q_norm_w).transpose(0, 2, 1, 3)
        k = rmsnorm(k, k_norm_w).transpose(0, 2, 1, 3)
        v = v.transpose(0, 2, 1, 3)
        cos, sin = rope_tables(S, hd)
        q = apply_rope(q, cos, sin)
        k = apply_rope(k, cos, sin)
        k = jnp.repeat(k, n_rep, axis=1)
        v = jnp.repeat(v, n_rep, axis=1)
        scale = 1.0 / jnp.sqrt(jnp.float32(hd))
        scores = jnp.einsum('bhqd,bhkd->bhqk', q, k) * scale
        causal = jnp.tril(jnp.ones((S, S), bool))
        scores = jnp.where(causal[None, None], scores, jnp.finfo(scores.dtype).min)
        attn = jnp.einsum('bhqk,bhkd->bhqd', jax.nn.softmax(scores, axis=-1), v)
        attn = attn.transpose(0, 2, 1, 3).reshape(B, S, Hq * hd)
        hidden = hidden + attn @ o_w.T
        h2 = rmsnorm(hidden, ffn_norm_w)
        T = B * S
        E = gate_w.shape[0]
        tok = h2.reshape(T, D)
        probs = jax.nn.softmax(tok @ gate_w.T, axis=-1)
        topv, topi = jax.lax.top_k(probs, TOP_K)
        topw = topv / (jnp.sum(topv, axis=-1, keepdims=True) + 1e-09)
        combine = jnp.zeros((T, E), tok.dtype).at[jnp.arange(T)[:, None], topi].set(topw)
        eg = jnp.einsum('td,eid->eti', tok, wg)
        eu = jnp.einsum('td,eid->eti', tok, wu)
        eo = jnp.einsum('eti,edi->etd', jax.nn.silu(eg) * eu, wd)
        moe_out = jnp.einsum('te,etd->td', combine, eo).reshape(B, S, D)
        return hidden + moe_out

    def _L1_cond_ref(x, timestep_embed, ada_w, ada_b, qkv_w, qkv_b, out_w, out_b, ffn_w1, ffn_b1, ffn_w2, ffn_b2):
        import jax, jax.numpy as jnp
        import numpy as np
        DIM = 256
        H = 16
        DH = 128
        INNER = H * DH
        MLP = 4 * DIM
        B, T = (2, 256)
        EPS = 1e-06

        def _ln(x):
            mu = jnp.mean(x, axis=-1, keepdims=True)
            var = jnp.var(x, axis=-1, keepdims=True)
            return (x - mu) * jax.lax.rsqrt(var + EPS)
        Bc, Tc, D = x.shape
        ada = (timestep_embed @ ada_w + ada_b)[:, None, :]
        shift1, scale1, gate1, shift2, scale2, gate2 = jnp.split(ada, 6, axis=-1)
        x1 = _ln(x) * (1.0 + scale1) + shift1
        qkv = (x1 @ qkv_w + qkv_b).reshape(Bc, Tc, 3, H, DH)
        q, k, v = (qkv[:, :, 0], qkv[:, :, 1], qkv[:, :, 2])
        scale = DH ** (-0.5)
        attn = jnp.einsum('bthd,bshd->bhts', q, k) * scale
        attn = jax.nn.softmax(attn, axis=-1)
        attn_out = jnp.einsum('bhts,bshd->bthd', attn, v).reshape(Bc, Tc, INNER)
        attn_out = attn_out @ out_w + out_b
        x = x + gate1 * attn_out
        x2 = _ln(x) * (1.0 + scale2) + shift2
        h = jax.nn.gelu(x2 @ ffn_w1 + ffn_b1, approximate=False)
        x = x + gate2 * (h @ ffn_w2 + ffn_b2)
        return x

    def _L1_ffn_ref(x, A, B, Wr, br):
        import jax, jax.numpy as jnp
        import numpy as np
        RANK = 64
        SCALING = 1.0 / RANK
        TEMPERATURE = 1.0
        batch, seq, d = x.shape
        E, out_dim = (B.shape[0], B.shape[1])
        x_flat = x.reshape(-1, d)
        logits = (x_flat @ Wr.T + br) / TEMPERATURE
        probs = jax.nn.softmax(logits, axis=-1)
        expert_idx = jnp.argmax(probs, axis=-1)
        expert_weight = jnp.max(probs, axis=-1)
        h = jnp.einsum('nd,erd->ner', x_flat, A)
        y = jnp.einsum('ner,eor->neo', h, B) * SCALING
        sel = jnp.take_along_axis(y, expert_idx[:, None, None], axis=1)[:, 0, :]
        out_flat = sel * expert_weight[:, None]
        return out_flat.reshape(batch, seq, out_dim)
    x = x + _L0_ffn_ref(_L0_cond_ref(x, cond_2048[:, None, :], L0_cond_b), L0_ffn_attn_norm_w, L0_ffn_q_w, L0_ffn_k_w, L0_ffn_v_w, L0_ffn_o_w, L0_ffn_q_norm_w, L0_ffn_k_norm_w, L0_ffn_ffn_norm_w, L0_ffn_gate_w, L0_ffn_wg, L0_ffn_wu, L0_ffn_wd)
    x = x + _L1_ffn_ref(_L1_cond_ref(x, cond_2048, L1_cond_ada_w, L1_cond_ada_b, L1_cond_qkv_w, L1_cond_qkv_b, L1_cond_out_w, L1_cond_out_b, L1_cond_ffn_w1, L1_cond_ffn_b1, L1_cond_ffn_w2, L1_cond_ffn_b2), L1_ffn_A, L1_ffn_B, L1_ffn_Wr, L1_ffn_br)
    return x

_drawn_inputs = setup_inputs


def setup_inputs(seed=0):
    import zlib

    import numpy as np

    out = dict(_drawn_inputs(seed))
    spreads = {'L0_ffn_attn_norm_w': (1.0, 0.2),
     'L0_ffn_q_norm_w': (1.0, 0.6),
     'L0_ffn_k_norm_w': (1.0, 0.6),
     'L0_ffn_ffn_norm_w': (1.0, 0.6),
     'L1_cond_ada_b': (0.0, 0.8),
     'L1_cond_qkv_b': (0.0, 0.8),
     'L1_cond_out_b': (0.0, 0.8),
     'L1_cond_ffn_b1': (0.0, 0.8),
     'L1_cond_ffn_b2': (0.0, 0.8),
     'L1_ffn_br': (0.0, 2.0)}
    factors = {'L0_ffn_gate_w': 7.096,
     'L0_ffn_wg': 6.09,
     'L0_ffn_wu': 6.048,
     'L0_ffn_wd': 6.005,
     'L1_cond_ada_w': 8.0,
     'L1_cond_qkv_w': 8.0,
     'L1_cond_out_w': 8.0,
     'L1_cond_ffn_w1': 8.0,
     'L1_cond_ffn_w2': 8.0,
     'L1_ffn_A': 8.0,
     'L1_ffn_B': 8.0,
     'L1_ffn_Wr': 8.0}
    for name, (base, spread) in spreads.items():
        noise = np.random.default_rng([zlib.crc32(name.encode()), seed]).standard_normal(out[name].shape)
        drawn = base * np.exp(spread * noise) if base else spread * noise
        out[name] = jnp.asarray(drawn.astype(out[name].dtype))
    for name, factor in factors.items():
        out[name] = (out[name] * factor).astype(out[name].dtype)
    return out
```

```python
from contextlib import ExitStack

import numpy as np

import concourse.bass as bass
from concourse import mybir

ALU = mybir.AluOpType
ACT = mybir.ActivationFunctionType
F32 = mybir.dt.float32
U32 = mybir.dt.uint32
AX_X = mybir.AxisListType.X

P = 128
D = 256
DH = 128
DK = D // P
BATCH, SEQ = 32, 32
TOK = BATCH * SEQ
TILES = TOK // P
BT = P // SEQ
HQ, HKV = 16, 4
REP = HQ // HKV
BANK = 512
CHUNKS = TOK // BANK
CB = BANK // SEQ
CT = BANK // P
QKV0 = 2 * HKV * DH + HQ * DH
NPROJ = QKV0 // BANK
NE, INTER = 8, 176
EI = NE * INTER
MI = EI // P
GROUPS = HQ // 4
MLP = 4 * D
MM = MLP // P
RANK = 64
ER = NE * RANK
MR = ER // P
NADA = 6 * DK
NEG = -1.0e30

COLS = {}
_at = 0
for _name, _n in (("convw", DK * SEQ), ("convb", DK), ("anw", DK), ("fnw", DK), ("adab", NADA),
                  ("bq", HQ), ("bk", HQ), ("bv", HQ), ("outb", DK), ("b1", MM), ("b2", DK), ("br", NE)):
    COLS[_name] = (_at, _at + _n)
    _at += _n
NCOLS = _at
CONSTS = {}
_at = 0
for _name, _n in (("ident", P), ("cos", DH), ("sin", DH), ("causal", SEQ), ("iota", NE)):
    CONSTS[_name] = (_at, _at + _n)
    _at += _n
NCONSTS = _at


def build_program(nc, x_tok, x_T, cond_T, cols, consts, rope_w, expert_rows, w_qkv0, w_o0, w_gate0,
                  w_g, w_u, w_d, w_ada, w_qkv1, w_o1, w_1, w_2, w_a, w_b, w_r, out):
    with ExitStack() as ctx:
        def sb(name, shape, dt=F32):
            return ctx.enter_context(nc.sbuf_tensor(name, shape, dt))

        def sem(name):
            return ctx.enter_context(nc.semaphore(name))

        qkv_o_w = sb("qkv_o_w", [P, DK * QKV0 + HQ * D])
        ffn_w = sb("ffn_w", [P, 2 * DK * EI + MI * D])
        col = sb("col", [P, NCOLS])
        cst = sb("cst", [P, NCONSTS])
        tables = sb("tables", [P, 4, DH])
        erows = sb("erows", [NE, EI + ER])
        gate_w = sb("gate_w", [P, DK, NE])
        r_w = sb("r_w", [P, DK, NE])
        cond = sb("cond", [P, DK, BATCH])
        ada = sb("ada", [P, NADA, BATCH])
        xT = sb("xT", [P, DK, TOK])
        yT = sb("yT", [P, DK, TOK])
        ywT = sb("ywT", [P, DK, TOK])
        hid = sb("hid", [P, TILES, D])
        xres = sb("xres", [P, TILES, D])
        work = sb("work", [P, 11776])
        bd = sb("bd", [P, 2, 16, BT, SEQ])
        attnT = sb("attnT", [P, 4 * BANK])
        sm_s = sb("sm_s", [P, 16, SEQ])
        ropew = sm_s[:].rearrange("p h k -> p (h k)").rearrange("p (i d) -> p i d", i=4)
        sm_e = sb("sm_e", [P, 16, SEQ])
        sm_m = sb("sm_m", [P, 16])
        sm_d = sb("sm_d", [P, 16])
        sm_r = sb("sm_r", [P, 16])
        stat = sb("stat", [P, 64])
        half = sb("half", [P, 32])
        ssq = sb("ssq", [P, 2, 20])
        nrm = sb("nrm", [P, 2, 20])
        nrt = sb("nrt", [P, 2, 20])
        junk = sb("junk", [P, 3, D])
        rt = sb("rt", [P, 10, TILES, NE])
        ridx = sb("ridx", [P, TILES, 8], U32)
        bst = sb("bst", [P, TILES, 8])

        ps = ctx.enter_context(nc.psum_tensor("ps", [P, 8, BANK], F32))

        def c_(name, k=0, n=1):
            return col[:, COLS[name][0] + k:COLS[name][0] + k + n]

        def k_(name):
            return cst[:, CONSTS[name][0]:CONSTS[name][1]]

        ident = k_("ident")
        wqkv0 = qkv_o_w[:, 0:DK * QKV0].rearrange("p (m n) -> p m n", m=DK)
        wo = qkv_o_w[:, DK * QKV0:].rearrange("p (h n) -> p h n", h=HQ)
        G1 = DK * 3 * BANK
        wqkv1 = [qkv_o_w[:, i * G1:(i + 1) * G1].rearrange("p (m s n) -> p m s n", m=DK, s=3) for i in range(2)]
        assert 2 * G1 == DK * QKV0
        wada = ffn_w[:, 0:DK * 6 * D].rearrange("p (m n) -> p m n", m=DK)
        wg = ffn_w[:, 0:DK * EI].rearrange("p (m n) -> p m n", m=DK)
        wu = ffn_w[:, DK * EI:2 * DK * EI].rearrange("p (m n) -> p m n", m=DK)
        wd = ffn_w[:, 2 * DK * EI:].rearrange("p (m n) -> p m n", m=MI)
        o = 0
        w1 = ffn_w[:, o:o + DK * MLP].rearrange("p (m n) -> p m n", m=DK); o += DK * MLP
        w2 = ffn_w[:, o:o + MM * D].rearrange("p (m n) -> p m n", m=MM); o += MM * D
        wa = ffn_w[:, o:o + DK * ER].rearrange("p (m n) -> p m n", m=DK); o += DK * ER
        wb = ffn_w[:, o:o + MR * D].rearrange("p (m n) -> p m n", m=MR)

        def carve(sizes):
            at, found = 0, []
            for n in sizes:
                found.append(work[:, at:at + n])
                at += n
            assert at <= 11776, at
            return found

        NQK = QKV0 - BANK
        raw_, qr_, kn, r2, qkT, v0_ = carve([3 * BANK, 2 * NQK, BANK, BANK, NQK, 3 * BANK])
        raw = raw_.rearrange("p (r n) -> p r n", r=3)
        qr = qr_.rearrange("p (r n) -> p r n", r=2)
        v0 = v0_.rearrange("p (r n) -> p r n", r=3)
        h2T_, cmbT_, sg_, hu_, hm_, hn_ = carve([DK * TOK, TOK, 2 * BANK, 2 * BANK, 2 * BANK, 2 * D])
        h2T = h2T_.rearrange("p (m n) -> p m n", m=DK)
        sg = sg_.rearrange("p (r n) -> p r n", r=2)
        hu = hu_.rearrange("p (r n) -> p r n", r=2)
        hm = hm_.rearrange("p (r n) -> p r n", r=2)
        hn = hn_.rearrange("p (r n) -> p r n", r=2)
        qT1, kT1, v1_, z_ = carve([4 * BANK, 4 * BANK, 2 * 4 * BANK, 2 * D])
        v1 = v1_.rearrange("p (r t n) -> p r t n", r=2, t=CT)
        z = z_.rearrange("p (r n) -> p r n", r=2)
        gT_, x2s_, z2_, hT_, hw_, ln_, fin_ = carve([MM * BANK, 2 * D, 2 * D, 2 * BANK, 2 * BANK, BANK, 2 * D])
        gT = gT_.rearrange("p (m n) -> p m n", m=MM)
        x2s = x2s_.rearrange("p (r n) -> p r n", r=2)
        z2 = z2_.rearrange("p (r n) -> p r n", r=2)
        hw = hw_.rearrange("p (r n) -> p r n", r=2)
        lw = ln_.rearrange("p (r n) -> p r n", r=1)
        fin = fin_.rearrange("p (r n) -> p r n", r=2)
        hT = hT_.rearrange("p (r n) -> p r n", r=2)
        hmk = bd[:].rearrange("p r a b c -> p (r a b c)")[:, 0:4 * BANK].rearrange("p (m n) -> p m n", m=MR)

        def batches(ap, n):
            return ap.rearrange("p (b l) -> p b l", b=n)

        def over(ap, n):
            return ap.unsqueeze(2).broadcast_to([ap.shape[0], ap.shape[1], n])

        def rep(ap, n):
            return ap.unsqueeze(1).broadcast_to([ap.shape[0], n, ap.shape[1]])

        ld_x, ld_cols, ld_consts, ld_ada, ld_qkv0, ld_o0, ld_small, ld_xtok = [
            sem("ld_" + n) for n in ("x", "cols", "consts", "ada", "qkv0", "o0", "small", "xtok")]
        ld_moe, ld_qkv1, ld_o1, ld_ffn1 = [sem("ld_" + n) for n in ("moe", "qkv1", "o1", "ffn1")]
        ld_qkv1b = sem("ld_qkv1b")
        stored = sem("stored")
        s_half_set = sem("half_set")
        s_pool_chain = sem("pool_chain")
        s_dve_chain = sem("dve_chain")
        s_conv_step = sem("conv_step")
        s_yw_ready = sem("yw_ready")
        s_tables_ready = sem("tables_ready")
        s_bd_zero = sem("bd_zero")
        s_ada_mm = sem("ada_mm")
        s_ada_ready = sem("ada_ready")
        s_ytok_T = sem("ytok_T")
        s_ytok_copied = sem("ytok_copied")
        s_yrstd = sem("yrstd")
        s_proj0 = sem("proj0")
        s_raw_ready = sem("raw_ready")
        s_v0_ready = sem("v0_ready")
        s_squares = sem("squares")
        s_nrm_ready = sem("nrm_ready")
        s_roped = sem("roped")
        s_qkT_in_psum = sem("qkT_in_psum")
        s_qkT_copied = sem("qkT_copied")
        s_s0 = sem("s0")
        s_s0_taken = sem("s0_taken")
        s_s0_shifted = sem("s0_shifted")
        s_e0 = sem("e0")
        s_bd0 = sem("bd0")
        s_pv0 = sem("pv0")
        s_pv0_copied = sem("pv0_copied")
        s_o0 = sem("o0")
        s_hid_attn = sem("hid_attn")
        s_frstd = sem("frstd")
        s_hn_ready = sem("hn_ready")
        s_hnT = sem("hnT")
        s_h2_ready = sem("h2_ready")
        s_glog = sem("glog")
        s_gsh = sem("gsh")
        s_gexp = sem("gexp")
        s_comb = sem("comb")
        s_combT_psum = sem("combT_psum")
        s_combT_ready = sem("combT_ready")
        s_moe_g = sem("moe_g")
        s_moe_u = sem("moe_u")
        s_moe_c = sem("moe_c")
        s_sg_ready = sem("sg_ready")
        s_hu_ready = sem("hu_ready")
        s_hm_ready = sem("hm_ready")
        s_hm_used = sem("hm_used")
        s_x1_ready = sem("x1_ready")
        s_lnst = sem("lnst")
        s_lrstd = sem("lrstd")
        s_z_ready = sem("z_ready")
        s_zT = sem("zT")
        s_xT1_copied = sem("xT1_copied")
        s_xn1_ready = sem("xn1_ready")
        s_proj1 = sem("proj1")
        s_q1_copied = sem("q1_copied")
        s_s1 = sem("s1")
        s_s1_taken = sem("s1_taken")
        s_s1_shifted = sem("s1_shifted")
        s_e1 = sem("e1")
        s_bd1 = sem("bd1")
        s_pv1 = sem("pv1")
        s_pv1_copied = sem("pv1_copied")
        s_o1 = sem("o1")
        s_acc1 = sem("acc1")
        s_x2_ready = sem("x2_ready")
        s_x2T_psum = sem("x2T_psum")
        s_x2s_copied = sem("x2s_copied")
        s_ln2st = sem("ln2st")
        s_l2rstd = sem("l2rstd")
        s_z2_ready = sem("z2_ready")
        s_z2T = sem("z2T")
        s_xn3_ready = sem("xn3_ready")
        s_ffn1 = sem("ffn1")
        s_gelu = sem("gelu")
        s_ffn2 = sem("ffn2")
        s_x4_ready = sem("x4_ready")
        s_rlog = sem("rlog")
        s_rsh = sem("rsh")
        s_rexp = sem("rexp")
        s_wsel = sem("wsel")
        s_wselT = sem("wselT")
        s_wselT_ready = sem("wselT_ready")
        s_lora_h = sem("lora_h")
        s_lora_w = sem("lora_w")
        s_hw_copied = sem("hw_copied")
        s_hmask = sem("hmask")
        s_lora_y = sem("lora_y")
        s_y_ready = sem("y_ready")

        block = ctx.enter_context(nc.Block())
        QK = NPROJ - 1
        U = GROUPS * CHUNKS

        @block.sync
        def _(sp):
            sp.dma_start(xT[:], x_T).then_inc(ld_x, 16)
            sp.dma_start(col[:], cols).then_inc(ld_cols, 16)
            sp.dma_start(cst[:], consts).then_inc(ld_consts, 16)
            sp.dma_start(cond[:], cond_T).then_inc(ld_ada, 16)
            sp.dma_start(wada, w_ada).then_inc(ld_ada, 16)
            sp.dma_start(ropew, rope_w).then_inc(ld_small, 16)
            sp.dma_start(wqkv0, w_qkv0).then_inc(ld_qkv0, 16)
            sp.dma_start(wo, w_o0).then_inc(ld_o0, 16)
            sp.dma_start(gate_w[:], w_gate0).then_inc(ld_small, 16)
            sp.dma_start(r_w[:], w_r).then_inc(ld_small, 16)
            sp.dma_start(erows[:], expert_rows).then_inc(ld_small, 16)
            sp.dma_start(xres[:], x_tok).then_inc(ld_xtok, 16)
            sp.wait_ge(s_ada_mm, 1)
            sp.dma_start(wg, w_g).then_inc(ld_moe, 16)
            sp.dma_start(wu, w_u).then_inc(ld_moe, 16)
            sp.dma_start(wd, w_d).then_inc(ld_moe, 16)
            sp.wait_ge(s_proj0, TILES * NPROJ)
            sp.dma_start(wqkv1[0], w_qkv1[0]).then_inc(ld_qkv1, 16)
            sp.dma_start(wqkv1[1], w_qkv1[1]).then_inc(ld_qkv1b, 16)
            sp.wait_ge(s_o0, TILES)
            sp.dma_start(wo, w_o1).then_inc(ld_o1, 16)
            sp.wait_ge(s_hm_used, MI * CHUNKS)
            sp.dma_start(w1, w_1).then_inc(ld_ffn1, 16)
            sp.dma_start(w2, w_2).then_inc(ld_ffn1, 16)
            sp.dma_start(wa, w_a).then_inc(ld_ffn1, 16)
            sp.dma_start(wb, w_b).then_inc(ld_ffn1, 16)
            for j in range(2, GROUPS):
                sp.wait_ge(s_proj1, 12 * CHUNKS * (j - 1))
                sp.dma_start(wqkv1[j % 2], w_qkv1[j]).then_inc(ld_qkv1 if j % 2 == 0 else ld_qkv1b, 16)
            for t in range(TILES):
                sp.wait_ge(s_y_ready, t + 1)
                sp.dma_start(out[:, t, :], xres[:, t, :]).then_inc(stored, 16)
            sp.wait_ge(stored, 16 * TILES)

        @block.gpsimd
        def _(pool):
            done = [0]

            def link(ins):
                done[0] += 1
                ins.then_inc(s_pool_chain, 1)
                pool.wait_ge(s_pool_chain, done[0])

            def inv_root(dst, src, n, scale, eps, done_sem):
                link(nc.gpsimd.tensor_scalar(dst, src, scale, eps, ALU.mult, ALU.add))
                nc.gpsimd.tensor_tensor(dst, dst, half[:, 0:n], ALU.pow).then_inc(done_sem, 1)

            link(nc.gpsimd.memset(half[:], -0.5))
            nc.gpsimd.memset(bd[:], 0.0).then_inc(s_bd_zero, 1)
            for t in range(TILES):
                pool.wait_ge(s_squares, t + 1)
                inv_root(stat[:, 8 + t:9 + t], stat[:, t:t + 1], 1, 1.0 / D, 1e-6, s_yrstd)
            for t in range(TILES):
                r = stat[:, 8 + t:9 + t]
                pool.wait_ge(s_yrstd, t + 1)
                for a, n, k in ((0, HKV, 1), (HKV, HQ, QK)):
                    pool.wait_ge(s_squares, TILES + 4 * (QK * t + k))
                    if t >= 2:
                        pool.wait_ge(s_s0_taken, t - 1)
                        pool.wait_ge(s_roped, QK * (t - 1))
                    dst = nrt[:, t % 2, a:a + n]
                    link(nc.gpsimd.tensor_scalar(dst, ssq[:, t % 2, a:a + n], r, r, ALU.mult, ALU.mult))
                    link(nc.gpsimd.tensor_scalar(dst, dst, 1.0 / DH, 1e-6, ALU.mult, ALU.add))
                    link(nc.gpsimd.tensor_tensor(dst, dst, half[:, 0:n], ALU.pow))
                    nc.gpsimd.tensor_scalar(nrm[:, t % 2, a:a + n], dst, r, 1.0 if a == 0 else DH ** -0.5,
                                            ALU.mult, ALU.mult).then_inc(s_nrm_ready, 1)
            for t in range(TILES):
                pool.wait_ge(s_squares, TILES + 4 * QK * TILES + t + 1)
                inv_root(stat[:, 24 + t:25 + t], stat[:, 16 + t:17 + t], 1, 1.0 / D, 1e-6, s_frstd)
            for t in range(TILES):
                pool.wait_ge(s_lnst, t + 1)
                inv_root(stat[:, 32 + t:33 + t], bst[:, t, 7:8], 1, 1.0, 1e-6, s_lrstd)
            for t in range(TILES):
                pool.wait_ge(s_ln2st, t + 1)
                inv_root(stat[:, 40 + t:41 + t], bst[:, t, 7:8], 1, 1.0, 1e-6, s_l2rstd)

        @block.scalar
        def _(act):
            squares = [0]

            def square(src, n, total):
                if squares[0] >= 3:
                    act.wait_ge(s_squares, squares[0] - 2)
                nc.scalar.activation(junk[:, squares[0] % 3, 0:n], src, ACT.Square,
                                     accum_out=total).then_inc(s_squares, 1)
                squares[0] += 1

            for t in range(TILES):
                act.wait_ge(s_ytok_T, t + 1)
                b = 2 + t % 2
                nc.scalar.activation(hid[:, t, :], ps[:, b, 0:D], ACT.Copy).then_inc(s_ytok_copied, 1)
                square(ps[:, b, 0:D], D, stat[:, t:t + 1])

            def take_proj(t):
                for k in range(NPROJ):
                    n = NPROJ * t + k
                    act.wait_ge(s_proj0, n + 1)
                    src = ps[:, n % 2, :]
                    if k == NPROJ - 1:
                        act.wait_ge(s_yrstd, t + 1)
                        if t >= 3:
                            act.wait_ge(s_pv0, 4 * (t - 2))
                        nc.scalar.activation(v0[:, t % 3, :], src, ACT.Copy,
                                             scale=stat[:, 8 + t:9 + t]).then_inc(s_v0_ready, 1)
                        continue
                    if t >= 2:
                        act.wait_ge(s_nrm_ready, 2 * (t - 1))
                    m = QK * t + k
                    for h in range(4):
                        square(src[:, h * DH:(h + 1) * DH], DH, ssq[:, t % 2, 4 * k + h:4 * k + h + 1])
                    if m >= 3:
                        act.wait_ge(s_roped, m - 2)
                    nc.scalar.activation(raw[:, m % 3, :], src, ACT.Copy).then_inc(s_raw_ready, 1)

            def take_qkT(t):
                if t >= 1:
                    act.wait_ge(s_s0, t)
                for k in range(QK):
                    f = QK * t + k
                    act.wait_ge(s_qkT_in_psum, f + 1)
                    nc.scalar.activation(qkT[:, k * BANK:(k + 1) * BANK], ps[:, 2 + f % 2, :],
                                         ACT.Copy).then_inc(s_qkT_copied, 1)

            def take_pv0(t):
                if t >= 1:
                    act.wait_ge(s_o0, t)
                for j in range(4):
                    n = 4 * t + j
                    act.wait_ge(s_pv0, n + 1)
                    nc.scalar.activation(attnT[:, j * BANK:(j + 1) * BANK], ps[:, 5 + n % 2, :],
                                         ACT.Copy).then_inc(s_pv0_copied, 1)

            def exp0(t):
                act.wait_ge(s_s0_shifted, t + 1)
                nc.scalar.activation(sm_e[:], sm_s[:], ACT.Exp).then_inc(s_e0, 1)

            for s in range(TILES + 2):
                if s < TILES:
                    take_proj(s)
                if 1 <= s <= TILES:
                    take_qkT(s - 1)
                if s >= 2:
                    take_pv0(s - 2)
                if 1 <= s <= TILES:
                    exp0(s - 1)

            for t in range(TILES):
                act.wait_ge(s_hid_attn, t + 1)
                square(hid[:, t, :], D, stat[:, 16 + t:17 + t])
            act.wait_ge(s_gsh, 1)
            nc.scalar.activation(rt[:, 2], rt[:, 1], ACT.Exp).then_inc(s_gexp, 1)
            for c in range(CHUNKS):
                act.wait_ge(s_combT_psum, TILES)
                nc.scalar.activation(cmbT_[0:NE, c * BANK:(c + 1) * BANK], ps[0:NE, 4 + c, :],
                                     ACT.Copy).then_inc(s_combT_ready, 1)
            for n in range(CHUNKS * MI):
                act.wait_ge(s_moe_g, n + 1)
                if n >= 2:
                    act.wait_ge(s_hu_ready, n - 1)
                nc.scalar.activation(sg[:, n % 2, :], ps[:, n % 2, :], ACT.Silu).then_inc(s_sg_ready, 1)

            for t in range(TILES):
                act.wait_ge(s_zT, t + 1)
                src = ps[:, t % 2, 0:D].rearrange("p (m n) -> p m n", m=DK)
                nc.scalar.activation(xT[:, :, t * P:(t + 1) * P], src, ACT.Copy).then_inc(s_xT1_copied, 1)

            def take_proj1(u):
                j = u // CHUNKS
                for k in range(12):
                    n = 12 * u + k
                    act.wait_ge(s_proj1, n + 1)
                    src = ps[:, n % 2, :]
                    if k < 8:
                        if k == 0 and u >= 1:
                            act.wait_ge(s_s1, u)
                        dst, b = (qT1, "bq") if k < 4 else (kT1, "bk")
                        h = k % 4
                        nc.scalar.activation(dst[:, h * BANK:(h + 1) * BANK], src, ACT.Identity,
                                             bias=c_(b, 4 * j + h)).then_inc(s_q1_copied, 1)
                    else:
                        if k == 8 and u >= 2:
                            act.wait_ge(s_pv1, 4 * (u - 1))
                        nc.scalar.activation(v1[:, u % 2, k - 8, :], src, ACT.Copy).then_inc(s_q1_copied, 1)

            def take_pv1(u):
                if u >= 1:
                    act.wait_ge(s_o1, 2 * u)
                for h in range(4):
                    n = 4 * u + h
                    act.wait_ge(s_pv1, n + 1)
                    nc.scalar.activation(attnT[:, h * BANK:(h + 1) * BANK], ps[:, 5 + n % 2, :], ACT.Identity,
                                         bias=c_("bv", 4 * (u // CHUNKS) + h)).then_inc(s_pv1_copied, 1)

            for u in range(U + 1):
                if u < U:
                    take_proj1(u)
                if u >= 1:
                    take_pv1(u - 1)
                if u < U:
                    act.wait_ge(s_s1_shifted, u + 1)
                    nc.scalar.activation(sm_e[:], sm_s[:], ACT.Exp, scale=DH ** -0.5).then_inc(s_e1, 1)

            for t in range(TILES):
                act.wait_ge(s_x2T_psum, t + 1)
                if t >= 2:
                    act.wait_ge(s_z2_ready, t - 1)
                nc.scalar.activation(x2s[:, t % 2, :], ps[:, 2 + t % 2, 0:D], ACT.Copy).then_inc(s_x2s_copied, 1)
            for c in range(CHUNKS):
                for m in range(MM):
                    n = MM * c + m
                    act.wait_ge(s_ffn1, n + 1)
                    if m == 0 and c >= 1:
                        act.wait_ge(s_ffn2, DK * c)
                    nc.scalar.activation(gT[:, m, :], ps[:, n % 2, :], ACT.Gelu,
                                         bias=c_("b1", m)).then_inc(s_gelu, 1)
            act.wait_ge(s_rsh, 1)
            nc.scalar.activation(rt[:, 2], rt[:, 1], ACT.Exp).then_inc(s_rexp, 1)
            act.wait_ge(s_wselT, TILES)
            for c in range(CHUNKS):
                nc.scalar.activation(gT_[0:NE, c * BANK:(c + 1) * BANK], ps[0:NE, 4 + c, :],
                                     ACT.Copy).then_inc(s_wselT_ready, 1)
            for n in range(CHUNKS * MR):
                act.wait_ge(s_lora_w, n + 1)
                if n >= 2:
                    act.wait_ge(s_hmask, n - 1)
                nc.scalar.activation(hw[:, n % 2, :], ps[:, 2 + n % 2, :], ACT.Copy).then_inc(s_hw_copied, 1)

        @block.vector
        def _(dve):
            done = [0]
            V = nc.vector

            def link(ins):
                done[0] += 1
                ins.then_inc(s_dve_chain, 1)
                dve.wait_ge(s_dve_chain, done[0])

            dve.wait_ge(ld_x, 16)
            dve.wait_ge(ld_cols, 16)
            n = 0
            for c in range(CHUNKS):
                for delay in range(SEQ):
                    for m in range(DK):
                        src = batches(xT[:, m, c * BANK:(c + 1) * BANK], CB)
                        dst = batches(yT[:, m, c * BANK:(c + 1) * BANK], CB)
                        tap = c_("convw", m * SEQ + SEQ - 1 - delay)
                        if delay == 0:
                            ins = V.tensor_scalar(dst, src, tap, c_("convb", m), ALU.mult, ALU.add)
                        else:
                            dve.wait_ge(s_conv_step, n - 1)
                            ins = V.scalar_tensor_tensor(dst[:, :, delay:SEQ], src[:, :, 0:SEQ - delay], tap,
                                                         dst[:, :, delay:SEQ], ALU.mult, ALU.add)
                        ins.then_inc(s_conv_step, 1)
                        n += 1
                dve.wait_ge(s_conv_step, n)
                for m in range(DK):
                    V.tensor_scalar(ywT[:, m, c * BANK:(c + 1) * BANK], yT[:, m, c * BANK:(c + 1) * BANK],
                                    c_("anw", m), None, ALU.mult).then_inc(s_yw_ready, 1)
            dve.wait_ge(ld_consts, 16)
            dve.wait_ge(ld_small, 64)
            for i in range(4):
                V.tensor_tensor(tables[:, i, :], k_("cos" if i % 2 == 0 else "sin"), ropew[:, i, :],
                                ALU.mult).then_inc(s_tables_ready, 1)
            dve.wait_ge(s_tables_ready, 4)
            dve.wait_ge(s_ada_mm, 1)
            V.tensor_tensor(ada[:], ps[:, 4, 0:NADA * BATCH].rearrange("p (n b) -> p n b", n=NADA),
                                 over(c_("adab", 0, NADA), BATCH), ALU.add).then_inc(s_ada_ready, 1)
            dve.wait_ge(s_ada_ready, 1)
            for i in (DK, 4 * DK):
                link(V.tensor_scalar(ada[:, i:i + DK, :], ada[:, i:i + DK, :], 1.0, None, ALU.add))

            HD = DH // 2

            def rope(t):
                for k in range(QK):
                    m = QK * t + k
                    dve.wait_ge(s_raw_ready, m + 1)
                    src = raw[:, m % 3, :]
                    i = 0
                    if k == 0:
                        dve.wait_ge(s_nrm_ready, 2 * t + 1)
                        link(V.tensor_tensor(kn.rearrange("p (h d) -> p h d", h=4), src.rearrange("p (h d) -> p h d", h=4),
                                             over(nrm[:, t % 2, 0:HKV], DH), ALU.mult))
                        src = kn
                        i = 2
                        if t >= 2:
                            dve.wait_ge(s_qkT_in_psum, QK * (t - 1))
                    s4 = src.rearrange("p (h d) -> p h d", h=4)
                    q4 = qr[:, t % 2, k * BANK:(k + 1) * BANK].rearrange("p (h d) -> p h d", h=4)
                    r4 = r2.rearrange("p (h d) -> p h d", h=4)
                    V.tensor_tensor(q4, s4, rep(tables[:, i, :], 4), ALU.mult)
                    V.tensor_tensor(r4[:, :, 0:HD], s4[:, :, HD:DH], rep(tables[:, i + 1, 0:HD], 4), ALU.mult)
                    link(V.tensor_tensor(r4[:, :, HD:DH], s4[:, :, 0:HD], rep(tables[:, i + 1, HD:DH], 4), ALU.mult))
                    V.tensor_tensor(q4, q4, r4, ALU.add).then_inc(s_roped, 1)
                    dve.wait_ge(s_roped, m + 1)

            def softmax_tail(e_sem, e_count, slot, bd_sem, pv_sem, pv_count):
                dve.wait_ge(e_sem, e_count)
                link(V.tensor_reduce(sm_d[:], sm_e[:], AX_X, ALU.add))
                link(V.reciprocal(sm_r[:], sm_d[:]))
                link(V.tensor_tensor(sm_e[:], sm_e[:], over(sm_r[:], SEQ), ALU.mult))
                if pv_count:
                    dve.wait_ge(pv_sem, pv_count)
                for b in range(BT):
                    rows = slice(SEQ * b, SEQ * (b + 1))
                    V.transpose(bd[rows, slot, :, b, :], sm_e[rows]).then_inc(bd_sem, 1)

            def softmax0(t):
                dve.wait_ge(s_nrm_ready, 2 * t + 2)
                dve.wait_ge(s_s0, t + 1)
                ins = V.tensor_tensor(sm_s[:], ps[:, 4, :].rearrange("p (h k) -> p h k", h=HQ),
                                      over(nrm[:, t % 2, HKV:HKV + HQ], SEQ), ALU.mult)
                ins.then_inc(s_s0_taken, 1)
                dve.wait_ge(s_s0_taken, t + 1)
                link(V.tensor_tensor(sm_s[:], sm_s[:], rep(k_("causal"), HQ), ALU.add))
                link(V.tensor_reduce(sm_m[:], sm_s[:], AX_X, ALU.max))
                V.tensor_tensor(sm_s[:], sm_s[:], over(sm_m[:], SEQ), ALU.subtract).then_inc(s_s0_shifted, 1)
                softmax_tail(s_e0, t + 1, t % 2, s_bd0, s_pv0, 4 * (t - 1) if t >= 2 else 0)

            def add_attn(t):
                dve.wait_ge(s_o0, t + 1)
                dve.wait_ge(s_ytok_copied, t + 1)
                dve.wait_ge(s_squares, t + 1)
                V.tensor_tensor(hid[:, t, :], ps[:, 7, 0:D], hid[:, t, :],
                                ALU.add).then_inc(s_hid_attn, 1)

            dve.wait_ge(s_bd_zero, 1)
            for s in range(TILES + 2):
                if s < TILES:
                    rope(s)
                if 1 <= s <= TILES:
                    softmax0(s - 1)
                if s >= 2:
                    add_attn(s - 2)

            def to_h2T(t):
                dve.wait_ge(s_hnT, t + 1)
                for m in range(DK):
                    V.tensor_scalar(h2T[:, m, t * P:(t + 1) * P], ps[:, 2 + t % 2, m * P:(m + 1) * P],
                                    c_("fnw", m), None, ALU.mult).then_inc(s_h2_ready, 1)

            for t in range(TILES + 1):
                if t < TILES:
                    dve.wait_ge(s_frstd, t + 1)
                    if t >= 2:
                        dve.wait_ge(s_hnT, t - 1)
                    V.tensor_scalar(hn[:, t % 2, :], hid[:, t, :], stat[:, 24 + t:25 + t], None,
                                    ALU.mult).then_inc(s_hn_ready, 1)
                if t >= 1:
                    to_h2T(t - 1)

            def shifted(logits, bias):
                src = logits
                if bias is not None:
                    link(V.tensor_tensor(rt[:, 0], logits, rep(bias, TILES), ALU.add))
                    src = rt[:, 0]
                link(V.tensor_reduce(bst[:, :, 0], src, AX_X, ALU.max))
                return V.tensor_tensor(rt[:, 1], src, over(bst[:, :, 0], NE), ALU.subtract)

            def probs():
                link(V.tensor_reduce(bst[:, :, 1], rt[:, 2], AX_X, ALU.add))
                link(V.reciprocal(bst[:, :, 2], bst[:, :, 1]))
                link(V.tensor_tensor(rt[:, 3], rt[:, 2], over(bst[:, :, 2], NE), ALU.mult))
                for t in range(TILES):
                    ins = V.max(rt[:, 4, t, :], rt[:, 3, t, :])
                link(ins)
                for t in range(TILES):
                    ins = V.max_index(ridx[:, t, :], rt[:, 4, t, :], rt[:, 3, t, :])
                link(ins)
                link(V.tensor_copy(rt[:, 5], ridx[:]))

            def one_hot(dst, k):
                return V.tensor_tensor(dst, rep(k_("iota"), TILES), over(rt[:, 5, :, k], NE), ALU.is_equal)

            dve.wait_ge(s_glog, TILES)
            shifted(ps[:, 7, 0:TILES * NE].rearrange("p (t e) -> p t e", t=TILES), None).then_inc(s_gsh, 1)
            dve.wait_ge(s_gexp, 1)
            probs()
            link(V.tensor_tensor(bst[:, :, 3], rt[:, 4, :, 0], rt[:, 4, :, 1], ALU.add))
            link(V.tensor_scalar(bst[:, :, 3], bst[:, :, 3], 1e-9, None, ALU.add))
            link(V.reciprocal(bst[:, :, 4], bst[:, :, 3]))
            link(V.tensor_tensor(rt[:, 6], rt[:, 4], over(bst[:, :, 4], NE), ALU.mult))
            link(one_hot(rt[:, 7], 0))
            link(one_hot(rt[:, 8], 1))
            link(V.tensor_tensor(rt[:, 7], rt[:, 7], over(rt[:, 6, :, 0], NE), ALU.mult))
            link(V.tensor_tensor(rt[:, 8], rt[:, 8], over(rt[:, 6, :, 1], NE), ALU.mult))
            V.tensor_tensor(rt[:, 9], rt[:, 7], rt[:, 8], ALU.add).then_inc(s_comb, 1)

            dve.wait_ge(ld_xtok, 16)
            for c in range(CHUNKS):
                for m in range(MI):
                    n = MI * c + m
                    dve.wait_ge(s_sg_ready, n + 1)
                    dve.wait_ge(s_moe_u, n + 1)
                    V.tensor_tensor(hu[:, n % 2, :], sg[:, n % 2, :], ps[:, 2 + n % 2, :],
                                    ALU.mult).then_inc(s_hu_ready, 1)
                    dve.wait_ge(s_hu_ready, n + 1)
                    dve.wait_ge(s_moe_c, n + 1)
                    if n >= 2:
                        dve.wait_ge(s_hm_used, n - 1)
                    V.tensor_tensor(hm[:, n % 2, :], hu[:, n % 2, :], ps[:, 4 + n % 2, :],
                                    ALU.mult).then_inc(s_hm_ready, 1)
                dve.wait_ge(s_hm_used, MI * (c + 1))
                tt = slice(c * CT, (c + 1) * CT)
                for a in range(2):
                    t2 = slice(c * CT + 2 * a, c * CT + 2 * a + 2)
                    link(V.tensor_tensor(hid[:, t2, :], ps[:, 6 + a, :].rearrange("p (b n) -> p b n", b=2),
                                         hid[:, t2, :], ALU.add))
                V.tensor_tensor(xres[:, tt, :], xres[:, tt, :], hid[:, tt, :], ALU.add).then_inc(s_x1_ready, 1)

            def ln_stats(src, t, done_sem):
                link(V.bn_stats(bst[:, t, 0:6], src))
                V.bn_aggr(bst[:, t, 6:8], bst[:, t, 0:6]).then_inc(done_sem, 1)

            def ln_apply(dst, src, t, r, done_sem):
                V.tensor_scalar(dst, src, bst[:, t, 6:7], stat[:, r + t:r + t + 1], ALU.subtract,
                                ALU.mult).then_inc(done_sem, 1)

            def modulate(dst, src, t, scale, shift, done_sem):
                for m in range(DK):
                    d4 = batches(dst[:, m, t * P:(t + 1) * P], BT)
                    s4 = batches(src[:, m * P:(m + 1) * P], BT)
                    link(V.tensor_tensor(d4, s4, over(ada[:, scale * DK + m, BT * t:BT * (t + 1)], SEQ), ALU.mult))
                    V.tensor_tensor(d4, d4, over(ada[:, shift * DK + m, BT * t:BT * (t + 1)], SEQ),
                                    ALU.add).then_inc(done_sem, 1)

            dve.wait_ge(s_x1_ready, CHUNKS)
            for t in range(TILES + 2):
                if t < TILES:
                    ln_stats(xres[:, t, :], t, s_lnst)
                if 1 <= t <= TILES:
                    dve.wait_ge(s_lrstd, t)
                    if t >= 3:
                        dve.wait_ge(s_zT, t - 2)
                    ln_apply(z[:, (t - 1) % 2, :], xres[:, t - 1, :], t - 1, 32, s_z_ready)
                if t >= 2:
                    dve.wait_ge(s_zT, t - 1)
                    modulate(yT, ps[:, 2 + (t - 2) % 2, :], t - 2, 1, 0, s_xn1_ready)

            def softmax1(u):
                dve.wait_ge(s_s1, u + 1)
                s4 = ps[:, 4, :].rearrange("p (h k) -> p h k", h=16)
                link(V.tensor_reduce(sm_m[:], s4, AX_X, ALU.max))
                V.tensor_tensor(sm_s[:], s4, over(sm_m[:], SEQ), ALU.subtract).then_inc(s_s1_shifted, 1)
                softmax_tail(s_e1, u + 1, u % 2, s_bd1, s_pv1, 4 * (u - 1) if u >= 2 else 0)

            def add_out(u):
                j, c = divmod(u, CHUNKS)
                for m in range(DK):
                    n = DK * u + m
                    dve.wait_ge(s_o1, n + 1)
                    dst, src = ywT[:, m, c * BANK:(c + 1) * BANK], ps[:, 7 if m else 3, :]
                    if j == 0:
                        ins = V.tensor_copy(dst, src)
                    else:
                        ins = V.tensor_tensor(dst, src, dst, ALU.add)
                    ins.then_inc(s_acc1, 1)

            for u in range(U + 1):
                if u < U:
                    softmax1(u)
                if u >= 1:
                    add_out(u - 1)

            def gated(acc, gate, bias, res, c, m):
                s = slice(c * BANK, (c + 1) * BANK)
                link(V.scalar_tensor_tensor(batches(ywT[:, m, s], CB), batches(acc, CB), c_(bias, m),
                                            over(ada[:, gate * DK + m, CB * c:CB * (c + 1)], SEQ), ALU.add, ALU.mult))
                return V.tensor_tensor(res[:, m, s], res[:, m, s], ywT[:, m, s], ALU.add)

            dve.wait_ge(s_acc1, DK * U)
            dve.wait_ge(s_xT1_copied, TILES)
            for c in range(CHUNKS):
                for m in range(DK):
                    gated(ywT[:, m, c * BANK:(c + 1) * BANK], 2, "outb", xT, c, m).then_inc(s_x2_ready, 1)
            for t in range(TILES + 2):
                if t < TILES:
                    dve.wait_ge(s_x2s_copied, t + 1)
                    ln_stats(x2s[:, t % 2, :], t, s_ln2st)
                    dve.wait_ge(s_l2rstd, t + 1)
                    if t >= 2:
                        dve.wait_ge(s_z2T, t - 1)
                    ln_apply(z2[:, t % 2, :], x2s[:, t % 2, :], t, 40, s_z2_ready)
                if 1 <= t <= TILES:
                    dve.wait_ge(s_z2T, t)
                    modulate(yT, ps[:, (t - 1) % 2, :], t - 1, 4, 3, s_xn3_ready)
            dve.wait_ge(s_x2_ready, DK * CHUNKS)
            for c in range(CHUNKS):
                for m in range(DK):
                    dve.wait_ge(s_ffn2, DK * c + m + 1)
                    gated(ps[:, 4 + m, :], 5, "b2", xT, c, m).then_inc(s_x4_ready, 1)
            dve.wait_ge(s_x4_ready, DK * CHUNKS)
            dve.wait_ge(s_rlog, TILES)
            shifted(ps[:, 7, 0:TILES * NE].rearrange("p (t e) -> p t e", t=TILES),
                    c_("br", 0, NE)).then_inc(s_rsh, 1)
            dve.wait_ge(s_rexp, 1)
            probs()
            link(one_hot(rt[:, 7], 0))
            V.scalar_tensor_tensor(rt[:, 9], rt[:, 7], 1.0 / RANK, over(rt[:, 4, :, 0], NE), ALU.mult,
                                   ALU.mult).then_inc(s_wsel, 1)
            for n in range(CHUNKS * MR):
                c, m = divmod(n, MR)
                dve.wait_ge(s_lora_h, n + 1)
                dve.wait_ge(s_hw_copied, n + 1)
                if n >= MR:
                    dve.wait_ge(s_lora_y, CT * c)
                V.tensor_tensor(hmk[:, m, :], ps[:, n % 2, :], hw[:, n % 2, :], ALU.mult).then_inc(s_hmask, 1)
                if m == MR - 1:
                    for t in range(c * CT, (c + 1) * CT):
                        dve.wait_ge(s_lora_y, t + 1)
                        V.tensor_tensor(xres[:, t, :], ps[:, 6 + t % 2, 0:D], xres[:, t, :],
                                        ALU.add).then_inc(s_y_ready, 1)

        @block.tensor
        def _(pe):
            mm = nc.tensor.matmul

            def tokens(t):
                return slice(t * P, (t + 1) * P)

            pe.wait_ge(ld_ada, 32)
            for n in range(NADA):
                for m in range(DK):
                    last = mm(ps[:, 4, n * BATCH:(n + 1) * BATCH], wada[:, m, n * P:(n + 1) * P], cond[:, m, :],
                              start=(m == 0), stop=(m == DK - 1))
            last.then_inc(s_ada_mm, 1)
            pe.wait_ge(ld_consts, 16)
            for t in range(TILES):
                pe.wait_ge(s_conv_step, DK * SEQ * (t // CT + 1))
                if t >= 2:
                    pe.wait_ge(s_squares, t - 1)
                    pe.wait_ge(s_ytok_copied, t - 1)
                for m in range(DK):
                    last = nc.tensor.transpose(ps[:, 2 + t % 2, m * P:(m + 1) * P], yT[:, m, tokens(t)], ident)
                last.then_inc(s_ytok_T, 1)

            pe.wait_ge(ld_qkv0, 16)

            def proj(t):
                pe.wait_ge(s_yw_ready, DK * (t // CT + 1))
                for k in range(NPROJ):
                    n = NPROJ * t + k
                    if n >= 2:
                        a, b = divmod(n - 2, NPROJ)
                        if b == NPROJ - 1:
                            pe.wait_ge(s_v0_ready, a + 1)
                        else:
                            pe.wait_ge(s_raw_ready, QK * a + b + 1)
                    for m in range(DK):
                        last = mm(ps[:, n % 2, :], ywT[:, m, tokens(t)], wqkv0[:, m, k * BANK:(k + 1) * BANK],
                                  start=(m == 0), stop=(m == DK - 1))
                    last.then_inc(s_proj0, 1)

            def turn_qk(t):
                if t == 0:
                    pe.wait_ge(s_ytok_copied, TILES)
                    pe.wait_ge(s_squares, TILES)
                for k in range(QK):
                    f = QK * t + k
                    pe.wait_ge(s_roped, f + 1)
                    if f >= 2:
                        pe.wait_ge(s_qkT_copied, f - 1)
                    for h in range(4):
                        last = nc.tensor.transpose(ps[:, 2 + f % 2, h * DH:(h + 1) * DH],
                                                   qr[:, t % 2, k * BANK + h * DH:k * BANK + (h + 1) * DH], ident)
                    last.then_inc(s_qkT_in_psum, 1)

            def scores0(t):
                pe.wait_ge(s_qkT_copied, QK * (t + 1))
                if t == 0:
                    pe.wait_ge(s_ada_ready, 1)
                if t >= 1:
                    pe.wait_ge(s_s0_taken, t)
                for h in range(HQ):
                    for b in range(BT):
                        q = BANK + h * P + b * SEQ
                        k = (h // REP) * P + b * SEQ
                        last = mm(ps[b * SEQ:(b + 1) * SEQ, 4, h * SEQ:(h + 1) * SEQ], qkT[:, q:q + SEQ],
                                  qkT[:, k:k + SEQ], start=True, stop=True)
                last.then_inc(s_s0, 1)

            def pv(t):
                pe.wait_ge(s_v0_ready, t + 1)
                pe.wait_ge(s_bd0, BT * (t + 1))
                for j in range(HKV):
                    n = 4 * t + j
                    if n >= 2:
                        pe.wait_ge(s_pv0_copied, n - 1)
                    mm(ps[:, 5 + n % 2, :], v0[:, t % 3, j * DH:(j + 1) * DH],
                       bd[:, t % 2, REP * j:REP * (j + 1)].rearrange("p h b q -> p (h b q)"),
                       start=True, stop=True).then_inc(s_pv0, 1)

            def oproj(t):
                pe.wait_ge(s_pv0_copied, 4 * (t + 1))
                if t >= 1:
                    pe.wait_ge(s_hid_attn, t)
                for h in range(HQ):
                    last = mm(ps[:, 7, 0:D], attnT[:, h * P:(h + 1) * P], wo[:, h, :],
                              start=(h == 0), stop=(h == HQ - 1))
                last.then_inc(s_o0, 1)

            for s in range(TILES + 2):
                if s < TILES:
                    proj(s)
                if 1 <= s <= TILES:
                    turn_qk(s - 1)
                    scores0(s - 1)
                if s >= 2:
                    if s == 2:
                        pe.wait_ge(ld_o0, 16)
                    pv(s - 2)
                    oproj(s - 2)

            pe.wait_ge(ld_small, 64)
            pe.wait_ge(s_qkT_copied, QK * TILES)
            pe.wait_ge(s_hid_attn, TILES)

            def logits0(t):
                pe.wait_ge(s_h2_ready, DK * (t + 1))
                for m in range(DK):
                    last = mm(ps[:, 7, t * NE:(t + 1) * NE], h2T[:, m, tokens(t)], gate_w[:, m, :],
                              start=(m == 0), stop=(m == DK - 1))
                last.then_inc(s_glog, 1)

            for t in range(TILES + 1):
                if t < TILES:
                    pe.wait_ge(s_hn_ready, t + 1)
                    if t >= 2:
                        pe.wait_ge(s_h2_ready, DK * (t - 1))
                    for m in range(DK):
                        last = nc.tensor.transpose(ps[:, 2 + t % 2, m * P:(m + 1) * P], hn[:, t % 2, m * P:(m + 1) * P],
                                                   ident)
                    last.then_inc(s_hnT, 1)
                if t >= 1:
                    logits0(t - 1)

            pe.wait_ge(s_comb, 1)
            for t in range(TILES):
                nc.tensor.transpose(ps[0:NE, 4 + t // CT, (t % CT) * P:(t % CT + 1) * P], rt[:, 9, t, :],
                                    ident).then_inc(s_combT_psum, 1)
            pe.wait_ge(s_combT_ready, CHUNKS)
            pe.wait_ge(ld_moe, 48)

            def moe_up(n):
                c, m = divmod(n, MI)
                s = slice(c * BANK, (c + 1) * BANK)
                if n >= 2:
                    pe.wait_ge(s_sg_ready, n - 1)
                for k in range(DK):
                    last = mm(ps[:, n % 2, :], wg[:, k, m * P:(m + 1) * P], h2T[:, k, s], start=(k == 0), stop=(k == DK - 1))
                last.then_inc(s_moe_g, 1)
                if n >= 2:
                    pe.wait_ge(s_hu_ready, n - 1)
                for k in range(DK):
                    last = mm(ps[:, 2 + n % 2, :], wu[:, k, m * P:(m + 1) * P], h2T[:, k, s], start=(k == 0), stop=(k == DK - 1))
                last.then_inc(s_moe_u, 1)
                if n >= 2:
                    pe.wait_ge(s_hm_ready, n - 1)
                mm(ps[:, 4 + n % 2, :], erows[:, m * P:(m + 1) * P], cmbT_[0:NE, s], start=True,
                   stop=True).then_inc(s_moe_c, 1)

            def moe_down(n):
                c, m = divmod(n, MI)
                pe.wait_ge(s_hm_ready, n + 1)
                if m == 0 and c == 0:
                    pe.wait_ge(s_gsh, 1)
                if m == 0 and c >= 1:
                    pe.wait_ge(s_x1_ready, c)
                for t in range(CT):
                    last = mm(ps[:, 6 + t // 2, (t % 2) * D:(t % 2 + 1) * D], hm[:, n % 2, t * P:(t + 1) * P], wd[:, m, :],
                              start=(m == 0 and t % 2 == 0), stop=(m == MI - 1), skip_group_check=True)
                last.then_inc(s_hm_used, 1)

            NM = CHUNKS * MI
            for n in range(NM + 1):
                if n < NM:
                    moe_up(n)
                if n >= 1:
                    moe_down(n - 1)

            pe.wait_ge(s_hu_ready, NM)
            for t in range(TILES):
                pe.wait_ge(s_z_ready, t + 1)
                if t >= 2:
                    pe.wait_ge(s_xn1_ready, DK * (t - 1))
                    pe.wait_ge(s_xT1_copied, t - 1)
                for m in range(DK):
                    nc.tensor.transpose(ps[:, 2 + t % 2, m * P:(m + 1) * P], z[:, t % 2, m * P:(m + 1) * P], ident)
                for m in range(DK):
                    last = nc.tensor.transpose(ps[:, t % 2, m * P:(m + 1) * P],
                                               xres[:, t, m * P:(m + 1) * P], ident)
                last.then_inc(s_zT, 1)
            pe.wait_ge(s_xT1_copied, TILES)

            def proj1(u):
                j, c = divmod(u, CHUNKS)
                W = wqkv1[j % 2]
                pe.wait_ge(ld_qkv1 if j % 2 == 0 else ld_qkv1b, 16 * (j // 2 + 1))
                pe.wait_ge(s_xn1_ready, DK * CT * (c + 1))
                for k in range(12):
                    n = 12 * u + k
                    if n >= 2:
                        pe.wait_ge(s_q1_copied, n - 1)
                    for m in range(DK):
                        if k < 8:
                            a, h = divmod(k, 4)
                            args = (W[:, m, a, h * DH:(h + 1) * DH], yT[:, m, c * BANK:(c + 1) * BANK])
                        else:
                            args = (yT[:, m, tokens(c * CT + k - 8)], W[:, m, 2, :])
                        last = mm(ps[:, n % 2, :], *args, start=(m == 0), stop=(m == DK - 1))
                    last.then_inc(s_proj1, 1)

            def scores1(u):
                pe.wait_ge(s_q1_copied, 12 * u + 8)
                if u == 0:
                    pe.wait_ge(s_hm_ready, NM)
                if u >= 1:
                    pe.wait_ge(s_s1_shifted, u)
                for h in range(4):
                    for t in range(CT):
                        for b in range(BT):
                            q = h * BANK + t * P + b * SEQ
                            k = 4 * h + t
                            last = mm(ps[b * SEQ:(b + 1) * SEQ, 4, k * SEQ:(k + 1) * SEQ], qT1[:, q:q + SEQ],
                                      kT1[:, q:q + SEQ], start=True, stop=True)
                last.then_inc(s_s1, 1)

            def pv1(u):
                pe.wait_ge(s_q1_copied, 12 * (u + 1))
                pe.wait_ge(s_bd1, BT * (u + 1))
                for h in range(4):
                    n = 4 * u + h
                    if n >= 2:
                        pe.wait_ge(s_pv1_copied, n - 1)
                    for t in range(CT):
                        last = mm(ps[:, 5 + n % 2, t * P:(t + 1) * P], v1[:, u % 2, t, h * DH:(h + 1) * DH],
                                  bd[:, u % 2, 4 * h + t].rearrange("p b q -> p (b q)"), start=True, stop=True)
                    last.then_inc(s_pv1, 1)

            def out1(u):
                j = u // CHUNKS
                pe.wait_ge(s_pv1_copied, 4 * (u + 1))
                if u >= 1:
                    pe.wait_ge(s_acc1, DK * u)
                for m in range(DK):
                    bank = 7 if m else 3
                    for h in range(4):
                        last = mm(ps[:, bank, :], wo[:, 4 * j + h, m * P:(m + 1) * P], attnT[:, h * BANK:(h + 1) * BANK],
                                  start=(h == 0), stop=(h == 3))
                    last.then_inc(s_o1, 1)

            pe.wait_ge(s_xn1_ready, DK * TILES)
            pe.wait_ge(s_x1_ready, CHUNKS)
            for u in range(U + 1):
                if u < U:
                    proj1(u)
                    scores1(u)
                if u >= 1:
                    if u == 1:
                        pe.wait_ge(ld_o1, 16)
                    pv1(u - 1)
                    out1(u - 1)

            pe.wait_ge(s_acc1, DK * U)
            pe.wait_ge(s_q1_copied, 12 * U)

            def turn_z2(t):
                pe.wait_ge(s_z2_ready, t + 1)
                if t >= 2:
                    pe.wait_ge(s_xn3_ready, DK * (t - 1))
                for m in range(DK):
                    last = nc.tensor.transpose(ps[:, t % 2, m * P:(m + 1) * P], z2[:, t % 2, m * P:(m + 1) * P], ident)
                last.then_inc(s_z2T, 1)

            for t in range(TILES + 1):
                if t < TILES:
                    pe.wait_ge(s_x2_ready, DK * (t // CT + 1))
                    if t >= 2:
                        pe.wait_ge(s_x2s_copied, t - 1)
                    for m in range(DK):
                        last = nc.tensor.transpose(ps[:, 2 + t % 2, m * P:(m + 1) * P], xT[:, m, tokens(t)], ident)
                    last.then_inc(s_x2T_psum, 1)
                if t >= 1:
                    turn_z2(t - 1)

            pe.wait_ge(ld_ffn1, 64)
            pe.wait_ge(s_xn3_ready, DK * TILES)
            pe.wait_ge(s_s1_shifted, U)
            for c in range(CHUNKS):
                for k in range(MM):
                    n = MM * c + k
                    if n >= 2:
                        pe.wait_ge(s_gelu, n - 1)
                    for m in range(DK):
                        last = mm(ps[:, n % 2, :], w1[:, m, k * P:(k + 1) * P], yT[:, m, c * BANK:(c + 1) * BANK],
                                  start=(m == 0), stop=(m == DK - 1))
                    last.then_inc(s_ffn1, 1)
                pe.wait_ge(s_gelu, MM * (c + 1))
                if c >= 1:
                    pe.wait_ge(s_x4_ready, DK * c)
                if c == 0:
                    pe.wait_ge(s_pv1_copied, 4 * U)
                for m in range(DK):
                    for k in range(MM):
                        last = mm(ps[:, 4 + m, :], w2[:, k, m * P:(m + 1) * P], gT[:, k, :], start=(k == 0), stop=(k == MM - 1))
                    last.then_inc(s_ffn2, 1)

            for t in range(TILES):
                pe.wait_ge(s_x4_ready, DK * (t // CT + 1))
                for m in range(DK):
                    last = mm(ps[:, 7, t * NE:(t + 1) * NE], xT[:, m, tokens(t)], r_w[:, m, :],
                              start=(m == 0), stop=(m == DK - 1))
                last.then_inc(s_rlog, 1)
            pe.wait_ge(s_wsel, 1)
            for t in range(TILES):
                nc.tensor.transpose(ps[0:NE, 4 + t // CT, (t % CT) * P:(t % CT + 1) * P], rt[:, 9, t, :],
                                    ident).then_inc(s_wselT, 1)
            pe.wait_ge(s_wselT_ready, CHUNKS)
            pe.wait_ge(s_x2s_copied, TILES)

            def lora_up(n):
                c, m = divmod(n, MR)
                s = slice(c * BANK, (c + 1) * BANK)
                if n >= 2:
                    pe.wait_ge(s_hmask, n - 1)
                for k in range(DK):
                    last = mm(ps[:, n % 2, :], wa[:, k, m * P:(m + 1) * P], xT[:, k, s], start=(k == 0), stop=(k == DK - 1))
                last.then_inc(s_lora_h, 1)
                mm(ps[:, 2 + n % 2, :], erows[:, EI + m * P:EI + (m + 1) * P], gT_[0:NE, s], start=True,
                   stop=True).then_inc(s_lora_w, 1)

            for c in range(CHUNKS):
                for m in range(MR):
                    lora_up(MR * c + m)
                pe.wait_ge(s_hmask, MR * (c + 1))
                for t in range(c * CT, (c + 1) * CT):
                    if t >= 2:
                        pe.wait_ge(s_y_ready, t - 1)
                    for m in range(MR):
                        last = mm(ps[:, 6 + t % 2, 0:D], hmk[:, m, (t % CT) * P:(t % CT + 1) * P],
                                  wb[:, m, :], start=(m == 0), stop=(m == MR - 1))
                    last.then_inc(s_lora_y, 1)


def _by_row(a, n):
    return np.ascontiguousarray(a.reshape(n, P, -1).transpose(1, 0, 2))


def _columns(a):
    return a.reshape(-1, P).T


def _constants():
    freqs = (1.0 / np.float32(1000000.0) ** (np.arange(0, DH, 2, dtype=np.float32) / np.float32(DH))).astype(np.float32)
    angle = np.outer(np.arange(SEQ, dtype=np.float32), freqs).astype(np.float32)
    cos, sin = np.cos(angle), np.sin(angle)
    causal = np.where(np.tril(np.ones((SEQ, SEQ), bool)), 0.0, NEG)
    return np.concatenate([
        np.eye(P), np.tile(np.concatenate([cos, cos], 1), (BT, 1)), np.tile(np.concatenate([-sin, sin], 1), (BT, 1)),
        np.tile(causal, (BT, 1)), np.tile(np.arange(NE), (P, 1))], axis=1).astype(np.float32)


def kernel(**inputs):
    import concourse.bacc as bacc
    from concourse.bass_utils import run_bass_kernel_spmd

    a = {k: np.asarray(v) for k, v in inputs.items()}
    x = a["x"].reshape(TOK, D)
    qw, kw = a["L0_ffn_q_norm_w"], a["L0_ffn_k_norm_w"]
    turn = np.roll(np.arange(DH), -(DH // 2))
    rope_w = np.stack([qw, qw[turn], kw, kw[turn]])
    rows = np.concatenate([np.repeat(np.eye(NE), INTER, axis=1), np.repeat(np.eye(NE), RANK, axis=1)], axis=1)
    qkv_b = a["L1_cond_qkv_b"].reshape(3, HQ * DH)
    cols = np.concatenate([
        _by_row(a["cond_2048"].T, DK).reshape(P, -1), _columns(a["L0_cond_b"]), _columns(a["L0_ffn_attn_norm_w"]),
        _columns(a["L0_ffn_ffn_norm_w"]), _columns(a["L1_cond_ada_b"]), _columns(qkv_b[0]), _columns(qkv_b[1]),
        _columns(qkv_b[2]), _columns(a["L1_cond_out_b"]), _columns(a["L1_cond_ffn_b1"]), _columns(a["L1_cond_ffn_b2"]),
        np.broadcast_to(a["L1_ffn_br"], (P, NE))], axis=1)
    wqkv0 = np.concatenate([a["L0_ffn_k_w"], a["L0_ffn_q_w"], a["L0_ffn_v_w"]]).T
    wqkv1 = a["L1_cond_qkv_w"].reshape(DK, P, 3, GROUPS, 4 * DH).transpose(3, 1, 0, 2, 4)
    arrays = {
        "x_tok": _by_row(x, TILES),
        "x_T": _by_row(x.T, DK),
        "cond_T": _by_row(a["cond_2048"].T, DK),
        "cols": cols,
        "consts": _constants(),
        "rope_w": np.broadcast_to(rope_w, (P, 4, DH)),
        "expert_rows": rows.astype(np.float32),
        "w_qkv0": _by_row(wqkv0, DK),
        "w_o0": _by_row(a["L0_ffn_o_w"].T, HQ),
        "w_gate0": _by_row(a["L0_ffn_gate_w"].T, DK),
        "w_g": _by_row(a["L0_ffn_wg"].reshape(EI, D).T, DK),
        "w_u": _by_row(a["L0_ffn_wu"].reshape(EI, D).T, DK),
        "w_d": _by_row(a["L0_ffn_wd"].transpose(0, 2, 1).reshape(EI, D), MI),
        "w_ada": _by_row(a["L1_cond_ada_w"], DK),
        "w_qkv1": wqkv1,
        "w_o1": _by_row(a["L1_cond_out_w"], HQ),
        "w_1": _by_row(a["L1_cond_ffn_w1"], DK),
        "w_2": _by_row(a["L1_cond_ffn_w2"], MM),
        "w_a": _by_row(a["L1_ffn_A"].reshape(ER, D).T, DK),
        "w_b": _by_row(a["L1_ffn_B"].transpose(0, 2, 1).reshape(ER, D), MR),
        "w_r": _by_row(a["L1_ffn_Wr"].T, DK),
    }
    arrays = {k: np.ascontiguousarray(v) for k, v in arrays.items()}
    nc = bacc.Bacc("TRN2", target_bir_lowering=False, num_devices=1)
    aps = {k: nc.dram_tensor("in_" + k, v.shape, mybir.dt.from_np(v.dtype), kind="ExternalInput").ap()
           for k, v in arrays.items()}
    out = nc.dram_tensor("out", (P, TILES, D), F32, kind="ExternalOutput").ap()
    build_program(nc, out=out, **aps)
    r = run_bass_kernel_spmd(nc, [{"in_" + k: v for k, v in arrays.items()}], core_ids=[0])
    got = r.results[0]["out"]
    return got.transpose(1, 0, 2).reshape(BATCH, SEQ, D)
```

```python
from contextlib import ExitStack

import numpy as np

import concourse.bass as bass
from concourse import mybir

ALU = mybir.AluOpType
ACT = mybir.ActivationFunctionType
F32 = mybir.dt.float32
U32 = mybir.dt.uint32
F32R = mybir.dt.float32r
AX_X = mybir.AxisListType.X

P = 128
D = 256
DH = 128
DK = D // P
BATCH, SEQ = 32, 32
TOK = BATCH * SEQ
TILES = TOK // P
BT = P // SEQ
HQ, HKV = 16, 4
REP = HQ // HKV
BANK = 512
CHUNKS = TOK // BANK
CB = BANK // SEQ
CT = BANK // P
QKV0 = 2 * HKV * DH + HQ * DH
NPROJ = QKV0 // BANK
NE, INTER = 8, 176
EI = NE * INTER
MI = EI // P
GROUPS = HQ // 4
MLP = 4 * D
MM = MLP // P
RANK = 64
ER = NE * RANK
MR = ER // P
NADA = 6 * DK
NEG = -1.0e30
PIECE = DK * BANK
WSLOTS = 6
RAWS = 4
STREAM = 3 * D
SS = 3

COLS = {}
_at = 0
for _name, _n in (("convw", DK * SEQ), ("convb", DK), ("anw", DK), ("fnw", DK), ("adab", NADA),
                  ("bq", HQ), ("bk", HQ), ("bv", HQ), ("outb", DK), ("b1", MM), ("b2", DK), ("br", NE)):
    COLS[_name] = (_at, _at + _n)
    _at += _n
NCOLS = _at
CONSTS = {}
_at = 0
for _name, _n in (("ident", P), ("cos", DH), ("sin", DH), ("causal", SEQ), ("iota", NE)):
    CONSTS[_name] = (_at, _at + _n)
    _at += _n
NCONSTS = _at


def build_program(nc, x_tok, x_T, cond_T, cols, consts, rope_w, w_qkv0, w_o0, w_gate0, w_moe, w_ada,
                  w_attn1, w_ffn1, w_lora, w_r, out):
    with ExitStack() as ctx:
        def sb(name, shape, dt=F32):
            return ctx.enter_context(nc.sbuf_tensor(name, shape, dt))

        def sem(name):
            return ctx.enter_context(nc.semaphore(name))

        col = sb("col", [P, NCOLS])
        cst = sb("cst", [P, NCONSTS])
        tables = sb("tables", [P, 4, DH])
        gate_w = sb("gate_w", [P, DK, NE])
        r_w = sb("r_w", [P, DK, NE])
        cond = sb("cond", [P, DK, BATCH])
        ada = sb("ada", [P, NADA, BATCH])
        xT = sb("xT", [P, DK, TOK])
        yT = sb("yT", [P, DK, TOK])
        act_hi = sb("act_hi", [P, DK, TOK], F32R)
        act_lo = sb("act_lo", [P, DK, TOK], F32R)
        hid = sb("hid", [P, TILES, D])
        xres = sb("xres", [P, TILES, D])
        w_hi = sb("w_hi", [P, WSLOTS, DK, BANK], F32R)
        w_lo = sb("w_lo", [P, WSLOTS, DK, BANK], F32R)
        raw_w = sb("raw_w", [P, RAWS * PIECE])
        strm_hi = sb("strm_hi", [P, SS, 4, P], F32R)
        strm_lo = sb("strm_lo", [P, SS, 4, P], F32R)
        raw_s = sb("raw_s", [P, SS * STREAM])
        work = sb("work", [P, 9728])
        bd = sb("bd", [P, 2, 16, BT, SEQ])
        sm_s = sb("sm_s", [P, 16, SEQ])
        sm_e = sb("sm_e", [P, 16, SEQ])
        sm_m = sb("sm_m", [P, 16])
        sm_d = sb("sm_d", [P, 16])
        sm_r = sb("sm_r", [P, 16])
        stat = sb("stat", [P, 48])
        half = sb("half", [P, HQ])
        ssq = sb("ssq", [P, 2, HKV + HQ])
        nrm = sb("nrm", [P, 2, HKV + HQ])
        nrt = sb("nrt", [P, 2, HKV + HQ])
        junk = sb("junk", [P, 3, D])
        rt = sb("rt", [P, 10, TILES, NE])
        ridx = sb("ridx", [P, TILES, 8], U32)
        bst = sb("bst", [P, TILES, 8])
        ps = ctx.enter_context(nc.psum_tensor("ps", [P, 8, BANK], F32))
        comb_dram = nc.dram_tensor("comb_dram", [2, NE, TOK], F32, kind="Internal").ap()

        def c_(name, k=0, n=1):
            return col[:, COLS[name][0] + k:COLS[name][0] + k + n]

        def k_(name):
            return cst[:, CONSTS[name][0]:CONSTS[name][1]]

        ident = k_("ident")
        raw_p = raw_w[:].rearrange("p (s n) -> p s n", s=RAWS)
        wo0 = raw_w[:].rearrange("p (h n) -> p h n", h=HQ)
        raw_t = raw_s[:].rearrange("p (s n) -> p s n", s=SS)
        attnT = raw_s[:, 0:4 * BANK]
        ropew = sm_s[:].rearrange("p h k -> p (h k)").rearrange("p (i d) -> p i d", i=4)
        wada = bd[:].rearrange("p r a b c -> p (r a b c)")[:, 0:DK * 6 * D].rearrange("p (m n) -> p m n", m=DK)

        def carve(sizes):
            at, found = 0, []
            for n in sizes:
                found.append(work[:, at:at + n])
                at += n
            assert at <= 9728, at
            return found

        NQK = QKV0 - BANK
        NR = 5
        diag = work[:, 0:SEQ * P].rearrange("p (k n) -> p k n", k=SEQ)
        raw_, qr, kn, r2, qkT, v0_ = carve([NR * BANK, NQK, BANK, BANK, NQK, 2 * BANK])
        raw = raw_.rearrange("p (r n) -> p r n", r=NR)
        v0 = v0_.rearrange("p (r n) -> p r n", r=2)
        h2_, cmbT, sg_, hu_, hm_, cb_ = carve([DK * TOK, TOK, 2 * BANK, BANK, 3 * BANK, 3 * TOK])
        h2 = h2_.rearrange("p (m n) -> p m n", m=DK)
        hn = cb_[:, 0:2 * D].rearrange("p (r n) -> p r n", r=2)
        sg = sg_.rearrange("p (r n) -> p r n", r=2)
        hm = hm_.rearrange("p (r n) -> p r n", r=3)
        cb = cb_.rearrange("p (r n) -> p r n", r=3)
        qT1, kT1 = carve([4 * BANK, 4 * BANK])
        v1_ = work[:, 8 * BANK:16 * BANK]
        v1 = v1_.rearrange("p (r t n) -> p r t n", r=2, t=CT)
        zx = work[:, 16 * BANK:16 * BANK + 6 * D]
        z = zx[:, 0:2 * D].rearrange("p (r n) -> p r n", r=2)
        mt = zx[:, 2 * D:4 * D].rearrange("p (r n) -> p r n", r=2)
        x2s = qT1.rearrange("p (t n) -> p t n", t=TILES)
        z2 = kT1.rearrange("p (t n) -> p t n", t=TILES)
        g32 = v1_[:, 0:2 * BANK].rearrange("p (r n) -> p r n", r=2)
        hmk = v1_[:, 3 * BANK:6 * BANK].rearrange("p (r n) -> p r n", r=3)
        cb1 = work[:, 0:4 * TOK].rearrange("p (r n) -> p r n", r=MR)
        selT = work[:, 4 * TOK + 6 * BANK:5 * TOK + 6 * BANK]
        w_hi2 = w_hi[:].rearrange("p s k n -> p (s k) n")
        w_lo2 = w_lo[:].rearrange("p s k n -> p (s k) n")

        def flat(ap):
            return ap.rearrange("p a b -> p (a b)")

        def f32(ap):
            return ap.bitcast(F32)

        def batches(ap, n):
            return ap.rearrange("p (b l) -> p b l", b=n)

        def over(ap, n):
            return ap.unsqueeze(len(ap.shape)).broadcast_to([*ap.shape, n])

        def rep(ap, n):
            return ap.unsqueeze(1).broadcast_to([ap.shape[0], n, ap.shape[1]])

        ld_x = sem("ld_x")
        ld_cols = sem("ld_cols")
        ld_consts = sem("ld_consts")
        ld_piece = [sem(f"ld_piece{i}") for i in range(RAWS)]
        ld_ada = sem("ld_ada")
        ld_small = sem("ld_small")
        ld_xtok = sem("ld_xtok")
        ld_o0 = sem("ld_o0")
        ld_slice = [sem(f"ld_slice{i}") for i in range(SS)]
        st_comb = sem("st_comb")
        ld_cb = [sem(f"ld_cb{i}") for i in range(SS)]
        ld_cb1 = [sem(f"ld_cb1_{i}") for i in range(MR)]
        stored = sem("stored")
        s_out1 = sem("out1")
        s_proj1 = sem("proj1")
        s_piece_lo = sem("piece_lo")
        s_o0 = sem("o0")
        s_combT_ready = sem("combT_ready")
        s_hm_ready = sem("hm_ready")
        s_hm_used = sem("hm_used")
        s_slice_lo = sem("slice_lo")
        s_hmk_used = sem("hmk_used")
        s_selT_ready = sem("selT_ready")
        s_y_ready = sem("y_ready")
        s_pool_chain = sem("pool_chain")
        s_piece_hi = sem("piece_hi")
        s_slice_hi = sem("slice_hi")
        s_squares = sem("squares")
        s_yrstd = sem("yrstd")
        s_s0_taken = sem("s0_taken")
        s_roped = sem("roped")
        s_nrm_ready = sem("nrm_ready")
        s_ada_mm = sem("ada_mm")
        s_bd_zero = sem("bd_zero")
        s_frstd = sem("frstd")
        s_lnst = sem("lnst")
        s_lrstd = sem("lrstd")
        s_ln2st = sem("ln2st")
        s_l2rstd = sem("l2rstd")
        s_diag = sem("diag")
        s_ytok_T = sem("ytok_T")
        s_ytok_copied = sem("ytok_copied")
        s_proj0 = sem("proj0")
        s_pv0 = sem("pv0")
        s_v0_ready = sem("v0_ready")
        s_raw_ready = sem("raw_ready")
        s_s0 = sem("s0")
        s_qkT_in_psum = sem("qkT_in_psum")
        s_qkT_copied = sem("qkT_copied")
        s_pv0_copied = sem("pv0_copied")
        s_y1 = sem("y1")
        s_s0_shifted = sem("s0_shifted")
        s_e0 = sem("e0")
        s_hid_attn = sem("hid_attn")
        s_gsh = sem("gsh")
        s_gexp = sem("gexp")
        s_combT_psum = sem("combT_psum")
        s_moe_g = sem("moe_g")
        s_hu_ready = sem("hu_ready")
        s_sg_ready = sem("sg_ready")
        s_moe_u = sem("moe_u")
        s_zT = sem("zT")
        s_xT1_copied = sem("xT1_copied")
        s_s1 = sem("s1")
        s_q1_copied = sem("q1_copied")
        s_pv1 = sem("pv1")
        s_pv1_hi = sem("pv1_hi")
        s_s1_shifted = sem("s1_shifted")
        s_e1 = sem("e1")
        s_x2T = sem("x2T")
        s_x2s_copied = sem("x2s_copied")
        s_ffn_up = sem("ffn_up")
        s_glo = sem("glo")
        s_gelu = sem("gelu")
        s_ffn_down = sem("ffn_down")
        s_rsh = sem("rsh")
        s_rexp = sem("rexp")
        s_selT_psum = sem("selT_psum")
        s_lora_up = sem("lora_up")
        s_dve_chain = sem("dve_chain")
        s_yw_ready = sem("yw_ready")
        s_conv_step = sem("conv_step")
        s_conv_mm = sem("conv_mm")
        s_tables_ready = sem("tables_ready")
        s_ada_ready = sem("ada_ready")
        s_bd0 = sem("bd0")
        s_hnT = sem("hnT")
        s_h2_f32 = sem("h2_f32")
        s_h2_ready = sem("h2_ready")
        s_hn_ready = sem("hn_ready")
        s_glog = sem("glog")
        s_comb = sem("comb")
        s_x1_ready = sem("x1_ready")
        s_z_ready = sem("z_ready")
        s_xn1_ready = sem("xn1_ready")
        s_pv1_lo = sem("pv1_lo")
        s_acc1 = sem("acc1")
        s_x2_ready = sem("x2_ready")
        s_z2_ready = sem("z2_ready")
        s_z2T = sem("z2T")
        s_xn3_ready = sem("xn3_ready")
        s_bd1 = sem("bd1")
        s_ghi = sem("ghi")
        s_x4_ready = sem("x4_ready")
        s_x4_split = sem("x4_split")
        s_rlog = sem("rlog")
        s_wsel = sem("wsel")
        s_hmk_ready = sem("hmk_ready")

        block = ctx.enter_context(nc.Block())
        QK = NPROJ - 1
        U = GROUPS * CHUNKS
        NP1 = 4 * GROUPS
        NM = CHUNKS * MI
        NF = CHUNKS * MM
        NL = CHUNKS * MR
        HD = DH // 2
        FFN = [(0, 0), (1, 0), (0, 1), (1, 1)] + [(m, c) for m in range(2, MM) for c in range(CHUNKS)]

        def piece_free(i):
            j, s = divmod(i - WSLOTS, 4)
            u = CHUNKS * j + CHUNKS - 1
            return (s_out1, 4 * (u + 1)) if s == 3 else (s_proj1, 12 * u + 4 * (s + 1))

        @block.sync
        def _(sp):
            sp.dma_start(xT[:], x_T).then_inc(ld_x, 16)
            sp.dma_start(col[:], cols).then_inc(ld_cols, 16)
            sp.dma_start(cst[:], consts).then_inc(ld_consts, 16)
            for i in range(RAWS):
                sp.dma_start(raw_p[:, i, :], w_qkv0[i]).then_inc(ld_piece[i], 16)
            sp.dma_start(cond[:], cond_T).then_inc(ld_ada, 16)
            sp.dma_start(wada, w_ada).then_inc(ld_ada, 16)
            sp.dma_start(ropew, rope_w).then_inc(ld_small, 16)
            sp.dma_start(gate_w[:], w_gate0).then_inc(ld_small, 16)
            sp.dma_start(r_w[:], w_r).then_inc(ld_small, 16)
            for i in range(RAWS, NPROJ):
                sp.wait_ge(s_piece_lo, i - RAWS + 1)
                sp.dma_start(raw_p[:, i % RAWS, :], w_qkv0[i]).then_inc(ld_piece[i % RAWS], 16)
            sp.dma_start(xres[:], x_tok).then_inc(ld_xtok, 16)
            sp.wait_ge(s_piece_lo, NPROJ)
            sp.dma_start(wo0, w_o0).then_inc(ld_o0, 16)
            sp.wait_ge(s_o0, TILES)
            for f in range(SS):
                sp.dma_start(raw_t[:, f, :], w_moe[f]).then_inc(ld_slice[f], 16)
            for i in range(RAWS):
                sp.dma_start(raw_p[:, i, :], w_attn1[i]).then_inc(ld_piece[i], 16)
            sp.wait_ge(s_combT_ready, CHUNKS)
            sp.dma_start(comb_dram[0], cmbT[0:NE, :]).then_inc(st_comb, 16)
            sp.wait_ge(st_comb, 16)

            def spread(dst, layer, m, width, done_sem):
                lo, at = m * P, 0
                parts = []
                while at < P:
                    e = (lo + at) // width
                    n = min(P - at, (e + 1) * width - lo - at)
                    parts.append((e, at, n))
                    at += n
                if len(parts) == 1:
                    e, at, n = parts[0]
                    parts = [(e, 0, n // 2), (e, n // 2, n - n // 2)]
                for e, at, n in parts:
                    sp.dma_start(dst[at:at + n, :], comb_dram[layer, e:e + 1, :].broadcast_to([n, TOK])).then_inc(done_sem, 16)

            for m in range(MI):
                if m >= SS:
                    sp.wait_ge(s_hm_ready, CHUNKS * (m - SS + 1))
                spread(cb[:, m % SS, :], 0, m, INTER, ld_cb[m % SS])
                if m >= SS:
                    sp.wait_ge(s_hm_used, CHUNKS * (m - SS + 1))
                    sp.dma_start(raw_t[:, m % SS, :], w_moe[m]).then_inc(ld_slice[m % SS], 16)
                if m in (6, 7):
                    i = m - 2
                    sp.wait_ge(s_piece_lo, NPROJ + i - RAWS + 1)
                    sp.dma_start(raw_p[:, i % RAWS, :], w_attn1[i]).then_inc(ld_piece[i % RAWS], 16)
            for i in range(6, 8):
                sp.wait_ge(s_piece_lo, NPROJ + i - RAWS + 1)
                sp.dma_start(raw_p[:, i % RAWS, :], w_attn1[i]).then_inc(ld_piece[i % RAWS], 16)
            sp.wait_ge(s_hm_used, NM)
            for f in range(SS):
                sp.dma_start(raw_t[:, f, 0:2 * D], w_ffn1[f]).then_inc(ld_slice[f], 16)
            for i in range(8, NP1):
                sp.wait_ge(s_piece_lo, NPROJ + i - RAWS + 1)
                sp.dma_start(raw_p[:, i % RAWS, :], w_attn1[i]).then_inc(ld_piece[i % RAWS], 16)
            for f in range(SS, MM + MR):
                if f - SS < MM:
                    sp.wait_ge(s_slice_lo, MI + f - SS + 1)
                else:
                    sp.wait_ge(s_hmk_used, CHUNKS * (f - SS - MM + 1))
                src = w_ffn1[f] if f < MM else w_lora[f - MM]
                sp.dma_start(raw_t[:, f % SS, 0:2 * D], src).then_inc(ld_slice[f % SS], 16)
                if f == MM + MR - 2:
                    sp.wait_ge(s_selT_ready, CHUNKS)
                    sp.dma_start(comb_dram[1], selT[0:NE, :]).then_inc(st_comb, 16)
                    sp.wait_ge(st_comb, 32)
                    for m in range(MR):
                        spread(cb1[:, m, :], 1, m, RANK, ld_cb1[m])
            for t in range(TILES):
                sp.wait_ge(s_y_ready, t // 2 + 1)
                sp.dma_start(out[:, t, :], xres[:, t, :]).then_inc(stored, 16)
            sp.wait_ge(stored, 16 * TILES)

        @block.gpsimd
        def _(pool):
            G = nc.gpsimd
            done = [0]

            def link(ins):
                done[0] += 1
                ins.then_inc(s_pool_chain, 1)
                pool.wait_ge(s_pool_chain, done[0])

            def inv_root(dst, src, n, scale, eps, done_sem):
                link(G.tensor_scalar(dst, src, scale, eps, ALU.mult, ALU.add))
                G.tensor_tensor(dst, dst, half[:, 0:n], ALU.pow).then_inc(done_sem, 1)

            def piece_lo(i, raw_slot, slot):
                pool.wait_ge(s_piece_hi, i + 1)
                G.tensor_tensor(flat(w_lo[:, slot]), raw_p[:, raw_slot, :], flat(f32(w_hi[:, slot])),
                                ALU.subtract).then_inc(s_piece_lo, 1)

            def slice_lo(n, f, parts):
                pool.wait_ge(s_slice_hi, n + 1)
                G.tensor_tensor(flat(strm_lo[:, f % SS, 0:parts, :]), raw_t[:, f % SS, 0:parts * P],
                                flat(f32(strm_hi[:, f % SS, 0:parts, :])), ALU.subtract).then_inc(s_slice_lo, 1)

            link(G.memset(half[:], -0.5))
            for i in range(NPROJ):
                piece_lo(i, i % RAWS, i)

            def stats0(t):
                pool.wait_ge(s_squares, (4 * QK + 1) * t + 1)
                inv_root(stat[:, 8 + t:9 + t], stat[:, t:t + 1], 1, 1.0 / D, 1e-6, s_yrstd)
                r = stat[:, 8 + t:9 + t]
                pool.wait_ge(s_yrstd, t + 1)
                for a, n, k in ((0, HKV, 1), (HKV, HQ, QK)):
                    pool.wait_ge(s_squares, (4 * QK + 1) * t + 1 + 4 * k)
                    if t >= 2:
                        pool.wait_ge(s_s0_taken, t - 1)
                        pool.wait_ge(s_roped, QK * (t - 1))
                    dst = nrt[:, t % 2, a:a + n]
                    link(G.tensor_scalar(dst, ssq[:, t % 2, a:a + n], r, r, ALU.mult, ALU.mult))
                    link(G.tensor_scalar(dst, dst, 1.0 / DH, 1e-6, ALU.mult, ALU.add))
                    link(G.tensor_tensor(dst, dst, half[:, 0:n], ALU.pow))
                    G.tensor_scalar(nrm[:, t % 2, a:a + n], dst, r, 1.0 if a == 0 else DH ** -0.5,
                                    ALU.mult, ALU.mult).then_inc(s_nrm_ready, 1)

            pool.wait_ge(s_ada_mm, 1)
            G.memset(bd[:], 0.0).then_inc(s_bd_zero, 1)
            for t in range(TILES):
                stats0(t)
            for t in range(TILES):
                pool.wait_ge(s_squares, (4 * QK + 1) * TILES + t + 1)
                inv_root(stat[:, 24 + t:25 + t], stat[:, 16 + t:17 + t], 1, 1.0 / D, 1e-6, s_frstd)
            for f in range(MI):
                slice_lo(f, f, 4)
                if f >= 2 and f - 2 < 6:
                    piece_lo(NPROJ + f - 2, (f - 2) % RAWS, f - 2)
            for t in range(TILES):
                pool.wait_ge(s_lnst, t + 1)
                inv_root(stat[:, 32 + t:33 + t], bst[:, t, 7:8], 1, 1.0, 1e-6, s_lrstd)
            for i in range(6, NP1):
                piece_lo(NPROJ + i, i % RAWS, i % WSLOTS)
            for c in range(CHUNKS):
                for t in range(c * CT, (c + 1) * CT):
                    pool.wait_ge(s_ln2st, t + 1)
                    inv_root(stat[:, 40 + t:41 + t], bst[:, t, 7:8], 1, 1.0, 1e-6, s_l2rstd)
            for f in range(MM + MR):
                slice_lo(MI + f, f, 4 if f < MM else 2)

        @block.scalar
        def _(act):
            A = nc.scalar.activation
            squares = [0]

            def square(src, n, total):
                if squares[0] >= 3:
                    act.wait_ge(s_squares, squares[0] - 2)
                A(junk[:, squares[0] % 3, 0:n], src, ACT.Square, accum_out=total).then_inc(s_squares, 1)
                squares[0] += 1

            def piece_hi(i, raw_slot, slot):
                uses = i // RAWS + 1 if i < NPROJ else (NPROJ - 1 - raw_slot) // RAWS + 1 + (i - NPROJ) // RAWS + 1
                act.wait_ge(ld_piece[raw_slot], 16 * uses)
                A(flat(w_hi[:, slot]), raw_p[:, raw_slot, :], ACT.Copy).then_inc(s_piece_hi, 1)

            def slice_hi(n, f, parts):
                uses = f // SS + 1 if n < MI else (MI - 1 - f % SS) // SS + 1 + f // SS + 1
                act.wait_ge(ld_slice[f % SS], 16 * uses)
                A(flat(strm_hi[:, f % SS, 0:parts, :]), raw_t[:, f % SS, 0:parts * P], ACT.Copy).then_inc(s_slice_hi, 1)

            act.wait_ge(ld_cols, 16)
            act.wait_ge(ld_consts, 16)
            for delay in range(SEQ):
                A(diag[:, delay, :], ident, ACT.Copy,
                  scale=c_("convw", SEQ - 1 - delay)).then_inc(s_diag, 1)
            for i in range(NPROJ):
                piece_hi(i, i % RAWS, i)

            def take_y(t):
                act.wait_ge(s_ytok_T, t + 1)
                A(hid[:, t, :], ps[:, 7, 0:D], ACT.Copy).then_inc(s_ytok_copied, 1)
                square(ps[:, 7, 0:D], D, stat[:, t:t + 1])

            def take_proj(t, k):
                n = NPROJ * t + k
                act.wait_ge(s_proj0, n + 1)
                src = ps[:, n % 2, :]
                if k == NPROJ - 1:
                    act.wait_ge(s_yrstd, t + 1)
                    if t >= 2:
                        act.wait_ge(s_pv0, 4 * (t - 1))
                    A(v0[:, t % 2, :], src, ACT.Copy, scale=stat[:, 8 + t:9 + t]).then_inc(s_v0_ready, 1)
                    return
                if t >= 2:
                    act.wait_ge(s_nrm_ready, 2 * (t - 1))
                m = QK * t + k
                if m >= NR:
                    act.wait_ge(s_roped, m - NR + 1)
                A(raw[:, m % NR, :], src, ACT.Copy).then_inc(s_raw_ready, 1)
                for h in range(4):
                    square(src[:, h * DH:(h + 1) * DH], DH, ssq[:, t % 2, 4 * k + h:4 * k + h + 1])

            def take_qkT(t):
                if t >= 1:
                    act.wait_ge(s_s0, t)
                for k in range(QK):
                    f = QK * t + k
                    act.wait_ge(s_qkT_in_psum, f + 1)
                    A(qkT[:, k * BANK:(k + 1) * BANK], ps[:, 2 + f % 2, :], ACT.Copy).then_inc(s_qkT_copied, 1)

            def take_pv0(t):
                if t >= 1:
                    act.wait_ge(s_o0, t)
                for j in range(4):
                    n = 4 * t + j
                    act.wait_ge(s_pv0, n + 1)
                    A(attnT[:, j * BANK:(j + 1) * BANK], ps[:, 5 + n % 2, :], ACT.Copy).then_inc(s_pv0_copied, 1)

            act.wait_ge(s_y1, 1)
            for s in range(TILES + 1):
                if s < TILES:
                    take_y(s)
                    take_proj(s, 0)
                    take_proj(s, 1)
                if s >= 1:
                    act.wait_ge(s_s0_shifted, s)
                    A(sm_e[:], sm_s[:], ACT.Exp).then_inc(s_e0, 1)
                if s < TILES:
                    for k in range(2, NPROJ):
                        take_proj(s, k)
                if s >= 1:
                    take_pv0(s - 1)
                if s < TILES:
                    take_qkT(s)

            for t in range(TILES):
                act.wait_ge(s_hid_attn, t + 1)
                square(hid[:, t, :], D, stat[:, 16 + t:17 + t])
            slice_hi(0, 0, 4)
            act.wait_ge(s_gsh, 1)
            A(rt[:, 2], rt[:, 1], ACT.Exp).then_inc(s_gexp, 1)
            slice_hi(1, 1, 4)
            slice_hi(2, 2, 4)
            act.wait_ge(s_combT_psum, TILES)
            for c in range(CHUNKS):
                A(cmbT[0:NE, c * BANK:(c + 1) * BANK], ps[0:NE, 2 + c, :], ACT.Copy).then_inc(s_combT_ready, 1)
            for n in range(NM):
                act.wait_ge(s_moe_g, n + 1)
                if n >= 2:
                    act.wait_ge(s_hu_ready, n - 1)
                A(sg[:, n % 2, :], ps[:, 4 + 2 * (n % 2), :], ACT.Silu).then_inc(s_sg_ready, 1)
                f = n // CHUNKS + 1
                if n % CHUNKS == 0 and SS <= f < MI:
                    act.wait_ge(s_moe_u, CHUNKS * (f - SS + 1))
                    slice_hi(f, f, 4)
                i = n // CHUNKS - 1
                if n % CHUNKS and 0 <= i < WSLOTS:
                    piece_hi(NPROJ + i, i % RAWS, i)

            def take_x1(t):
                act.wait_ge(s_zT, t + 1)
                src = ps[:, 6 + t % 2, 0:D].rearrange("p (m n) -> p m n", m=DK)
                A(xT[:, :, t * P:(t + 1) * P], src, ACT.Copy).then_inc(s_xT1_copied, 1)

            def take_proj1(u):
                j = u // CHUNKS
                for k in range(12):
                    n = 12 * u + k
                    act.wait_ge(s_proj1, n + 1)
                    src = ps[:, n % 2, :]
                    if k < 8:
                        if k == 0 and u >= 1:
                            act.wait_ge(s_s1, u)
                        dst, b = (qT1, "bq") if k < 4 else (kT1, "bk")
                        h = k % 4
                        A(dst[:, h * BANK:(h + 1) * BANK], src, ACT.Identity,
                          bias=c_(b, 4 * j + h)).then_inc(s_q1_copied, 1)
                    else:
                        if k == 8 and u >= 2:
                            act.wait_ge(s_pv1, 4 * (u - 1))
                        A(v1[:, u % 2, k - 8, :], src, ACT.Copy).then_inc(s_q1_copied, 1)

            def take_pv1(u):
                for h in range(4):
                    n = 4 * u + h
                    act.wait_ge(s_pv1, n + 1)
                    if n >= SS:
                        act.wait_ge(s_out1, n - SS + 1)
                    A(flat(strm_hi[:, n % SS]), ps[:, 4 + n % 2, :], ACT.Identity,
                      bias=c_("bv", 4 * (u // CHUNKS) + h)).then_inc(s_pv1_hi, 1)

            for t in range(CT):
                take_x1(t)
            for u in range(U + 1):
                if u < U:
                    take_proj1(u)
                if u == 0:
                    for t in range(CT, TILES):
                        take_x1(t)
                if u >= 1:
                    take_pv1(u - 1)
                if u < U:
                    act.wait_ge(s_s1_shifted, u + 1)
                    A(sm_e[:], sm_s[:], ACT.Exp, scale=DH ** -0.5).then_inc(s_e1, 1)
                j = u // CHUNKS
                if u < U:
                    for i in ((4 * j + 6, 4 * j + 7, 4 * j + 8) if u % CHUNKS == CHUNKS - 1 else (4 * j + 5,)):
                        if WSLOTS <= i < NP1:
                            used_sem, count = piece_free(i)
                            act.wait_ge(used_sem, count)
                            piece_hi(NPROJ + i, i % RAWS, i % WSLOTS)
                if u == U - 1:
                    for t in range(CT):
                        act.wait_ge(s_x2T, t + 1)
                        A(x2s[:, t, :], ps[:, 2 + t % 2, 0:D], ACT.Copy).then_inc(s_x2s_copied, 1)
            act.wait_ge(s_out1, 4 * U)
            slice_hi(MI, 0, 4)
            slice_hi(MI + 1, 1, 4)
            for t in range(CT, TILES):
                act.wait_ge(s_x2T, t + 1)
                A(x2s[:, t, :], ps[:, 2 + t % 2, 0:D], ACT.Copy).then_inc(s_x2s_copied, 1)
            slice_hi(MI + 2, 2, 4)
            for n, (m, c) in enumerate(FFN):
                act.wait_ge(s_ffn_up, n + 1)
                if n >= 2:
                    act.wait_ge(s_glo, n - 1)
                A(g32[:, n % 2, :], ps[:, 4 + n % 4, :], ACT.Gelu, bias=c_("b1", m)).then_inc(s_gelu, 1)
                if n >= 4 and n % 2 == 0 and SS + (n - 4) // 2 < MM:
                    f = SS + (n - 4) // 2
                    act.wait_ge(s_ffn_down, CHUNKS * (f - SS + 1) if f > SS + 1 else (3 if f == SS else 4))
                    slice_hi(MI + f, f, 4)
            for f in range(MM, MM + SS):
                act.wait_ge(s_ffn_down, CHUNKS * (f - SS + 1))
                slice_hi(MI + f, f, 2)
            act.wait_ge(s_rsh, 1)
            A(rt[:, 2], rt[:, 1], ACT.Exp).then_inc(s_rexp, 1)
            act.wait_ge(s_selT_psum, TILES)
            for c in range(CHUNKS):
                A(selT[0:NE, c * BANK:(c + 1) * BANK], ps[0:NE, 2 + c, :], ACT.Copy).then_inc(s_selT_ready, 1)
            act.wait_ge(s_lora_up, CHUNKS)
            slice_hi(MI + MM + SS, MM + SS, 2)

        @block.vector
        def _(dve):
            done = [0]
            V = nc.vector

            def link(ins):
                done[0] += 1
                ins.then_inc(s_dve_chain, 1)
                dve.wait_ge(s_dve_chain, done[0])

            dve.wait_ge(ld_x, 16)
            dve.wait_ge(ld_cols, 16)

            def tap(c, m, delay):
                src = batches(xT[:, m, c * BANK:(c + 1) * BANK], CB)
                dst = batches(yT[:, m, c * BANK:(c + 1) * BANK], CB)
                weight = c_("convw", m * SEQ + SEQ - 1 - delay)
                if delay == 0:
                    return V.tensor_scalar(dst, src, weight, c_("convb", m), ALU.mult, ALU.add)
                return V.scalar_tensor_tensor(dst[:, :, delay:SEQ], src[:, :, 0:SEQ - delay], weight,
                                              dst[:, :, delay:SEQ], ALU.mult, ALU.add)

            def split_y(c, m):
                s = slice(c * BANK, (c + 1) * BANK)
                link(V.tensor_scalar(act_hi[:, m, s], yT[:, m, s], c_("anw", m), None, ALU.mult))
                V.scalar_tensor_tensor(act_lo[:, m, s], yT[:, m, s], c_("anw", m), f32(act_hi[:, m, s]),
                                       ALU.mult, ALU.subtract).then_inc(s_yw_ready, 1)

            n = 0
            for delay in range(SEQ):
                for m in range(DK):
                    if delay:
                        dve.wait_ge(s_conv_step, n - 1)
                    tap(0, m, delay).then_inc(s_conv_step, 1)
                    n += 1
            dve.wait_ge(s_conv_step, n)
            for m in range(DK):
                split_y(0, m)
            dve.wait_ge(s_conv_mm, 1)
            V.tensor_scalar(yT[:, 0, BANK:2 * BANK], ps[:, 2, :], c_("convb", 0), None, ALU.add).then_inc(s_y1, 1)
            dve.wait_ge(ld_consts, 16)
            dve.wait_ge(ld_small, 48)
            for i in range(4):
                V.tensor_tensor(tables[:, i, :], k_("cos" if i % 2 == 0 else "sin"), ropew[:, i, :],
                                ALU.mult).then_inc(s_tables_ready, 1)
            dve.wait_ge(s_ada_mm, 1)
            V.tensor_tensor(ada[:], ps[:, 4, 0:NADA * BATCH].rearrange("p (n b) -> p n b", n=NADA),
                            over(c_("adab", 0, NADA), BATCH), ALU.add).then_inc(s_ada_ready, 1)
            dve.wait_ge(s_ada_ready, 1)
            for i in (DK, 4 * DK):
                link(V.tensor_scalar(ada[:, i:i + DK, :], ada[:, i:i + DK, :], 1.0, None, ALU.add))
            dve.wait_ge(s_y1, 1)
            split_y(1, 0)
            dve.wait_ge(s_tables_ready, 4)

            def rope(t):
                for k in range(QK):
                    m = QK * t + k
                    dve.wait_ge(s_raw_ready, m + 1)
                    src = raw[:, m % NR, :]
                    i = 0
                    if k == 0:
                        dve.wait_ge(s_nrm_ready, 2 * t + 1)
                        link(V.tensor_tensor(kn.rearrange("p (h d) -> p h d", h=4), src.rearrange("p (h d) -> p h d", h=4),
                                             over(nrm[:, t % 2, 0:HKV], DH), ALU.mult))
                        src = kn
                        i = 2
                        if t >= 1:
                            dve.wait_ge(s_qkT_in_psum, QK * t)
                    s4 = src.rearrange("p (h d) -> p h d", h=4)
                    q4 = qr[:, k * BANK:(k + 1) * BANK].rearrange("p (h d) -> p h d", h=4)
                    r4 = r2.rearrange("p (h d) -> p h d", h=4)
                    V.tensor_tensor(q4, s4, rep(tables[:, i, :], 4), ALU.mult)
                    V.tensor_tensor(r4[:, :, 0:HD], s4[:, :, HD:DH], rep(tables[:, i + 1, 0:HD], 4), ALU.mult)
                    link(V.tensor_tensor(r4[:, :, HD:DH], s4[:, :, 0:HD], rep(tables[:, i + 1, HD:DH], 4), ALU.mult))
                    V.tensor_tensor(q4, q4, r4, ALU.add).then_inc(s_roped, 1)
                    dve.wait_ge(s_roped, m + 1)

            def softmax_tail(e_sem, e_count, slot, bd_sem, pv_sem, pv_count):
                dve.wait_ge(e_sem, e_count)
                link(V.tensor_reduce(sm_d[:], sm_e[:], AX_X, ALU.add))
                link(V.reciprocal(sm_r[:], sm_d[:]))
                link(V.tensor_tensor(sm_e[:], sm_e[:], over(sm_r[:], SEQ), ALU.mult))
                if pv_count:
                    dve.wait_ge(pv_sem, pv_count)
                for b in range(BT):
                    rows = slice(SEQ * b, SEQ * (b + 1))
                    V.transpose(bd[rows, slot, :, b, :], sm_e[rows]).then_inc(bd_sem, 1)

            def softmax0_head(t):
                dve.wait_ge(s_nrm_ready, 2 * t + 2)
                dve.wait_ge(s_s0, t + 1)
                V.tensor_tensor(sm_s[:], ps[:, 4, :].rearrange("p (h k) -> p h k", h=HQ),
                                over(nrm[:, t % 2, HKV:HKV + HQ], SEQ), ALU.mult).then_inc(s_s0_taken, 1)
                dve.wait_ge(s_s0_taken, t + 1)
                link(V.tensor_tensor(sm_s[:], sm_s[:], rep(k_("causal"), HQ), ALU.add))
                link(V.tensor_reduce(sm_m[:], sm_s[:], AX_X, ALU.max))
                V.tensor_tensor(sm_s[:], sm_s[:], over(sm_m[:], SEQ), ALU.subtract).then_inc(s_s0_shifted, 1)

            QUARTER = SEQ // 4
            for s in range(TILES + 1):
                if s >= 1:
                    if s == 1:
                        dve.wait_ge(s_bd_zero, 1)
                    softmax0_head(s - 1)
                    softmax_tail(s_e0, s, (s - 1) % 2, s_bd0, s_pv0, 4 * (s - 2) if s >= 3 else 0)
                if s < TILES:
                    rope(s)
                if s < 4:
                    for delay in range(s * QUARTER, (s + 1) * QUARTER):
                        link(tap(1, 1, delay))
                    if s == 3:
                        split_y(1, 1)
                if s >= 1:
                    dve.wait_ge(s_o0, s)
                    dve.wait_ge(s_squares, (4 * QK + 1) * (s - 1) + 1)
                    V.tensor_tensor(hid[:, s - 1, :], ps[:, 7, 0:D], hid[:, s - 1, :], ALU.add).then_inc(s_hid_attn, 1)

            def to_h2(t):
                dve.wait_ge(s_hnT, t + 1)
                s = slice(t * P, (t + 1) * P)
                for m in range(DK):
                    V.tensor_scalar(h2[:, m, s], ps[:, 2 + t % 2, m * P:(m + 1) * P], c_("fnw", m), None,
                                    ALU.mult).then_inc(s_h2_f32, 1)
                dve.wait_ge(s_h2_f32, DK * (t + 1))
                link(V.tensor_copy(act_hi[:, :, s], h2[:, :, s]))
                V.tensor_tensor(act_lo[:, :, s], h2[:, :, s], f32(act_hi[:, :, s]), ALU.subtract).then_inc(s_h2_ready, 1)

            for t in range(TILES + 1):
                if t < TILES:
                    dve.wait_ge(s_frstd, t + 1)
                    if t >= 2:
                        dve.wait_ge(s_hnT, t - 1)
                    V.tensor_scalar(hn[:, t % 2, :], hid[:, t, :], stat[:, 24 + t:25 + t], None,
                                    ALU.mult).then_inc(s_hn_ready, 1)
                if t >= 1:
                    to_h2(t - 1)

            def shifted(logits, bias):
                src = logits
                if bias is not None:
                    link(V.tensor_tensor(rt[:, 0], logits, rep(bias, TILES), ALU.add))
                    src = rt[:, 0]
                link(V.tensor_reduce(bst[:, :, 0], src, AX_X, ALU.max))
                return V.tensor_tensor(rt[:, 1], src, over(bst[:, :, 0], NE), ALU.subtract)

            def probs():
                link(V.tensor_reduce(bst[:, :, 1], rt[:, 2], AX_X, ALU.add))
                link(V.reciprocal(bst[:, :, 2], bst[:, :, 1]))
                link(V.tensor_tensor(rt[:, 3], rt[:, 2], over(bst[:, :, 2], NE), ALU.mult))
                for t in range(TILES):
                    ins = V.max(rt[:, 4, t, :], rt[:, 3, t, :])
                link(ins)
                for t in range(TILES):
                    ins = V.max_index(ridx[:, t, :], rt[:, 4, t, :], rt[:, 3, t, :])
                link(ins)
                link(V.tensor_copy(rt[:, 5], ridx[:]))

            def one_hot(dst, k):
                return V.tensor_tensor(dst, rep(k_("iota"), TILES), over(rt[:, 5, :, k], NE), ALU.is_equal)

            dve.wait_ge(s_glog, TILES)
            shifted(ps[:, 0, 0:TILES * NE].rearrange("p (t e) -> p t e", t=TILES), None).then_inc(s_gsh, 1)
            dve.wait_ge(s_gexp, 1)
            probs()
            link(V.tensor_tensor(bst[:, :, 3], rt[:, 4, :, 0], rt[:, 4, :, 1], ALU.add))
            link(V.tensor_scalar(bst[:, :, 3], bst[:, :, 3], 1e-9, None, ALU.add))
            link(V.reciprocal(bst[:, :, 4], bst[:, :, 3]))
            link(V.tensor_tensor(rt[:, 6], rt[:, 4], over(bst[:, :, 4], NE), ALU.mult))
            link(one_hot(rt[:, 7], 0))
            link(one_hot(rt[:, 8], 1))
            link(V.tensor_tensor(rt[:, 7], rt[:, 7], over(rt[:, 6, :, 0], NE), ALU.mult))
            link(V.tensor_tensor(rt[:, 8], rt[:, 8], over(rt[:, 6, :, 1], NE), ALU.mult))
            V.tensor_tensor(rt[:, 9], rt[:, 7], rt[:, 8], ALU.add).then_inc(s_comb, 1)

            for n in range(NM):
                m, c = divmod(n, CHUNKS)
                dve.wait_ge(s_sg_ready, n + 1)
                dve.wait_ge(s_moe_u, n + 1)
                if n >= 1:
                    dve.wait_ge(s_hm_ready, n)
                V.tensor_tensor(hu_, sg[:, n % 2, :], ps[:, 5 + 2 * (n % 2), :], ALU.mult).then_inc(s_hu_ready, 1)
                dve.wait_ge(s_hu_ready, n + 1)
                dve.wait_ge(ld_cb[m % SS], 32 * (m // SS + 1))
                if n >= 3:
                    dve.wait_ge(s_hm_used, n - 2)
                V.tensor_tensor(hm[:, n % 3, :], hu_, cb[:, m % SS, c * BANK:(c + 1) * BANK],
                                ALU.mult).then_inc(s_hm_ready, 1)
            dve.wait_ge(ld_xtok, 16)
            for a in range(4):
                t2 = slice(2 * a, 2 * a + 2)
                if a == 0:
                    dve.wait_ge(s_hm_used, NM)
                link(V.tensor_tensor(hid[:, t2, :], ps[:, a, :].rearrange("p (b n) -> p b n", b=2), hid[:, t2, :], ALU.add))
                V.tensor_tensor(xres[:, t2, :], xres[:, t2, :], hid[:, t2, :], ALU.add).then_inc(s_x1_ready, 1)

            def ln_stats(src, t, done_sem):
                link(V.bn_stats(bst[:, t, 0:6], src))
                V.bn_aggr(bst[:, t, 6:8], bst[:, t, 0:6]).then_inc(done_sem, 1)

            def ln_apply(dst, src, t, r, done_sem):
                V.tensor_scalar(dst, src, bst[:, t, 6:7], stat[:, r + t:r + t + 1], ALU.subtract,
                                ALU.mult).then_inc(done_sem, 1)

            def modulate(src, t, scale, shift, done_sem):
                four = "p (m b l) -> p m b l"
                s = slice(t * P, (t + 1) * P)
                b4 = slice(BT * t, BT * (t + 1))
                m4 = mt[:, t % 2, :].rearrange(four, m=DK, b=BT)
                m3 = mt[:, t % 2, :].rearrange("p (m n) -> p m n", m=DK)
                link(V.tensor_tensor(m4, src.rearrange(four, m=DK, b=BT),
                                     over(ada[:, scale * DK:(scale + 1) * DK, b4], SEQ), ALU.mult))
                link(V.tensor_tensor(m4, m4, over(ada[:, shift * DK:(shift + 1) * DK, b4], SEQ), ALU.add))
                link(V.tensor_copy(act_hi[:, :, s], m3))
                V.tensor_tensor(act_lo[:, :, s], m3, f32(act_hi[:, :, s]), ALU.subtract).then_inc(done_sem, 1)

            def ln1(tiles):
                a = tiles[0]
                for t in range(a, a + CT + 2):
                    if t < a + CT:
                        dve.wait_ge(s_x1_ready, t // 2 + 1)
                        ln_stats(xres[:, t, :], t, s_lnst)
                    if a + 1 <= t <= a + CT:
                        dve.wait_ge(s_lrstd, t)
                        if t >= 3:
                            dve.wait_ge(s_zT, t - 2)
                        ln_apply(z[:, (t - 1) % 2, :], xres[:, t - 1, :], t - 1, 32, s_z_ready)
                    if t >= a + 2:
                        dve.wait_ge(s_zT, t - 1)
                        modulate(ps[:, 4 + t % 2, 0:D], t - 2, 1, 0, s_xn1_ready)

            ln1(range(0, CT))
            ln1(range(CT, TILES))

            def softmax1_head(u):
                dve.wait_ge(s_s1, u + 1)
                s4 = ps[:, 2, :].rearrange("p (h k) -> p h k", h=16)
                link(V.tensor_reduce(sm_m[:], s4, AX_X, ALU.max))
                V.tensor_tensor(sm_s[:], s4, over(sm_m[:], SEQ), ALU.subtract).then_inc(s_s1_shifted, 1)

            def low_heads(u):
                for h in range(4):
                    n = 4 * u + h
                    dve.wait_ge(s_pv1_hi, n + 1)
                    V.scalar_tensor_tensor(flat(strm_lo[:, n % SS]), ps[:, 4 + n % 2, :], c_("bv", 4 * (u // CHUNKS) + h),
                                           flat(f32(strm_hi[:, n % SS])), ALU.add, ALU.subtract).then_inc(s_pv1_lo, 1)

            def add_out(u):
                j, c = divmod(u, CHUNKS)
                dve.wait_ge(s_out1, 4 * (u + 1))
                for m in range(DK):
                    dst, src = yT[:, m, c * BANK:(c + 1) * BANK], ps[:, 6 + m, :]
                    if j == 0:
                        ins = V.tensor_copy(dst, src)
                    else:
                        ins = V.tensor_tensor(dst, src, dst, ALU.add)
                    ins.then_inc(s_acc1, 1)

            def gated(acc, gate, bias, c, m):
                s = slice(c * BANK, (c + 1) * BANK)
                link(V.scalar_tensor_tensor(batches(yT[:, m, s], CB), batches(acc, CB), c_(bias, m),
                                            over(ada[:, gate * DK + m, CB * c:CB * (c + 1)], SEQ), ALU.add, ALU.mult))
                return V.tensor_tensor(xT[:, m, s], xT[:, m, s], yT[:, m, s], ALU.add)

            def residual2(c):
                dve.wait_ge(s_acc1, DK * (U - CHUNKS + c + 1))
                dve.wait_ge(s_xT1_copied, TILES)
                for m in range(DK):
                    gated(yT[:, m, c * BANK:(c + 1) * BANK], 2, "outb", c, m).then_inc(s_x2_ready, 1)

            def norm2(c):
                for t in range(c * CT, (c + 1) * CT + 1):
                    if t < (c + 1) * CT:
                        dve.wait_ge(s_x2s_copied, t + 1)
                        ln_stats(x2s[:, t, :], t, s_ln2st)
                    if t > c * CT:
                        dve.wait_ge(s_l2rstd, t)
                        ln_apply(z2[:, t - 1, :], x2s[:, t - 1, :], t - 1, 40, s_z2_ready)

            def modulate2(c):
                for t in range(c * CT, (c + 1) * CT):
                    dve.wait_ge(s_z2T, t + 1)
                    modulate(ps[:, t % 2, 0:D], t, 4, 3, s_xn3_ready)

            for u in range(U + 1):
                if u < U:
                    softmax1_head(u)
                if u >= 1:
                    if u == U:
                        residual2(0)
                        norm2(0)
                    low_heads(u - 1)
                if u < U:
                    softmax_tail(s_e1, u + 1, u % 2, s_bd1, s_pv1, 4 * (u - 1) if u >= 2 else 0)
                if u >= 1:
                    add_out(u - 1)
            residual2(1)
            modulate2(0)
            norm2(1)
            modulate2(1)
            for n in range(NF):
                dve.wait_ge(s_gelu, n + 1)
                if n >= 4:
                    dve.wait_ge(s_ffn_down, n - 3)
                V.tensor_copy(w_hi2[:, n % 4, :], g32[:, n % 2, :]).then_inc(s_ghi, 1)
                dve.wait_ge(s_ghi, n + 1)
                V.tensor_tensor(w_lo2[:, n % 4, :], g32[:, n % 2, :], f32(w_hi2[:, n % 4, :]),
                                ALU.subtract).then_inc(s_glo, 1)
            dve.wait_ge(s_x2_ready, DK * CHUNKS)
            for c in range(CHUNKS):
                s = slice(c * BANK, (c + 1) * BANK)
                dve.wait_ge(s_ffn_down, NF - CHUNKS + 1 + c)
                for m in range(DK):
                    gated(ps[:, 2 * c + m, :], 5, "b2", c, m).then_inc(s_x4_ready, 1)
                dve.wait_ge(s_x4_ready, DK * (c + 1))
                link(V.tensor_copy(act_hi[:, :, s], xT[:, :, s]))
                V.tensor_tensor(act_lo[:, :, s], xT[:, :, s], f32(act_hi[:, :, s]), ALU.subtract).then_inc(s_x4_split, 1)
            dve.wait_ge(s_rlog, TILES)
            shifted(ps[:, 0, 0:TILES * NE].rearrange("p (t e) -> p t e", t=TILES), c_("br", 0, NE)).then_inc(s_rsh, 1)
            dve.wait_ge(s_rexp, 1)
            probs()
            link(one_hot(rt[:, 7], 0))
            V.scalar_tensor_tensor(rt[:, 9], rt[:, 7], 1.0 / RANK, over(rt[:, 4, :, 0], NE), ALU.mult,
                                   ALU.mult).then_inc(s_wsel, 1)
            for n in range(NL):
                m, c = divmod(n, CHUNKS)
                dve.wait_ge(s_lora_up, n + 1)
                dve.wait_ge(ld_cb1[m], 32)
                if n >= 3:
                    dve.wait_ge(s_hmk_used, n - 2)
                V.tensor_tensor(hmk[:, n % 3, :], ps[:, 4 + n % 4, :], cb1[:, m, c * BANK:(c + 1) * BANK],
                                ALU.mult).then_inc(s_hmk_ready, 1)
            for a in range(4):
                t2 = slice(2 * a, 2 * a + 2)
                dve.wait_ge(s_hmk_used, NL - 1 + a // 2)
                V.tensor_tensor(xres[:, t2, :], ps[:, a, :].rearrange("p (b n) -> p b n", b=2), xres[:, t2, :],
                                ALU.add).then_inc(s_y_ready, 1)

        @block.tensor
        def _(pe):
            mm = nc.tensor.matmul

            def tokens(t):
                return slice(t * P, (t + 1) * P)

            def split_mm(dst, terms, start=True, stop=True):
                for i, (ah, al, bh, bl) in enumerate(terms):
                    mm(dst, ah, bh, start=start and i == 0, stop=False)
                    mm(dst, ah, bl, start=False, stop=False)
                    last = mm(dst, al, bh, start=False, stop=stop and i == len(terms) - 1)
                return last

            pe.wait_ge(ld_x, 16)
            src, dst = batches(xT[:, 0, BANK:2 * BANK], CB), batches(ps[:, 2, :], CB)
            for delay in range(SEQ):
                pe.wait_ge(s_diag, delay + 1)
                last = mm(dst[:, :, delay:SEQ], diag[:, delay, :], src[:, :, 0:SEQ - delay], start=(delay == 0),
                          stop=(delay == SEQ - 1))
            last.then_inc(s_conv_mm, 1)
            pe.wait_ge(ld_ada, 32)
            for n in range(NADA):
                for m in range(DK):
                    last = mm(ps[:, 4, n * BATCH:(n + 1) * BATCH], wada[:, m, n * P:(n + 1) * P], cond[:, m, :],
                              start=(m == 0), stop=(m == DK - 1))
            last.then_inc(s_ada_mm, 1)

            def turn_y(t):
                pe.wait_ge(s_yw_ready, DK * (t // CT + 1))
                if t >= 2:
                    pe.wait_ge(s_hid_attn, t - 1)
                for m in range(DK):
                    last = nc.tensor.transpose(ps[:, 7, m * P:(m + 1) * P], yT[:, m, tokens(t)], ident)
                last.then_inc(s_ytok_T, 1)

            def proj(t):
                for k in range(NPROJ):
                    n = NPROJ * t + k
                    if t == 0:
                        pe.wait_ge(s_piece_lo, k + 1)
                    if n >= 2:
                        a, b = divmod(n - 2, NPROJ)
                        if b == NPROJ - 1:
                            pe.wait_ge(s_v0_ready, a + 1)
                        else:
                            pe.wait_ge(s_squares, (4 * QK + 1) * a + 1 + 4 * (b + 1))
                    split_mm(ps[:, n % 2, :],
                             [(act_hi[:, m, tokens(t)], act_lo[:, m, tokens(t)], w_hi[:, k, m, :], w_lo[:, k, m, :])
                              for m in range(DK)]).then_inc(s_proj0, 1)

            def turn_qk(t):
                for k in range(QK):
                    f = QK * t + k
                    pe.wait_ge(s_roped, f + 1)
                    if f >= 2:
                        pe.wait_ge(s_qkT_copied, f - 1)
                    for h in range(4):
                        last = nc.tensor.transpose(ps[:, 2 + f % 2, h * DH:(h + 1) * DH],
                                                   qr[:, k * BANK + h * DH:k * BANK + (h + 1) * DH], ident)
                    last.then_inc(s_qkT_in_psum, 1)

            def scores0(t):
                pe.wait_ge(s_qkT_copied, QK * (t + 1))
                if t == 0:
                    pe.wait_ge(s_ada_ready, 1)
                if t >= 1:
                    pe.wait_ge(s_s0_taken, t)
                for h in range(HQ):
                    for b in range(BT):
                        q = BANK + h * P + b * SEQ
                        k = (h // REP) * P + b * SEQ
                        last = mm(ps[b * SEQ:(b + 1) * SEQ, 4, h * SEQ:(h + 1) * SEQ], qkT[:, q:q + SEQ],
                                  qkT[:, k:k + SEQ], start=True, stop=True)
                last.then_inc(s_s0, 1)

            def pv0(t):
                pe.wait_ge(s_v0_ready, t + 1)
                pe.wait_ge(s_bd0, BT * (t + 1))
                for j in range(HKV):
                    n = 4 * t + j
                    if n >= 2:
                        pe.wait_ge(s_pv0_copied, n - 1)
                    mm(ps[:, 5 + n % 2, :], v0[:, t % 2, j * DH:(j + 1) * DH],
                       bd[:, t % 2, REP * j:REP * (j + 1)].rearrange("p h b q -> p (h b q)"),
                       start=True, stop=True).then_inc(s_pv0, 1)

            def oproj(t):
                if t + 1 < TILES:
                    pe.wait_ge(s_ytok_copied, t + 2)
                    pe.wait_ge(s_squares, (4 * QK + 1) * (t + 1) + 1)
                else:
                    pe.wait_ge(s_hid_attn, t)
                for h in range(HQ):
                    if h % REP == 0:
                        pe.wait_ge(s_pv0_copied, 4 * t + h // REP + 1)
                    last = mm(ps[:, 7, 0:D], attnT[:, h * P:(h + 1) * P], wo0[:, h, :], start=(h == 0), stop=(h == HQ - 1))
                last.then_inc(s_o0, 1)

            for s in range(TILES + 1):
                if s < TILES:
                    turn_y(s)
                    proj(s)
                if s >= 1:
                    if s == 1:
                        pe.wait_ge(ld_o0, 16)
                    pv0(s - 1)
                    oproj(s - 1)
                if s < TILES:
                    if s == 0:
                        pe.wait_ge(s_y1, 1)
                    turn_qk(s)
                    scores0(s)

            pe.wait_ge(ld_small, 48)
            pe.wait_ge(s_qkT_copied, QK * TILES)
            pe.wait_ge(s_v0_ready, TILES)
            pe.wait_ge(s_squares, (4 * QK + 1) * TILES)

            def logits0(t):
                pe.wait_ge(s_h2_f32, DK * (t + 1))
                for m in range(DK):
                    last = mm(ps[:, 0, t * NE:(t + 1) * NE], h2[:, m, tokens(t)], gate_w[:, m, :],
                              start=(m == 0), stop=(m == DK - 1))
                last.then_inc(s_glog, 1)

            for t in range(TILES + 1):
                if t < TILES:
                    pe.wait_ge(s_hn_ready, t + 1)
                    if t >= 2:
                        pe.wait_ge(s_h2_f32, DK * (t - 1))
                    for m in range(DK):
                        last = nc.tensor.transpose(ps[:, 2 + t % 2, m * P:(m + 1) * P], hn[:, t % 2, m * P:(m + 1) * P],
                                                   ident)
                    last.then_inc(s_hnT, 1)
                if t >= 1:
                    logits0(t - 1)

            def halves(f, part, s):
                return [(strm_hi[:, f % SS, part + k, :], strm_lo[:, f % SS, part + k, :], act_hi[:, k, s], act_lo[:, k, s])
                        for k in range(DK)]

            def moe_up(n):
                m, c = divmod(n, CHUNKS)
                s = slice(c * BANK, (c + 1) * BANK)
                if c == 0:
                    pe.wait_ge(s_slice_lo, m + 1)
                if n < CHUNKS:
                    pe.wait_ge(s_h2_ready, CT * (c + 1))
                if n >= 2:
                    pe.wait_ge(s_sg_ready, n - 1)
                split_mm(ps[:, 4 + 2 * (n % 2), :], halves(m, 0, s)).then_inc(s_moe_g, 1)
                if n >= 2:
                    pe.wait_ge(s_hu_ready, n - 1)
                split_mm(ps[:, 5 + 2 * (n % 2), :], halves(m, DK, s)).then_inc(s_moe_u, 1)

            def moe_down(n):
                m, c = divmod(n, CHUNKS)
                pe.wait_ge(s_hm_ready, n + 1)
                for t in range(CT):
                    last = mm(ps[:, 2 * c + t // 2, (t % 2) * D:(t % 2 + 1) * D], hm[:, n % 3, t * P:(t + 1) * P],
                              raw_t[:, m % SS, 2 * D:3 * D], start=(m == 0 and t % 2 == 0), stop=(m == MI - 1),
                              skip_group_check=True)
                last.then_inc(s_hm_used, 1)

            pe.wait_ge(s_hid_attn, TILES)
            for n in range(NM + 2):
                if n < NM:
                    moe_up(n)
                if n == 1:
                    pe.wait_ge(s_comb, 1)
                    for t in range(TILES):
                        nc.tensor.transpose(ps[0:NE, 2 + t // CT, (t % CT) * P:(t % CT + 1) * P], rt[:, 9, t, :],
                                            ident).then_inc(s_combT_psum, 1)
                    pe.wait_ge(s_combT_ready, CHUNKS)
                if n >= 2:
                    moe_down(n - 2)

            def turn_z(t):
                pe.wait_ge(s_z_ready, t + 1)
                if t >= 2:
                    pe.wait_ge(s_xn1_ready, t - 1)
                    pe.wait_ge(s_xT1_copied, t - 1)
                for m in range(DK):
                    nc.tensor.transpose(ps[:, 4 + t % 2, m * P:(m + 1) * P], z[:, t % 2, m * P:(m + 1) * P], ident)
                for m in range(DK):
                    last = nc.tensor.transpose(ps[:, 6 + t % 2, m * P:(m + 1) * P], xres[:, t, m * P:(m + 1) * P], ident)
                last.then_inc(s_zT, 1)

            def proj1(u):
                j, c = divmod(u, CHUNKS)
                s = slice(c * BANK, (c + 1) * BANK)
                pe.wait_ge(s_xn1_ready, CT * (c + 1))
                for k in range(12):
                    n = 12 * u + k
                    i = 4 * j + k // 4
                    w = i % WSLOTS
                    if k % 4 == 0:
                        pe.wait_ge(s_piece_lo, NPROJ + i + 1)
                    if n >= 2:
                        pe.wait_ge(s_q1_copied, n - 1)
                    if k < 8:
                        h = slice((k % 4) * DH, (k % 4 + 1) * DH)
                        terms = [(w_hi[:, w, m, h], w_lo[:, w, m, h], act_hi[:, m, s], act_lo[:, m, s]) for m in range(DK)]
                    else:
                        t = tokens(c * CT + k - 8)
                        terms = [(act_hi[:, m, t], act_lo[:, m, t], w_hi[:, w, m, :], w_lo[:, w, m, :]) for m in range(DK)]
                    split_mm(ps[:, n % 2, :], terms).then_inc(s_proj1, 1)

            def scores1(u):
                pe.wait_ge(s_q1_copied, 12 * u + 8)
                if u >= 1:
                    pe.wait_ge(s_s1_shifted, u)
                for h in range(4):
                    for t in range(CT):
                        for b in range(BT):
                            q = h * BANK + t * P + b * SEQ
                            k = 4 * h + t
                            last = mm(ps[b * SEQ:(b + 1) * SEQ, 2, k * SEQ:(k + 1) * SEQ], qT1[:, q:q + SEQ],
                                      kT1[:, q:q + SEQ], start=True, stop=True)
                last.then_inc(s_s1, 1)

            def pv1(u, h):
                n = 4 * u + h
                if h == 0:
                    pe.wait_ge(s_q1_copied, 12 * (u + 1))
                    pe.wait_ge(s_bd1, BT * (u + 1))
                if n >= 2:
                    pe.wait_ge(s_pv1_lo, n - 1)
                for t in range(CT):
                    last = mm(ps[:, 4 + n % 2, t * P:(t + 1) * P], v1[:, u % 2, t, h * DH:(h + 1) * DH],
                              bd[:, u % 2, 4 * h + t].rearrange("p b q -> p (b q)"), start=True, stop=True)
                last.then_inc(s_pv1, 1)

            def out1(u, h):
                n = 4 * u + h
                i = 4 * (u // CHUNKS) + 3
                w = i % WSLOTS
                pe.wait_ge(s_pv1_lo, n + 1)
                if h == 0:
                    pe.wait_ge(s_piece_lo, NPROJ + i + 1)
                    if u >= 1:
                        pe.wait_ge(s_acc1, DK * u)
                for m in range(DK):
                    at = (h % 2) * D + m * P
                    last = split_mm(ps[:, 6 + m, :], [(w_hi[:, w, h // 2, at:at + P], w_lo[:, w, h // 2, at:at + P],
                                                       flat(strm_hi[:, n % SS]), flat(strm_lo[:, n % SS]))],
                                    start=(h == 0), stop=(h == 3))
                last.then_inc(s_out1, 1)

            def heads1(u):
                pv1(u, 0)
                pv1(u, 1)
                out1(u, 0)
                pv1(u, 2)
                out1(u, 1)
                pv1(u, 3)
                out1(u, 2)
                out1(u, 3)

            def turn_x2(c):
                pe.wait_ge(s_x2_ready, DK * (c + 1))
                for t in range(c * CT, (c + 1) * CT):
                    if t >= 2:
                        pe.wait_ge(s_x2s_copied, t - 1)
                    for m in range(DK):
                        last = nc.tensor.transpose(ps[:, 2 + t % 2, m * P:(m + 1) * P], xT[:, m, tokens(t)], ident)
                    last.then_inc(s_x2T, 1)

            def turn_z2(c):
                for t in range(c * CT, (c + 1) * CT):
                    pe.wait_ge(s_z2_ready, t + 1)
                    if t >= 2:
                        pe.wait_ge(s_xn3_ready, t - 1)
                    for m in range(DK):
                        last = nc.tensor.transpose(ps[:, t % 2, m * P:(m + 1) * P], z2[:, t, m * P:(m + 1) * P], ident)
                    last.then_inc(s_z2T, 1)

            pe.wait_ge(s_x1_ready, 1)
            for t in range(CT):
                turn_z(t)
            pe.wait_ge(s_x1_ready, 4)
            for u in range(U + 1):
                if u < U:
                    proj1(u)
                    scores1(u)
                if u == 0:
                    for t in range(CT, TILES):
                        turn_z(t)
                    pe.wait_ge(s_xn1_ready, TILES)
                    pe.wait_ge(s_xT1_copied, TILES)
                if u == U:
                    pe.wait_ge(s_s1_shifted, U)
                    turn_x2(0)
                if u >= 1:
                    heads1(u - 1)
            pe.wait_ge(s_q1_copied, 12 * U)
            turn_z2(0)
            turn_x2(1)

            def ffn_up(n):
                m, c = FFN[n]
                s = slice(c * BANK, (c + 1) * BANK)
                if c == 0:
                    pe.wait_ge(s_slice_lo, MI + m + 1)
                pe.wait_ge(s_xn3_ready, CT * (c + 1))
                if n >= 4:
                    pe.wait_ge(s_gelu, n - 3)
                split_mm(ps[:, 4 + n % 4, :], halves(m, 0, s)).then_inc(s_ffn_up, 1)

            def ffn_down(n):
                m, c = FFN[n]
                pe.wait_ge(s_glo, n + 1)
                for d in range(DK):
                    last = split_mm(ps[:, 2 * c + d, :], [(strm_hi[:, m % SS, DK + d, :], strm_lo[:, m % SS, DK + d, :],
                                                           w_hi2[:, n % 4, :], w_lo2[:, n % 4, :])],
                                    start=(m == 0), stop=(m == MM - 1))
                last.then_inc(s_ffn_down, 1)

            pe.wait_ge(s_acc1, DK * U)
            for n in range(NF + 2):
                if n < NF:
                    ffn_up(n)
                if n == 1:
                    turn_z2(1)
                    pe.wait_ge(s_xn3_ready, TILES)
                if n >= 2:
                    ffn_down(n - 2)

            pe.wait_ge(s_x4_ready, DK)

            def lora_up(n):
                m, c = divmod(n, CHUNKS)
                s = slice(c * BANK, (c + 1) * BANK)
                pe.wait_ge(s_x4_split, c + 1)
                if c == 0:
                    pe.wait_ge(s_slice_lo, MI + MM + m + 1)
                if n >= 4:
                    pe.wait_ge(s_hmk_ready, n - 3)
                if n < 4:
                    pe.wait_ge(s_gelu, NF)
                split_mm(ps[:, 4 + n % 4, :], halves(MM + m, 0, s)).then_inc(s_lora_up, 1)

            def lora_down(n):
                m, c = divmod(n, CHUNKS)
                pe.wait_ge(s_hmk_ready, n + 1)
                for t in range(CT):
                    last = mm(ps[:, 2 * c + t // 2, (t % 2) * D:(t % 2 + 1) * D], hmk[:, n % 3, t * P:(t + 1) * P],
                              raw_t[:, (MM + m) % SS, D:2 * D], start=(m == 0 and t % 2 == 0), stop=(m == MR - 1),
                              skip_group_check=True)
                last.then_inc(s_hmk_used, 1)

            for t in range(TILES):
                pe.wait_ge(s_x4_ready, DK * (t // CT + 1))
                for m in range(DK):
                    last = mm(ps[:, 0, t * NE:(t + 1) * NE], xT[:, m, tokens(t)], r_w[:, m, :],
                              start=(m == 0), stop=(m == DK - 1))
                last.then_inc(s_rlog, 1)
            for n in range(4):
                lora_up(n)
            pe.wait_ge(s_wsel, 1)
            for t in range(TILES):
                nc.tensor.transpose(ps[0:NE, 2 + t // CT, (t % CT) * P:(t % CT + 1) * P], rt[:, 9, t, :],
                                    ident).then_inc(s_selT_psum, 1)
            pe.wait_ge(s_selT_ready, CHUNKS)
            for n in range(NL):
                lora_down(n)
                if n + 4 < NL:
                    lora_up(n + 4)


def _by_row(a, n):
    return np.ascontiguousarray(a.reshape(n, P, -1).transpose(1, 0, 2))


def _columns(a):
    return a.reshape(-1, P).T


def _constants():
    freqs = (1.0 / np.float32(1000000.0) ** (np.arange(0, DH, 2, dtype=np.float32) / np.float32(DH))).astype(np.float32)
    angle = np.outer(np.arange(SEQ, dtype=np.float32), freqs).astype(np.float32)
    cos, sin = np.cos(angle), np.sin(angle)
    causal = np.where(np.tril(np.ones((SEQ, SEQ), bool)), 0.0, NEG)
    return np.concatenate([
        np.eye(P), np.tile(np.concatenate([cos, cos], 1), (BT, 1)), np.tile(np.concatenate([-sin, sin], 1), (BT, 1)),
        np.tile(causal, (BT, 1)), np.tile(np.arange(NE), (P, 1))], axis=1).astype(np.float32)


def kernel(**inputs):
    import concourse.bacc as bacc
    from concourse.bass_utils import run_bass_kernel_spmd

    a = {k: np.asarray(v) for k, v in inputs.items()}
    x = a["x"].reshape(TOK, D)
    qw, kw = a["L0_ffn_q_norm_w"], a["L0_ffn_k_norm_w"]
    turn = np.roll(np.arange(DH), -(DH // 2))
    rope_w = np.stack([qw, qw[turn], kw, kw[turn]])
    qkv_b = a["L1_cond_qkv_b"].reshape(3, HQ * DH)
    cols = np.concatenate([
        _by_row(a["cond_2048"].T, DK).reshape(P, -1), _columns(a["L0_cond_b"]), _columns(a["L0_ffn_attn_norm_w"]),
        _columns(a["L0_ffn_ffn_norm_w"]), _columns(a["L1_cond_ada_b"]), _columns(qkv_b[0]), _columns(qkv_b[1]),
        _columns(qkv_b[2]), _columns(a["L1_cond_out_b"]), _columns(a["L1_cond_ffn_b1"]), _columns(a["L1_cond_ffn_b2"]),
        np.broadcast_to(a["L1_ffn_br"], (P, NE))], axis=1)
    wqkv0 = np.concatenate([a["L0_ffn_k_w"], a["L0_ffn_q_w"], a["L0_ffn_v_w"]]).T
    wqkv1 = a["L1_cond_qkv_w"].reshape(DK, P, 3, GROUPS, BANK).transpose(3, 2, 1, 0, 4).reshape(GROUPS, 3, P, PIECE)
    wo1 = a["L1_cond_out_w"].reshape(GROUPS, 1, 4, P, D).transpose(0, 1, 3, 2, 4).reshape(GROUPS, 1, P, PIECE)

    def up_slices(w, n):
        return w.reshape(DK, P, n, P).transpose(2, 1, 0, 3).reshape(n, P, D)

    arrays = {
        "x_tok": _by_row(x, TILES),
        "x_T": _by_row(x.T, DK),
        "cond_T": _by_row(a["cond_2048"].T, DK),
        "cols": cols,
        "consts": _constants(),
        "rope_w": np.broadcast_to(rope_w, (P, 4, DH)),
        "w_qkv0": wqkv0.reshape(DK, P, NPROJ, BANK).transpose(2, 1, 0, 3).reshape(NPROJ, P, PIECE),
        "w_o0": _by_row(a["L0_ffn_o_w"].T, HQ),
        "w_gate0": _by_row(a["L0_ffn_gate_w"].T, DK),
        "w_moe": np.concatenate([
            up_slices(a["L0_ffn_wg"].reshape(EI, D).T, MI), up_slices(a["L0_ffn_wu"].reshape(EI, D).T, MI),
            a["L0_ffn_wd"].transpose(0, 2, 1).reshape(MI, P, D)], axis=2),
        "w_ada": _by_row(a["L1_cond_ada_w"], DK),
        "w_attn1": np.concatenate([wqkv1, wo1], axis=1).reshape(4 * GROUPS, P, PIECE),
        "w_ffn1": np.concatenate([up_slices(a["L1_cond_ffn_w1"], MM), a["L1_cond_ffn_w2"].reshape(MM, P, D)], axis=2),
        "w_lora": np.concatenate([up_slices(a["L1_ffn_A"].reshape(ER, D).T, MR),
                                  a["L1_ffn_B"].transpose(0, 2, 1).reshape(MR, P, D)], axis=2),
        "w_r": _by_row(a["L1_ffn_Wr"].T, DK),
    }
    arrays = {k: np.ascontiguousarray(v) for k, v in arrays.items()}
    nc = bacc.Bacc("TRN2", target_bir_lowering=False, num_devices=1)
    aps = {k: nc.dram_tensor("in_" + k, v.shape, mybir.dt.from_np(v.dtype), kind="ExternalInput").ap()
           for k, v in arrays.items()}
    out = nc.dram_tensor("out", (P, TILES, D), F32, kind="ExternalOutput").ap()
    build_program(nc, out=out, **aps)
    r = run_bass_kernel_spmd(nc, [{"in_" + k: v for k, v in arrays.items()}], core_ids=[0])
    got = r.results[0]["out"]
    return got.transpose(1, 0, 2).reshape(BATCH, SEQ, D)
```

```python
from contextlib import ExitStack

import numpy as np

import concourse.bass as bass
from concourse import mybir

ALU = mybir.AluOpType
ACT = mybir.ActivationFunctionType
F32 = mybir.dt.float32
U32 = mybir.dt.uint32
F32R = mybir.dt.float32r
AX_X = mybir.AxisListType.X

P = 128
D = 256
DH = 128
DK = D // P
BATCH, SEQ = 32, 32
TOK = BATCH * SEQ
TILES = TOK // P
BT = P // SEQ
HQ, HKV = 16, 4
REP = HQ // HKV
BANK = 512
CHUNKS = TOK // BANK
CB = BANK // SEQ
CT = BANK // P
QKV0 = 2 * HKV * DH + HQ * DH
NPROJ = QKV0 // BANK
NE, INTER = 8, 176
EI = NE * INTER
MI = EI // P
GROUPS = HQ // 4
MLP = 4 * D
MM = MLP // P
RANK = 64
ER = NE * RANK
MR = ER // P
NADA = 6 * DK
NEG = -1.0e30
PIECE = DK * BANK
WSLOTS = 6
RAWS = 4
STREAM = 3 * D
SS = 3

COLS = {}
_at = 0
for _name, _n in (("convw", DK * SEQ), ("convb", DK), ("anw", DK), ("fnw", DK), ("adab", NADA),
                  ("bq", HQ), ("bk", HQ), ("bv", HQ), ("outb", DK), ("b1", MM), ("b2", DK), ("br", NE)):
    COLS[_name] = (_at, _at + _n)
    _at += _n
NCOLS = _at
CONSTS = {}
_at = 0
for _name, _n in (("ident", P), ("cos", DH), ("sin", DH), ("causal", SEQ), ("iota", NE)):
    CONSTS[_name] = (_at, _at + _n)
    _at += _n
NCONSTS = _at


def build_program(nc, x_tok, x_T, cond_T, cols, consts, rope_w, w_qkv0, w_o0, w_gate0, w_moe, w_ada,
                  w_attn1, w_ffn1, w_lora, w_r, out):
    with ExitStack() as ctx:
        def sb(name, shape, dt=F32):
            return ctx.enter_context(nc.sbuf_tensor(name, shape, dt))

        def sem(name):
            return ctx.enter_context(nc.semaphore(name))

        col = sb("col", [P, NCOLS])
        cst = sb("cst", [P, NCONSTS])
        tables = sb("tables", [P, 4, DH])
        gate_w = sb("gate_w", [P, DK, NE])
        r_w = sb("r_w", [P, DK, NE])
        cond = sb("cond", [P, DK, BATCH])
        ada = sb("ada", [P, NADA, BATCH])
        xT = sb("xT", [P, DK, TOK])
        yT = sb("yT", [P, DK, TOK])
        act_hi = sb("act_hi", [P, DK, TOK], F32R)
        act_lo = sb("act_lo", [P, DK, TOK], F32R)
        hid = sb("hid", [P, TILES, D])
        xres = sb("xres", [P, TILES, D])
        w_hi = sb("w_hi", [P, WSLOTS, DK, BANK], F32R)
        w_lo = sb("w_lo", [P, WSLOTS, DK, BANK], F32R)
        raw_w = sb("raw_w", [P, RAWS * PIECE])
        strm_hi = sb("strm_hi", [P, SS, 4, P], F32R)
        strm_lo = sb("strm_lo", [P, SS, 4, P], F32R)
        raw_s = sb("raw_s", [P, SS * STREAM])
        work = sb("work", [P, 9728])
        bd = sb("bd", [P, 2, 16, BT, SEQ])
        sm_s = sb("sm_s", [P, 16, SEQ])
        sm_e = sb("sm_e", [P, 16, SEQ])
        sm_m = sb("sm_m", [P, 16])
        sm_d = sb("sm_d", [P, 16])
        sm_r = sb("sm_r", [P, 16])
        stat = sb("stat", [P, 48])
        half = sb("half", [P, HQ])
        ssq = sb("ssq", [P, 2, HKV + HQ])
        nrm = sb("nrm", [P, 2, HKV + HQ])
        nrt = sb("nrt", [P, 2, HKV + HQ])
        junk = sb("junk", [P, 3, D])
        rt = sb("rt", [P, 10, TILES, NE])
        ridx = sb("ridx", [P, TILES, 8], U32)
        bst = sb("bst", [P, TILES, 8])
        ps = ctx.enter_context(nc.psum_tensor("ps", [P, 8, BANK], F32))
        comb_dram = nc.dram_tensor("comb_dram", [2, NE, TOK], F32, kind="Internal").ap()

        def c_(name, k=0, n=1):
            return col[:, COLS[name][0] + k:COLS[name][0] + k + n]

        def k_(name):
            return cst[:, CONSTS[name][0]:CONSTS[name][1]]

        ident = k_("ident")
        raw_p = raw_w[:].rearrange("p (s n) -> p s n", s=RAWS)
        wo0 = raw_w[:].rearrange("p (h n) -> p h n", h=HQ)
        raw_t = raw_s[:].rearrange("p (s n) -> p s n", s=SS)
        attnT = raw_s[:, 0:4 * BANK]
        ropew = sm_s[:].rearrange("p h k -> p (h k)").rearrange("p (i d) -> p i d", i=4)
        wada = bd[:].rearrange("p r a b c -> p (r a b c)")[:, 0:DK * 6 * D].rearrange("p (m n) -> p m n", m=DK)

        def carve(sizes):
            at, found = 0, []
            for n in sizes:
                found.append(work[:, at:at + n])
                at += n
            assert at <= 9728, at
            return found

        NQK = QKV0 - BANK
        NR = 5
        PTAPS = 9
        diag = work[:, 0:DK * PTAPS * P].rearrange("p (k n) -> p k n", n=P)
        raw_, qr, kn, r2, qkT, v0_ = carve([NR * BANK, NQK, BANK, BANK, NQK, 2 * BANK])
        raw = raw_.rearrange("p (r n) -> p r n", r=NR)
        v0 = v0_.rearrange("p (r n) -> p r n", r=2)
        h2_, cmbT, sg_, hu_, hm_, cb_ = carve([DK * TOK, TOK, 2 * BANK, 2 * BANK, 3 * BANK, 3 * TOK])
        h2 = h2_.rearrange("p (m n) -> p m n", m=DK)
        hn = cb_[:, 0:3 * D].rearrange("p (r n) -> p r n", r=3)
        hu = hu_.rearrange("p (r n) -> p r n", r=2)
        sg = sg_.rearrange("p (r n) -> p r n", r=2)
        hm = hm_.rearrange("p (r n) -> p r n", r=3)
        cb = cb_.rearrange("p (r n) -> p r n", r=3)
        qT1, kT1 = carve([4 * BANK, 4 * BANK])
        v1_ = work[:, 8 * BANK:16 * BANK]
        v1 = v1_.rearrange("p (r t n) -> p r t n", r=2, t=CT)
        zx = work[:, 16 * BANK:16 * BANK + 6 * D]
        z = zx[:, 0:2 * D].rearrange("p (r n) -> p r n", r=2)
        mt = zx[:, 2 * D:4 * D].rearrange("p (r n) -> p r n", r=2)
        mt2 = zx[:, 0:4 * D].rearrange("p (r n) -> p r n", r=4)
        x2s = qT1.rearrange("p (t n) -> p t n", t=TILES)
        z2 = kT1.rearrange("p (t n) -> p t n", t=TILES)
        g32 = v1_[:, 0:2 * BANK].rearrange("p (r n) -> p r n", r=2)
        hmk = v1_[:, 3 * BANK:6 * BANK].rearrange("p (r n) -> p r n", r=3)
        cb1 = work[:, 0:4 * TOK].rearrange("p (r n) -> p r n", r=MR)
        h1 = bd[:].rearrange("p r a b c -> p (r a b c)").rearrange("p (r n) -> p r n", n=BANK)
        selT = work[:, 4 * TOK + 6 * BANK:5 * TOK + 6 * BANK]
        w_hi2 = w_hi[:].rearrange("p s k n -> p (s k) n")
        w_lo2 = w_lo[:].rearrange("p s k n -> p (s k) n")
        hid_hi, hid_lo = w_hi2[:, 8:10, :], w_lo2[:, 8:10, :]
        down_hi, down_lo = (w[:, 10:12, :].rearrange("p a b -> p (a b)")[:, 0:SS * D].rearrange("p (r n) -> p r n", r=SS)
                            for w in (w_hi2, w_lo2))

        def flat(ap):
            return ap.rearrange("p a b -> p (a b)")

        def f32(ap):
            return ap.bitcast(F32)

        def batches(ap, n):
            return ap.rearrange("p (b l) -> p b l", b=n)

        def over(ap, n):
            return ap.unsqueeze(len(ap.shape)).broadcast_to([*ap.shape, n])

        def rep(ap, n):
            return ap.unsqueeze(1).broadcast_to([ap.shape[0], n, ap.shape[1]])

        ld_x = sem("ld_x")
        ld_cols = sem("ld_cols")
        ld_consts = sem("ld_consts")
        ld_piece = [sem(f"ld_piece{i}") for i in range(RAWS)]
        ld_ada = sem("ld_ada")
        ld_small = sem("ld_small")
        ld_xtok = sem("ld_xtok")
        ld_o0 = sem("ld_o0")
        ld_slice = [sem(f"ld_slice{i}") for i in range(SS)]
        st_comb = sem("st_comb")
        ld_cb = [sem(f"ld_cb{i}") for i in range(SS)]
        ld_cb1 = [sem(f"ld_cb1_{i}") for i in range(CHUNKS * MR)]
        ld_tail = sem("ld_tail")
        stored = sem("stored")
        s_out1 = sem("out1")
        s_proj1 = sem("proj1")
        s_piece_lo = sem("piece_lo")
        s_o0 = sem("o0")
        s_combT_ready = sem("combT_ready")
        s_hm_ready = sem("hm_ready")
        s_hm_used = sem("hm_used")
        s_slice_lo = sem("slice_lo")
        s_hmk_used = sem("hmk_used")
        s_selT_ready = sem("selT_ready")
        s_y_ready = sem("y_ready")
        s_pool_chain = sem("pool_chain")
        s_piece_hi = sem("piece_hi")
        s_slice_hi = sem("slice_hi")
        s_squares = sem("squares")
        s_yrstd = sem("yrstd")
        s_s0_taken = sem("s0_taken")
        s_roped = sem("roped")
        s_nrm_ready = sem("nrm_ready")
        s_ada_mm = sem("ada_mm")
        s_bd_zero = sem("bd_zero")
        s_frstd = sem("frstd")
        s_lnst = sem("lnst")
        s_lrstd = sem("lrstd")
        s_ln2st = sem("ln2st")
        s_l2rstd = sem("l2rstd")
        s_diag = sem("diag")
        s_ytok_T = sem("ytok_T")
        s_ytok_copied = sem("ytok_copied")
        s_proj0 = sem("proj0")
        s_pv0 = sem("pv0")
        s_v0_ready = sem("v0_ready")
        s_raw_ready = sem("raw_ready")
        s_s0 = sem("s0")
        s_qkT_in_psum = sem("qkT_in_psum")
        s_qkT_copied = sem("qkT_copied")
        s_pv0_copied = sem("pv0_copied")
        s_y1 = sem("y1")
        s_s0_shifted = sem("s0_shifted")
        s_e0 = sem("e0")
        s_hid_attn = sem("hid_attn")
        s_gsh = sem("gsh")
        s_gexp = sem("gexp")
        s_combT_psum = sem("combT_psum")
        s_moe_g = sem("moe_g")
        s_hu_ready = sem("hu_ready")
        s_sg_ready = sem("sg_ready")
        s_moe_u = sem("moe_u")
        s_zT = sem("zT")
        s_xT1_copied = sem("xT1_copied")
        s_s1 = sem("s1")
        s_q1_copied = sem("q1_copied")
        s_pv1 = sem("pv1")
        s_pv1_hi = sem("pv1_hi")
        s_s1_shifted = sem("s1_shifted")
        s_e1 = sem("e1")
        s_x2T = sem("x2T")
        s_x2s_copied = sem("x2s_copied")
        s_ffn_up = sem("ffn_up")
        s_glo = sem("glo")
        s_gelu = sem("gelu")
        s_ffn_down = sem("ffn_down")
        s_rsh = sem("rsh")
        s_rexp = sem("rexp")
        s_selT_psum = sem("selT_psum")
        s_lora_up = sem("lora_up")
        s_dve_chain = sem("dve_chain")
        s_yw_ready = sem("yw_ready")
        s_conv_step = sem("conv_step")
        s_conv_mm = sem("conv_mm")
        s_tap11 = sem("tap11")
        s_mod = sem("mod")
        s_hm32 = sem("hm32")
        s_hm_hi = sem("hm_hi")
        s_x4_hi = sem("x4_hi")
        s_up_copied = sem("up_copied")
        s_mod_hi = sem("mod_hi")
        s_tables_ready = sem("tables_ready")
        s_ada_ready = sem("ada_ready")
        s_bd0 = sem("bd0")
        s_hnT = sem("hnT")
        s_h2_f32 = sem("h2_f32")
        s_h2_ready = sem("h2_ready")
        s_hn_ready = sem("hn_ready")
        s_glog = sem("glog")
        s_comb = sem("comb")
        s_x1_ready = sem("x1_ready")
        s_z_ready = sem("z_ready")
        s_xn1_ready = sem("xn1_ready")
        s_pv1_lo = sem("pv1_lo")
        s_acc1 = sem("acc1")
        s_x2_ready = sem("x2_ready")
        s_z2_ready = sem("z2_ready")
        s_z2T = sem("z2T")
        s_xn3_ready = sem("xn3_ready")
        s_bd1 = sem("bd1")
        s_ghi = sem("ghi")
        s_x4_ready = sem("x4_ready")
        s_x4_split = sem("x4_split")
        s_rlog = sem("rlog")
        s_wsel = sem("wsel")
        s_hmk_ready = sem("hmk_ready")

        block = ctx.enter_context(nc.Block())
        QK = NPROJ - 1
        QK_BANK = (2, 3, 0, 1, 2)
        TAPS1 = (3, 8, 16, 26, SEQ)
        TAPS0 = 8
        U = GROUPS * CHUNKS
        NP1 = 4 * GROUPS
        NM = CHUNKS * MI
        NF = CHUNKS * MM
        NL = CHUNKS * MR
        HD = DH // 2
        MOE = [(m, c) for m in range(MI - 2) for c in range(CHUNKS)] + [
            (MI - 2, 0), (MI - 1, 0), (MI - 2, 1), (MI - 1, 1)]
        Z_BEHIND = (4, 6, 8, 10)
        FFN = ([(m, c) for c in range(CHUNKS) for m in range(SS)]
               + [(m, c) for m in range(SS, MM - SS) for c in range(CHUNKS)]
               + [(m, c) for c in range(CHUNKS) for m in range(MM - SS, MM)])
        LORA = [(m, c) for c in range(CHUNKS) for m in (0, 3, 1, 2)]

        def parts_of(n, f):
            if MI <= n < MI + MM:
                slot = (4, 5, 2, 3)[f // 2]
                return tuple(w[:, slot, f % 2, :].rearrange("p (a b) -> p a b", b=P) for w in (w_hi, w_lo))
            return strm_hi[:, f % SS], strm_lo[:, f % SS]

        def piece_free(i):
            j, s = divmod(i - WSLOTS, 4)
            u = CHUNKS * j + CHUNKS - 1
            return (s_out1, 4 * (u + 1)) if s == 3 else (s_proj1, 12 * u + 4 * (s + 1))

        @block.sync
        def _(sp):
            sp.dma_start(xT[:], x_T).then_inc(ld_x, 16)
            sp.dma_start(col[:], cols).then_inc(ld_cols, 16)
            sp.dma_start(cst[:], consts).then_inc(ld_consts, 16)
            for i in range(RAWS):
                sp.dma_start(raw_p[:, i, :], w_qkv0[i]).then_inc(ld_piece[i], 16)
            sp.dma_start(cond[:], cond_T).then_inc(ld_ada, 16)
            sp.dma_start(wada, w_ada).then_inc(ld_ada, 16)
            sp.dma_start(ropew, rope_w).then_inc(ld_small, 16)
            sp.dma_start(gate_w[:], w_gate0).then_inc(ld_small, 16)
            sp.dma_start(r_w[:], w_r).then_inc(ld_small, 16)
            for i in range(RAWS, NPROJ):
                sp.wait_ge(s_piece_lo, i - RAWS + 1)
                sp.dma_start(raw_p[:, i % RAWS, :], w_qkv0[i]).then_inc(ld_piece[i % RAWS], 16)
            sp.dma_start(xres[:], x_tok).then_inc(ld_xtok, 16)
            sp.wait_ge(s_piece_lo, NPROJ)
            sp.dma_start(wo0, w_o0).then_inc(ld_o0, 16)
            sp.wait_ge(s_o0, TILES)
            for f in range(SS):
                sp.dma_start(raw_t[:, f, :], w_moe[f]).then_inc(ld_slice[f], 16)
            for i in range(RAWS):
                sp.dma_start(raw_p[:, i, :], w_attn1[i]).then_inc(ld_piece[i], 16)
            sp.wait_ge(s_combT_ready, CHUNKS)
            sp.dma_start(comb_dram[0], cmbT[0:NE, :]).then_inc(st_comb, 16)
            sp.wait_ge(st_comb, 16)

            def spread(dst, layer, m, width, done_sem, s=slice(0, TOK)):
                lo, at = m * P, 0
                parts = []
                while at < P:
                    e = (lo + at) // width
                    n = min(P - at, (e + 1) * width - lo - at)
                    parts.append((e, at, n))
                    at += n
                if len(parts) == 1:
                    e, at, n = parts[0]
                    parts = [(e, 0, n // 2), (e, n // 2, n - n // 2)]
                for e, at, n in parts:
                    sp.dma_start(dst[at:at + n, :], comb_dram[layer, e:e + 1, s].broadcast_to([n, s.stop - s.start])).then_inc(done_sem, 16)

            for m in range(MI):
                if m >= SS:
                    sp.wait_ge(s_hm_ready, CHUNKS * (m - SS + 1))
                spread(cb[:, m % SS, :], 0, m, INTER, ld_cb[m % SS])
                if m >= SS:
                    sp.wait_ge(s_slice_lo, m - SS + 1)
                    sp.dma_start(raw_t[:, m % SS, :], w_moe[m]).then_inc(ld_slice[m % SS], 16)
                if m in (6, 7):
                    i = m - 2
                    sp.wait_ge(s_piece_lo, NPROJ + i - RAWS + 1)
                    sp.dma_start(raw_p[:, i % RAWS, :], w_attn1[i]).then_inc(ld_piece[i % RAWS], 16)
            for i in range(6, 8):
                sp.wait_ge(s_piece_lo, NPROJ + i - RAWS + 1)
                sp.dma_start(raw_p[:, i % RAWS, :], w_attn1[i]).then_inc(ld_piece[i % RAWS], 16)
            sp.wait_ge(s_slice_lo, MI)
            for f in range(SS):
                sp.dma_start(raw_t[:, f, 0:2 * D], w_ffn1[f]).then_inc(ld_slice[f], 16)
            sp.dma_start(raw_t[:, 0, 2 * D:3 * D], w_lora[MR - 1, :, 0:D]).then_inc(ld_tail, 16)
            sp.dma_start(raw_t[:, 1, 2 * D:3 * D], w_lora[MR - 1, :, D:2 * D]).then_inc(ld_tail, 16)
            for i in range(8, NP1):
                sp.wait_ge(s_piece_lo, NPROJ + i - RAWS + 1)
                sp.dma_start(raw_p[:, i % RAWS, :], w_attn1[i]).then_inc(ld_piece[i % RAWS], 16)
            for f in range(SS, MM + MR - 1):
                sp.wait_ge(s_slice_lo, MI + f - SS + 1)
                src = w_ffn1[f] if f < MM else w_lora[f - MM]
                sp.dma_start(raw_t[:, f % SS, 0:2 * D], src).then_inc(ld_slice[f % SS], 16)
            for c in range(CHUNKS):
                s = slice(c * BANK, (c + 1) * BANK)
                sp.wait_ge(s_selT_ready, c + 1)
                sp.dma_start(comb_dram[1, :, s], selT[0:NE, s]).then_inc(st_comb, 16)
                sp.wait_ge(st_comb, 16 * (c + 2))
                for n in range(c * MR, (c + 1) * MR):
                    m = LORA[n][0]
                    spread(cb1[:, m, s], 1, m, RANK, ld_cb1[n], s)
            for t in range(TILES):
                sp.wait_ge(s_y_ready, t // 2 + 1)
                sp.dma_start(out[:, t, :], xres[:, t, :]).then_inc(stored, 16)
            sp.wait_ge(stored, 16 * TILES)

        @block.gpsimd
        def _(pool):
            G = nc.gpsimd
            done = [0]

            def link(ins):
                done[0] += 1
                ins.then_inc(s_pool_chain, 1)
                pool.wait_ge(s_pool_chain, done[0])

            def inv_root(dst, src, n, scale, eps, done_sem):
                link(G.tensor_scalar(dst, src, scale, eps, ALU.mult, ALU.add))
                G.tensor_tensor(dst, dst, half[:, 0:n], ALU.pow).then_inc(done_sem, 1)

            def piece_lo(i, raw_slot, slot):
                pool.wait_ge(s_piece_hi, i + 1)
                G.tensor_tensor(flat(w_lo[:, slot]), raw_p[:, raw_slot, :], flat(f32(w_hi[:, slot])),
                                ALU.subtract).then_inc(s_piece_lo, 1)

            def slice_lo(n, f, parts, last=True):
                pool.wait_ge(s_slice_hi, n + 1)
                hi, lo = parts_of(n, f)
                ins = G.tensor_tensor(flat(lo[:, 0:parts, :]), raw_t[:, f % SS, 0:parts * P],
                                      flat(f32(hi[:, 0:parts, :])), ALU.subtract)
                if last:
                    ins.then_inc(s_slice_lo, 1)

            link(G.memset(half[:], -0.5))
            pool.wait_ge(ld_x, 16)
            pool.wait_ge(ld_cols, 16)
            tapped = flat(hid[:, CT:TILES, :]).rearrange("p (r b l) -> p r b l", r=2, l=SEQ)

            def taps11(first, end):
                for delay in range(first, end):
                    n = SEQ - delay
                    src = batches(xT[:, 1, BANK:2 * BANK], CB)
                    dst = batches(yT[:, 1, BANK:2 * BANK], CB)
                    weight = c_("convw", 2 * SEQ - 1 - delay)
                    if delay == 0:
                        G.tensor_scalar(dst, src, weight, c_("convb", 1), ALU.mult, ALU.add).then_inc(s_tap11, 1)
                    else:
                        if delay > 1:
                            pool.wait_ge(s_tap11, delay - 1)
                        scaled = tapped[:, delay % 2, :, 0:n]
                        link(G.tensor_scalar(scaled, src[:, :, 0:n], weight, None, ALU.mult))
                        pool.wait_ge(s_tap11, delay)
                        G.tensor_tensor(dst[:, :, delay:SEQ], dst[:, :, delay:SEQ], scaled,
                                        ALU.add).then_inc(s_tap11, 1)

            taps11(0, TAPS1[0])
            for i in range(NPROJ):
                piece_lo(i, i % RAWS, i)

            def stats0(t):
                pool.wait_ge(s_squares, (4 * QK + 1) * t + 1)
                inv_root(stat[:, 8 + t:9 + t], stat[:, t:t + 1], 1, 1.0 / D, 1e-6, s_yrstd)
                r = stat[:, 8 + t:9 + t]
                pool.wait_ge(s_yrstd, t + 1)
                pool.wait_ge(s_squares, (4 * QK + 1) * (t + 1))
                for a, n in ((0, HKV), (HKV, HQ)):
                    if t >= 2:
                        pool.wait_ge(s_s0_taken, t - 1)
                        pool.wait_ge(s_roped, QK * (t - 1))
                    dst = nrt[:, t % 2, a:a + n]
                    link(G.tensor_scalar(dst, ssq[:, t % 2, a:a + n], r, r, ALU.mult, ALU.mult))
                    link(G.tensor_scalar(dst, dst, 1.0 / DH, 1e-6, ALU.mult, ALU.add))
                    link(G.tensor_tensor(dst, dst, half[:, 0:n], ALU.pow))
                    G.tensor_scalar(nrm[:, t % 2, a:a + n], dst, r, 1.0 if a == 0 else DH ** -0.5,
                                    ALU.mult, ALU.mult).then_inc(s_nrm_ready, 1)

            for t in range(TILES):
                stats0(t)
                if t == 0:
                    pool.wait_ge(s_ada_mm, 1)
                    G.memset(bd[:], 0.0).then_inc(s_bd_zero, 1)
                if t < 4:
                    taps11(TAPS1[t], TAPS1[t + 1])

            for t, n in ((0, TILES - 1), (TILES - 1, 1)):
                pool.wait_ge(s_squares, (4 * QK + 1) * TILES + t + n)
                inv_root(stat[:, 24 + t:24 + t + n], stat[:, 16 + t:16 + t + n], n, 1.0 / D, 1e-6, s_frstd)
            def moe_slice_lo(f):
                slice_lo(f, f, 4, last=False)
                G.tensor_tensor(down_lo[:, f % SS, :], raw_t[:, f % SS, 2 * D:3 * D], f32(down_hi[:, f % SS, :]),
                                ALU.subtract).then_inc(s_slice_lo, 1)

            for f in range(SS):
                moe_slice_lo(f)
            for f in range(SS, MI):
                moe_slice_lo(f)
                if f - SS < RAWS:
                    piece_lo(NPROJ + f - SS, (f - SS) % RAWS, f - SS)

            def mod_lo(n, t, src, done_sem):
                pool.wait_ge(s_mod_hi, n + 1)
                G.tensor_tensor(act_lo[:, :, t * P:(t + 1) * P], src.rearrange("p (m n) -> p m n", m=DK),
                                f32(act_hi[:, :, t * P:(t + 1) * P]), ALU.subtract).then_inc(done_sem, 1)

            for c in range(CHUNKS):
                for t in range(c * CT, (c + 1) * CT + 2):
                    if t < (c + 1) * CT:
                        pool.wait_ge(s_lnst, t + 1)
                        inv_root(stat[:, 32 + t:33 + t], bst[:, t, 7:8], 1, 1.0, 1e-6, s_lrstd)
                    if t >= c * CT + 2:
                        mod_lo(t - 2, t - 2, mt[:, t % 2, :], s_xn1_ready)
            for i in range(RAWS, NP1):
                piece_lo(NPROJ + i, i % RAWS, i % WSLOTS)
            def mod2(c):
                for t in range(c * CT, (c + 1) * CT):
                    pool.wait_ge(s_ln2st, t + 1)
                    inv_root(stat[:, 40 + t:41 + t], bst[:, t, 7:8], 1, 1.0, 1e-6, s_l2rstd)
                for t in range(c * CT, (c + 1) * CT):
                    mod_lo(TILES + t, t, mt2[:, t % 4, :], s_xn3_ready)

            for f in range(4):
                slice_lo(MI + f, f, 4)
            mod2(0)
            slice_lo(MI + 4, 4, 4)
            slice_lo(MI + 5, 5, 4)
            mod2(1)
            for f in range(6, MM):
                slice_lo(MI + f, f, 4)
            slice_lo(MI + MM, MM, 2)
            pool.wait_ge(s_slice_hi, MI + MM + 2)
            G.tensor_tensor(flat(strm_lo[:, MM % SS, 2:4, :]), raw_t[:, 0, 2 * D:3 * D],
                            flat(f32(strm_hi[:, MM % SS, 2:4, :])), ALU.subtract).then_inc(s_slice_lo, 1)
            for m in (1, 2):
                slice_lo(MI + MM + m + 1, MM + m, 2)

        @block.scalar
        def _(act):
            A = nc.scalar.activation
            squares = [0]

            def square(src, n, total):
                if squares[0] >= 3:
                    act.wait_ge(s_squares, squares[0] - 2)
                A(junk[:, squares[0] % 3, 0:n], src, ACT.Square, accum_out=total).then_inc(s_squares, 1)
                squares[0] += 1

            def piece_hi(i, raw_slot, slot):
                uses = i // RAWS + 1 if i < NPROJ else (NPROJ - 1 - raw_slot) // RAWS + 1 + (i - NPROJ) // RAWS + 1
                act.wait_ge(ld_piece[raw_slot], 16 * uses)
                A(flat(w_hi[:, slot]), raw_p[:, raw_slot, :], ACT.Copy).then_inc(s_piece_hi, 1)

            def slice_hi(n, f, parts, last=True):
                uses = f // SS + 1 if n < MI else (MI - 1 - f % SS) // SS + 1 + f // SS + 1
                act.wait_ge(ld_slice[f % SS], 16 * uses)
                ins = A(flat(parts_of(n, f)[0][:, 0:parts, :]), raw_t[:, f % SS, 0:parts * P], ACT.Copy)
                if last:
                    ins.then_inc(s_slice_hi, 1)

            def moe_slice_hi(f):
                slice_hi(f, f, 4, last=False)
                A(down_hi[:, f % SS, :], raw_t[:, f % SS, 2 * D:3 * D], ACT.Copy).then_inc(s_slice_hi, 1)

            act.wait_ge(ld_cols, 16)
            act.wait_ge(ld_consts, 16)
            for m in range(DK):
                for delay in range(PTAPS):
                    A(diag[:, m * PTAPS + delay, :], ident, ACT.Copy,
                      scale=c_("convw", m * SEQ + SEQ - 1 - delay)).then_inc(s_diag, 1)
            for i in range(NPROJ):
                piece_hi(i, i % RAWS, i)

            def take_y(t):
                act.wait_ge(s_ytok_T, t + 1)
                A(hid[:, t, :], ps[:, 7, 0:D], ACT.Copy).then_inc(s_ytok_copied, 1)
                square(ps[:, 7, 0:D], D, stat[:, t:t + 1])

            def take_proj(t, k):
                n = NPROJ * t + k
                act.wait_ge(s_proj0, n + 1)
                src = ps[:, k % 4, :]
                if k == NPROJ - 1:
                    act.wait_ge(s_yrstd, t + 1)
                    if t >= 2:
                        act.wait_ge(s_pv0, 4 * (t - 1))
                    A(v0[:, t % 2, :], src, ACT.Copy, scale=stat[:, 8 + t:9 + t]).then_inc(s_v0_ready, 1)
                    return
                if t >= 2:
                    act.wait_ge(s_nrm_ready, 2 * (t - 1))
                m = QK * t + k
                if m >= NR:
                    act.wait_ge(s_roped, m - NR + 1)
                A(raw[:, m % NR, :], src, ACT.Copy).then_inc(s_raw_ready, 1)
                at = HKV + 4 * k if k < QK - 1 else 0
                for h in range(4):
                    square(src[:, h * DH:(h + 1) * DH], DH, ssq[:, t % 2, at + h:at + h + 1])

            def take_qkT(t):
                if t >= 1:
                    act.wait_ge(s_s0, t)
                for k in range(QK):
                    f = QK * t + k
                    act.wait_ge(s_qkT_in_psum, f + 1)
                    A(qkT[:, k * BANK:(k + 1) * BANK], ps[:, QK_BANK[k], :], ACT.Copy).then_inc(s_qkT_copied, 1)

            def take_pv0(t, groups):
                if t >= 1:
                    act.wait_ge(s_o0, t)
                for j in groups:
                    n = 4 * t + j
                    act.wait_ge(s_pv0, n + 1)
                    A(attnT[:, j * BANK:(j + 1) * BANK], ps[:, 5 + n % 2, :], ACT.Copy).then_inc(s_pv0_copied, 1)

            act.wait_ge(s_y1, DK)
            take_y(0)
            for s in range(TILES + 1):
                if s < TILES:
                    take_proj(s, 0)
                if s >= 1:
                    act.wait_ge(s_s0_shifted, s)
                    A(sm_e[:], sm_s[:], ACT.Exp).then_inc(s_e0, 1)
                if s < TILES:
                    for k in range(1, QK):
                        take_proj(s, k)
                if s >= 1:
                    take_pv0(s - 1, (0, 1))
                if s < TILES:
                    take_proj(s, QK)
                if s >= 1:
                    take_pv0(s - 1, (2, 3))
                if s < TILES:
                    take_qkT(s)
                if s < TILES - 1:
                    take_y(s + 1)
                if s >= TILES - 1:
                    for t in range(TILES - 1) if s == TILES - 1 else (TILES - 1,):
                        act.wait_ge(s_hid_attn, t + 1)
                        square(hid[:, t, :], D, stat[:, 16 + t:17 + t])
            moe_slice_hi(0)
            act.wait_ge(s_gsh, 1)
            A(rt[:, 2], rt[:, 1], ACT.Exp).then_inc(s_gexp, 1)
            moe_slice_hi(1)
            moe_slice_hi(2)
            def hidden_hi(n):
                act.wait_ge(s_hm32, n + 1)
                if n >= 2:
                    act.wait_ge(s_hm_used, n - 1)
                A(hid_hi[:, n % 2, :], hm[:, n % 3, :], ACT.Copy).then_inc(s_hm_hi, 1)

            def gate(n):
                act.wait_ge(s_moe_g, n + 1)
                if n >= 2:
                    act.wait_ge(s_hu_ready, n - 1)
                A(sg[:, n % 2, :], ps[:, 4 + 2 * (n % 2), :], ACT.Silu).then_inc(s_sg_ready, 1)

            gate(0)
            gate(1)
            act.wait_ge(s_combT_psum, TILES)
            for c in range(CHUNKS):
                A(cmbT[0:NE, c * BANK:(c + 1) * BANK], ps[0:NE, 2 + c, :], ACT.Copy).then_inc(s_combT_ready, 1)
            for n in range(NM):
                if n >= 2:
                    gate(n)
                if n >= 1:
                    hidden_hi(n - 1)
                f = n // CHUNKS + 1
                if n % CHUNKS == 0 and SS <= f < MI:
                    act.wait_ge(s_hm_used, CHUNKS * (f - SS + 1))
                    moe_slice_hi(f)
                i = n // CHUNKS - 1
                if n % CHUNKS and 0 <= i < RAWS:
                    piece_hi(NPROJ + i, i % RAWS, i)
            hidden_hi(NM - 1)

            def take_x1(t):
                act.wait_ge(s_zT, t + 1)
                src = ps[:, 6 + t % 2, 0:D].rearrange("p (m n) -> p m n", m=DK)
                A(xT[:, :, t * P:(t + 1) * P], src, ACT.Copy).then_inc(s_xT1_copied, 1)

            def mod_hi(n, t, src):
                act.wait_ge(s_mod, n + 1)
                A(act_hi[:, :, t * P:(t + 1) * P], src.rearrange("p (m n) -> p m n", m=DK),
                  ACT.Copy).then_inc(s_mod_hi, 1)

            def take_proj1(u):
                j = u // CHUNKS
                for k in range(12):
                    if u == 0 and k in Z_BEHIND:
                        t = CT + Z_BEHIND.index(k)
                        take_x1(t)
                        if t > CT:
                            mod_hi(t - 1, t - 1, mt[:, (t - 1) % 2, :])
                    n = 12 * u + k
                    act.wait_ge(s_proj1, n + 1)
                    src = ps[:, n % 2, :]
                    if k < 8:
                        if k == 0 and u >= 1:
                            act.wait_ge(s_s1, u)
                        dst, b = (qT1, "bq") if k < 4 else (kT1, "bk")
                        h = k % 4
                        A(dst[:, h * BANK:(h + 1) * BANK], src, ACT.Identity,
                          bias=c_(b, 4 * j + h)).then_inc(s_q1_copied, 1)
                    else:
                        if k == 8 and u >= 2:
                            act.wait_ge(s_pv1, 4 * (u - 1))
                        A(v1[:, u % 2, k - 8, :], src, ACT.Copy).then_inc(s_q1_copied, 1)
                if u == 0:
                    mod_hi(TILES - 1, TILES - 1, mt[:, 1, :])

            def take_pv1(u, heads):
                for h in heads:
                    n = 4 * u + h
                    act.wait_ge(s_pv1, n + 1)
                    if n >= SS:
                        act.wait_ge(s_out1, n - SS + 1)
                    A(flat(strm_hi[:, n % SS]), ps[:, 4 + n % 2, :], ACT.Identity,
                      bias=c_("bv", 4 * (u // CHUNKS) + h)).then_inc(s_pv1_hi, 1)

            act.wait_ge(s_hm_used, NM)
            for i in range(RAWS, WSLOTS):
                piece_hi(NPROJ + i, i % RAWS, i)
            for t in range(CT + 1):
                if t < CT:
                    take_x1(t)
                if t >= 1:
                    mod_hi(t - 1, t - 1, mt[:, (t - 1) % 2, :])
            for u in range(U + 1):
                if u < U:
                    take_proj1(u)
                if u >= 1:
                    take_pv1(u - 1, (0, 1))
                if u < U:
                    act.wait_ge(s_s1_shifted, u + 1)
                    A(sm_e[:], sm_s[:], ACT.Exp, scale=DH ** -0.5).then_inc(s_e1, 1)
                if u >= 1:
                    take_pv1(u - 1, (2, 3))
                j = u // CHUNKS
                if u < U:
                    for i in ((4 * j + 6, 4 * j + 7, 4 * j + 8) if u % CHUNKS == CHUNKS - 1 else (4 * j + 5,)):
                        if WSLOTS <= i < NP1:
                            used_sem, count = piece_free(i)
                            act.wait_ge(used_sem, count)
                            piece_hi(NPROJ + i, i % RAWS, i % WSLOTS)
                if u == U - 1:
                    act.wait_ge(s_proj1, 12 * (U - 2))
                    act.wait_ge(s_out1, 4 * (U - 2))
                    for f in range(4):
                        slice_hi(MI + f, f, 4)
            for t in range(CT):
                act.wait_ge(s_x2T, t + 1)
                A(x2s[:, t, :], ps[:, 2 + t % 2, 0:D], ACT.Copy).then_inc(s_x2s_copied, 1)
            act.wait_ge(s_out1, 4 * U)
            slice_hi(MI + 4, 4, 4)
            slice_hi(MI + 5, 5, 4)
            for t in range(CT):
                mod_hi(TILES + t, t, mt2[:, t % 4, :])
            for t in range(CT, TILES):
                act.wait_ge(s_x2T, t + 1)
                A(x2s[:, t, :], ps[:, 2 + t % 2, 0:D], ACT.Copy).then_inc(s_x2s_copied, 1)
            for n, (m, c) in enumerate(FFN):
                if n in (2, 3):
                    for t in range(2 * n, 2 * n + 2):
                        mod_hi(TILES + t, t, mt2[:, t % 4, :])
                act.wait_ge(s_ffn_up, n + 1)
                if n >= 2:
                    act.wait_ge(s_glo, n - 1)
                A(g32[:, n % 2, :], ps[:, 4 + n % 4, :], ACT.Gelu, bias=c_("b1", m)).then_inc(s_gelu, 1)
                act.wait_ge(s_gelu, n + 1)
                if n >= 4:
                    act.wait_ge(s_ffn_down, n - 3)
                A(w_hi2[:, n % 4, :], g32[:, n % 2, :], ACT.Copy).then_inc(s_ghi, 1)
                if n in (4, 6):
                    slice_hi(MI + n // 2 + 4, n // 2 + 4, 4)
                if n == 8:
                    slice_hi(MI + MM, MM, 2)
                    act.wait_ge(ld_tail, 32)
                    A(flat(strm_hi[:, MM % SS, 2:4, :]), raw_t[:, 0, 2 * D:3 * D], ACT.Copy).then_inc(s_slice_hi, 1)
                if n in (10, 12):
                    slice_hi(MI + MM + n // 2 - 4, MM + n // 2 - 4, 2)

            def x4_hi(c):
                s = slice(c * BANK, (c + 1) * BANK)
                for m in range(DK):
                    act.wait_ge(s_x4_ready, DK * c + m + 1)
                    A(act_hi[:, m, s], xT[:, m, s], ACT.Copy).then_inc(s_x4_hi, 1)

            def router_exp(c):
                act.wait_ge(s_rsh, c + 1)
                A(rt[:, 2, c * CT:(c + 1) * CT], rt[:, 1, c * CT:(c + 1) * CT], ACT.Exp).then_inc(s_rexp, 1)

            def take_ups(first, end):
                for n in range(first, end):
                    act.wait_ge(s_lora_up, n + 1)
                    A(h1[:, n, :], ps[:, 4 + n % 4, :], ACT.Copy).then_inc(s_up_copied, 1)

            def take_selT(c):
                act.wait_ge(s_selT_psum, CT * (c + 1))
                A(selT[0:NE, c * BANK:(c + 1) * BANK], ps[0:NE, c, :], ACT.Copy).then_inc(s_selT_ready, 1)

            x4_hi(0)
            router_exp(0)
            x4_hi(1)
            take_ups(0, 3)
            take_selT(0)
            router_exp(1)
            take_ups(3, MR + 1)
            take_selT(1)
            take_ups(MR + 1, NL)

        @block.vector
        def _(dve):
            done = [0]
            V = nc.vector

            def link(ins):
                done[0] += 1
                ins.then_inc(s_dve_chain, 1)
                dve.wait_ge(s_dve_chain, done[0])

            dve.wait_ge(ld_x, 16)
            dve.wait_ge(ld_cols, 16)

            def tap(c, m, delay, first=0):
                src = batches(xT[:, m, c * BANK:(c + 1) * BANK], CB)
                dst = batches(yT[:, m, c * BANK:(c + 1) * BANK], CB)
                weight = c_("convw", m * SEQ + SEQ - 1 - delay)
                if delay == first:
                    return V.tensor_scalar(dst[:, :, delay:SEQ], src[:, :, 0:SEQ - delay], weight, c_("convb", m),
                                           ALU.mult, ALU.add)
                return V.scalar_tensor_tensor(dst[:, :, delay:SEQ], src[:, :, 0:SEQ - delay], weight,
                                              dst[:, :, delay:SEQ], ALU.mult, ALU.add)

            def split_y(c, m):
                s = slice(c * BANK, (c + 1) * BANK)
                link(V.tensor_scalar(act_hi[:, m, s], yT[:, m, s], c_("anw", m), None, ALU.mult))
                V.scalar_tensor_tensor(act_lo[:, m, s], yT[:, m, s], c_("anw", m), f32(act_hi[:, m, s]),
                                       ALU.mult, ALU.subtract).then_inc(s_yw_ready, 1)

            for delay in range(PTAPS, SEQ):
                for m in range(DK):
                    if delay > PTAPS:
                        dve.wait_ge(s_conv_step, DK * (delay - PTAPS - 1) + m + 1)
                    tap(0, m, delay, first=PTAPS).then_inc(s_conv_step, 1)
            dve.wait_ge(s_conv_step, DK * (SEQ - PTAPS))
            for m in range(DK):
                dve.wait_ge(s_conv_mm, m + 1)
                src, dst = batches(ps[:, 2 + m, :], CB), batches(yT[:, m, 0:BANK], CB)
                V.tensor_scalar(dst[:, :, 0:PTAPS], src[:, :, 0:PTAPS], c_("convb", m), None, ALU.add)
                V.tensor_tensor(dst[:, :, PTAPS:SEQ], src[:, :, PTAPS:SEQ], dst[:, :, PTAPS:SEQ],
                                ALU.add).then_inc(s_y1, 1)
                dve.wait_ge(s_y1, m + 1)
                split_y(0, m)
            dve.wait_ge(ld_consts, 16)
            dve.wait_ge(ld_small, 48)
            for i in range(4):
                V.tensor_tensor(tables[:, i, :], k_("cos" if i % 2 == 0 else "sin"), ropew[:, i, :],
                                ALU.mult).then_inc(s_tables_ready, 1)
            dve.wait_ge(s_tables_ready, 4)
            for delay in range(TAPS0):
                link(tap(1, 0, delay))

            def rope(t):
                for k in range(QK):
                    m = QK * t + k
                    dve.wait_ge(s_raw_ready, m + 1)
                    src = raw[:, m % NR, :]
                    i = 0
                    if k == 0 and t >= 1:
                        dve.wait_ge(s_qkT_in_psum, QK * t)
                    if k == QK - 1:
                        dve.wait_ge(s_nrm_ready, 2 * t + 1)
                        link(V.tensor_tensor(kn.rearrange("p (h d) -> p h d", h=4), src.rearrange("p (h d) -> p h d", h=4),
                                             over(nrm[:, t % 2, 0:HKV], DH), ALU.mult))
                        src = kn
                        i = 2
                    s4 = src.rearrange("p (h d) -> p h d", h=4)
                    q4 = qr[:, k * BANK:(k + 1) * BANK].rearrange("p (h d) -> p h d", h=4)
                    r4 = r2.rearrange("p (h d) -> p h d", h=4)
                    V.tensor_tensor(q4, s4, rep(tables[:, i, :], 4), ALU.mult)
                    V.tensor_tensor(r4[:, :, 0:HD], s4[:, :, HD:DH], rep(tables[:, i + 1, 0:HD], 4), ALU.mult)
                    link(V.tensor_tensor(r4[:, :, HD:DH], s4[:, :, 0:HD], rep(tables[:, i + 1, HD:DH], 4), ALU.mult))
                    V.tensor_tensor(q4, q4, r4, ALU.add).then_inc(s_roped, 1)
                    dve.wait_ge(s_roped, m + 1)

            def softmax_tail(e_sem, e_count, slot, bd_sem, pv_sem, pv_count):
                dve.wait_ge(e_sem, e_count)
                link(V.tensor_reduce(sm_d[:], sm_e[:], AX_X, ALU.add))
                link(V.reciprocal(sm_r[:], sm_d[:]))
                link(V.tensor_tensor(sm_e[:], sm_e[:], over(sm_r[:], SEQ), ALU.mult))
                if pv_count:
                    dve.wait_ge(pv_sem, pv_count)
                for b in range(BT):
                    rows = slice(SEQ * b, SEQ * (b + 1))
                    V.transpose(bd[rows, slot, :, b, :], sm_e[rows]).then_inc(bd_sem, 1)

            def softmax0_head(t):
                dve.wait_ge(s_nrm_ready, 2 * t + 2)
                dve.wait_ge(s_s0, t + 1)
                V.tensor_tensor(sm_s[:], ps[:, 4, :].rearrange("p (h k) -> p h k", h=HQ),
                                over(nrm[:, t % 2, HKV:HKV + HQ], SEQ), ALU.mult).then_inc(s_s0_taken, 1)
                dve.wait_ge(s_s0_taken, t + 1)
                link(V.tensor_tensor(sm_s[:], sm_s[:], rep(k_("causal"), HQ), ALU.add))
                link(V.tensor_reduce(sm_m[:], sm_s[:], AX_X, ALU.max))
                V.tensor_tensor(sm_s[:], sm_s[:], over(sm_m[:], SEQ), ALU.subtract).then_inc(s_s0_shifted, 1)

            def norm_h(t):
                dve.wait_ge(s_frstd, 1 if t < TILES - 1 else 2)
                if t >= 3:
                    dve.wait_ge(s_hnT, t - 2)
                V.tensor_scalar(hn[:, t % 3, :], hid[:, t, :], stat[:, 24 + t:25 + t], None,
                                ALU.mult).then_inc(s_hn_ready, 1)

            def to_h2(t):
                dve.wait_ge(s_hnT, t + 1)
                s = slice(t * P, (t + 1) * P)
                for m in range(DK):
                    V.tensor_scalar(h2[:, m, s], ps[:, t % 3, m * P:(m + 1) * P], c_("fnw", m), None,
                                    ALU.mult).then_inc(s_h2_f32, 1)
                dve.wait_ge(s_h2_f32, DK * (t + 1))
                link(V.tensor_copy(act_hi[:, :, s], h2[:, :, s]))
                V.tensor_tensor(act_lo[:, :, s], h2[:, :, s], f32(act_hi[:, :, s]), ALU.subtract).then_inc(s_h2_ready, 1)

            for s in range(TILES + 1):
                if s >= 1:
                    if s == 1:
                        dve.wait_ge(s_bd_zero, 1)
                    softmax0_head(s - 1)
                    if s == TILES:
                        for t in range(3):
                            norm_h(t)
                    softmax_tail(s_e0, s, (s - 1) % 2, s_bd0, s_pv0, 4 * (s - 2) if s >= 3 else 0)
                if s < TILES:
                    rope(s)
                if s == 0:
                    dve.wait_ge(s_ada_mm, 1)
                    V.tensor_tensor(ada[:], ps[:, 4, 0:NADA * BATCH].rearrange("p (n b) -> p n b", n=NADA),
                                    over(c_("adab", 0, NADA), BATCH), ALU.add).then_inc(s_ada_ready, 1)
                    dve.wait_ge(s_ada_ready, 1)
                    for i in (DK, 4 * DK):
                        link(V.tensor_scalar(ada[:, i:i + DK, :], ada[:, i:i + DK, :], 1.0, None, ALU.add))
                if s == TILES:
                    for t in range(TILES - 2):
                        to_h2(t)
                        if t + 3 < TILES - 1:
                            norm_h(t + 3)
                if s >= 1:
                    dve.wait_ge(s_o0, s)
                    dve.wait_ge(s_squares, (4 * QK + 1) * (s - 1) + 1)
                    V.tensor_tensor(hid[:, s - 1, :], ps[:, 7, 0:D], hid[:, s - 1, :], ALU.add).then_inc(s_hid_attn, 1)
                if s < 3:
                    left = SEQ - TAPS0
                    for delay in range(TAPS0 + s * left // 3, TAPS0 + (s + 1) * left // 3):
                        link(tap(1, 0, delay))
                if s == 2:
                    split_y(1, 0)
                if s == 3:
                    dve.wait_ge(s_tap11, SEQ)
                    split_y(1, 1)

            to_h2(TILES - 2)
            norm_h(TILES - 1)
            to_h2(TILES - 1)

            def shifted(logits, bias, g=slice(0, TILES)):
                src = logits
                if bias is not None:
                    link(V.tensor_tensor(rt[:, 0, g], logits, rep(bias, g.stop - g.start), ALU.add))
                    src = rt[:, 0, g]
                link(V.tensor_reduce(bst[:, g, 0], src, AX_X, ALU.max))
                return V.tensor_tensor(rt[:, 1, g], src, over(bst[:, g, 0], NE), ALU.subtract)

            def probs(g=slice(0, TILES)):
                link(V.tensor_reduce(bst[:, g, 1], rt[:, 2, g], AX_X, ALU.add))
                link(V.reciprocal(bst[:, g, 2], bst[:, g, 1]))
                link(V.tensor_tensor(rt[:, 3, g], rt[:, 2, g], over(bst[:, g, 2], NE), ALU.mult))
                for t in range(g.start, g.stop):
                    ins = V.max(rt[:, 4, t, :], rt[:, 3, t, :])
                link(ins)
                for t in range(g.start, g.stop):
                    ins = V.max_index(ridx[:, t, :], rt[:, 4, t, :], rt[:, 3, t, :])
                link(ins)
                link(V.tensor_copy(rt[:, 5, g], ridx[:, g]))

            def one_hot(dst, k, g=slice(0, TILES)):
                return V.tensor_tensor(dst, rep(k_("iota"), g.stop - g.start), over(rt[:, 5, g, k], NE), ALU.is_equal)

            dve.wait_ge(s_glog, TILES)
            shifted(ps[:, 3, 0:TILES * NE].rearrange("p (t e) -> p t e", t=TILES), None).then_inc(s_gsh, 1)
            dve.wait_ge(s_gexp, 1)
            probs()
            link(V.tensor_tensor(bst[:, :, 3], rt[:, 4, :, 0], rt[:, 4, :, 1], ALU.add))
            link(V.tensor_scalar(bst[:, :, 3], bst[:, :, 3], 1e-9, None, ALU.add))
            link(V.reciprocal(bst[:, :, 4], bst[:, :, 3]))
            link(V.tensor_tensor(rt[:, 6], rt[:, 4], over(bst[:, :, 4], NE), ALU.mult))
            link(one_hot(rt[:, 7], 0))
            link(one_hot(rt[:, 8], 1))
            link(V.tensor_tensor(rt[:, 7], rt[:, 7], over(rt[:, 6, :, 0], NE), ALU.mult))
            link(V.tensor_tensor(rt[:, 8], rt[:, 8], over(rt[:, 6, :, 1], NE), ALU.mult))
            V.tensor_tensor(rt[:, 9], rt[:, 7], rt[:, 8], ALU.add).then_inc(s_comb, 1)

            def weigh(n):
                m, c = MOE[n]
                dve.wait_ge(s_hu_ready, n + 1)
                dve.wait_ge(ld_cb[m % SS], 32 * (m // SS + 1))
                if n >= 3:
                    dve.wait_ge(s_hm_ready, n - 2)
                V.tensor_tensor(hm[:, n % 3, :], hu[:, n % 2, :], cb[:, m % SS, c * BANK:(c + 1) * BANK],
                                ALU.mult).then_inc(s_hm32, 1)
                dve.wait_ge(s_hm_hi, n + 1)
                V.tensor_tensor(hid_lo[:, n % 2, :], hm[:, n % 3, :], f32(hid_hi[:, n % 2, :]),
                                ALU.subtract).then_inc(s_hm_ready, 1)

            for n in range(NM):
                dve.wait_ge(s_sg_ready, n + 1)
                dve.wait_ge(s_moe_u, n + 1)
                if n >= 2:
                    dve.wait_ge(s_hm32, n - 1)
                V.tensor_tensor(hu[:, n % 2, :], sg[:, n % 2, :], ps[:, 5 + 2 * (n % 2), :], ALU.mult).then_inc(s_hu_ready, 1)
                if n == 1:
                    weigh(0)
                if n >= 1:
                    weigh(n)
            dve.wait_ge(ld_xtok, 16)

            def residual1(a):
                c = 2 * a // CT
                dve.wait_ge(s_hm_used, NM - CHUNKS * (CHUNKS - 1 - c))
                t2 = slice(2 * a, 2 * a + 2)
                link(V.tensor_tensor(hid[:, t2, :], ps[:, a, :].rearrange("p (b n) -> p b n", b=2), hid[:, t2, :], ALU.add))
                V.tensor_tensor(xres[:, t2, :], xres[:, t2, :], hid[:, t2, :], ALU.add).then_inc(s_x1_ready, 1)

            def ln_stats(src, t, done_sem):
                link(V.bn_stats(bst[:, t, 0:6], src))
                V.bn_aggr(bst[:, t, 6:8], bst[:, t, 0:6]).then_inc(done_sem, 1)

            def ln_apply(dst, src, t, r, done_sem):
                V.tensor_scalar(dst, src, bst[:, t, 6:7], stat[:, r + t:r + t + 1], ALU.subtract,
                                ALU.mult).then_inc(done_sem, 1)

            def modulate(src, n, t, dst, ring, scale, shift, done_sem):
                four = "p (m b l) -> p m b l"
                b4 = slice(BT * t, BT * (t + 1))
                m4 = dst.rearrange(four, m=DK, b=BT)
                if t >= ring:
                    dve.wait_ge(done_sem, t - ring + 1)
                link(V.tensor_tensor(m4, src.rearrange(four, m=DK, b=BT),
                                     over(ada[:, scale * DK:(scale + 1) * DK, b4], SEQ), ALU.mult))
                V.tensor_tensor(m4, m4, over(ada[:, shift * DK:(shift + 1) * DK, b4], SEQ), ALU.add).then_inc(s_mod, 1)

            def ln1(tiles):
                a = tiles[0]
                for t in range(a, a + CT + 2):
                    if t < a + CT:
                        if t % 2 == 0:
                            residual1(t // 2)
                        dve.wait_ge(s_x1_ready, t // 2 + 1)
                        ln_stats(xres[:, t, :], t, s_lnst)
                    if a + 1 <= t <= a + CT:
                        dve.wait_ge(s_lrstd, t)
                        if t >= 3:
                            dve.wait_ge(s_zT, t - 2)
                        ln_apply(z[:, (t - 1) % 2, :], xres[:, t - 1, :], t - 1, 32, s_z_ready)
                    if t >= a + 2:
                        dve.wait_ge(s_zT, t - 1)
                        modulate(ps[:, 4 + t % 2, 0:D], t - 2, t - 2, mt[:, t % 2, :], 2, 1, 0, s_xn1_ready)

            ln1(range(0, CT))
            ln1(range(CT, TILES))

            def softmax1_head(u):
                dve.wait_ge(s_s1, u + 1)
                s4 = ps[:, 2, :].rearrange("p (h k) -> p h k", h=16)
                link(V.tensor_reduce(sm_m[:], s4, AX_X, ALU.max))
                V.tensor_tensor(sm_s[:], s4, over(sm_m[:], SEQ), ALU.subtract).then_inc(s_s1_shifted, 1)

            def low_heads(u, heads):
                for h in heads:
                    n = 4 * u + h
                    dve.wait_ge(s_pv1_hi, n + 1)
                    V.scalar_tensor_tensor(flat(strm_lo[:, n % SS]), ps[:, 4 + n % 2, :], c_("bv", 4 * (u // CHUNKS) + h),
                                           flat(f32(strm_hi[:, n % SS])), ALU.add, ALU.subtract).then_inc(s_pv1_lo, 1)

            def add_out(u):
                j, c = divmod(u, CHUNKS)
                dve.wait_ge(s_out1, 4 * (u + 1))
                for m in range(DK):
                    dst, src = yT[:, m, c * BANK:(c + 1) * BANK], ps[:, 6 + m, :]
                    if j == 0:
                        ins = V.tensor_copy(dst, src)
                    else:
                        ins = V.tensor_tensor(dst, src, dst, ALU.add)
                    ins.then_inc(s_acc1, 1)

            def gated(acc, gate, bias, c, m):
                s = slice(c * BANK, (c + 1) * BANK)
                link(V.scalar_tensor_tensor(batches(yT[:, m, s], CB), batches(acc, CB), c_(bias, m),
                                            over(ada[:, gate * DK + m, CB * c:CB * (c + 1)], SEQ), ALU.add, ALU.mult))
                return V.tensor_tensor(xT[:, m, s], xT[:, m, s], yT[:, m, s], ALU.add)

            def residual2(c, ms):
                dve.wait_ge(s_acc1, DK * (U - CHUNKS + c + 1))
                dve.wait_ge(s_xT1_copied, TILES)
                for m in ms:
                    gated(yT[:, m, c * BANK:(c + 1) * BANK], 2, "outb", c, m).then_inc(s_x2_ready, 1)

            def hidden_lo(n):
                dve.wait_ge(s_ghi, n + 1)
                V.tensor_tensor(w_lo2[:, n % 4, :], g32[:, n % 2, :], f32(w_hi2[:, n % 4, :]),
                                ALU.subtract).then_inc(s_glo, 1)

            def norm2(c):
                for t in range(c * CT, (c + 1) * CT + 2):
                    if t < (c + 1) * CT:
                        dve.wait_ge(s_x2s_copied, t + 1)
                        ln_stats(x2s[:, t, :], t, s_ln2st)
                    if c * CT + 1 <= t <= (c + 1) * CT:
                        dve.wait_ge(s_l2rstd, t)
                        ln_apply(z2[:, t - 1, :], x2s[:, t - 1, :], t - 1, 40, s_z2_ready)
                    if t == TILES + 1:
                        hidden_lo(0)
                        hidden_lo(1)
                    if t >= c * CT + 2:
                        modulate2(t - 2)

            def modulate2(t):
                dve.wait_ge(s_z2T, t + 1)
                bank = t % 4 if t < CT else 2 + t % 2
                modulate(ps[:, bank, 0:D], TILES + t, t, mt2[:, t % 4, :], 4, 4, 3, s_xn3_ready)

            for u in range(U + 1):
                if u >= 1:
                    low_heads(u - 1, (0, 1))
                if u == U:
                    residual2(0, (0,))
                if u < U:
                    softmax1_head(u)
                if u >= 1:
                    low_heads(u - 1, (2,))
                if u == U:
                    residual2(0, (1,))
                if u >= 1:
                    low_heads(u - 1, (3,))
                if u < U:
                    softmax_tail(s_e1, u + 1, u % 2, s_bd1, s_pv1, 4 * (u - 1) if u >= 2 else 0)
                if u == U:
                    norm2(0)
                if u >= 1:
                    add_out(u - 1)
            residual2(1, range(DK))
            norm2(1)

            for n in range(2, NF):
                hidden_lo(n)
            def router1(c):
                g = slice(c * CT, (c + 1) * CT)
                dve.wait_ge(s_rlog, CT * (c + 1))
                shifted(ps[:, c, 0:CT * NE].rearrange("p (t e) -> p t e", t=CT), c_("br", 0, NE), g).then_inc(s_rsh, 1)
                dve.wait_ge(s_rexp, c + 1)
                probs(g)
                link(one_hot(rt[:, 7, g], 0, g))
                V.scalar_tensor_tensor(rt[:, 9, g], rt[:, 7, g], 1.0 / RANK, over(rt[:, 4, g, 0], NE), ALU.mult,
                                       ALU.mult).then_inc(s_wsel, 1)

            dve.wait_ge(s_x2_ready, DK * CHUNKS)
            for c in range(CHUNKS):
                s = slice(c * BANK, (c + 1) * BANK)
                dve.wait_ge(s_ffn_down, NF - SS * (CHUNKS - 1 - c))
                for m in range(DK):
                    gated(ps[:, 2 * c + m, :], 5, "b2", c, m).then_inc(s_x4_ready, 1)
                if c == CHUNKS - 1:
                    router1(0)
                for m in range(DK):
                    dve.wait_ge(s_x4_hi, DK * c + m + 1)
                    V.tensor_tensor(act_lo[:, m, s], xT[:, m, s], f32(act_hi[:, m, s]),
                                    ALU.subtract).then_inc(s_x4_split, 1)
            router1(1)
            def add_lora(c):
                dve.wait_ge(s_hmk_used, MR * (c + 1))
                for a in range(c * CT // 2, (c + 1) * CT // 2):
                    t2 = slice(2 * a, 2 * a + 2)
                    V.tensor_tensor(xres[:, t2, :], ps[:, (a + 2) % 4, :].rearrange("p (b n) -> p b n", b=2),
                                    xres[:, t2, :], ALU.add).then_inc(s_y_ready, 1)

            for n, (m, c) in enumerate(LORA):
                dve.wait_ge(s_up_copied, n + 1)
                dve.wait_ge(ld_cb1[n], 32)
                if n >= 3:
                    dve.wait_ge(s_hmk_used, n - 2)
                V.tensor_tensor(hmk[:, n % 3, :], h1[:, n, :], cb1[:, m, c * BANK:(c + 1) * BANK],
                                ALU.mult).then_inc(s_hmk_ready, 1)
                if n == MR + 2:
                    add_lora(0)
            add_lora(1)

        @block.tensor
        def _(pe):
            mm = nc.tensor.matmul

            def tokens(t):
                return slice(t * P, (t + 1) * P)

            def split_mm(dst, terms, start=True, stop=True, **flags):
                for i, (ah, al, bh, bl) in enumerate(terms):
                    mm(dst, ah, bh, start=start and i == 0, stop=False, **flags)
                    mm(dst, ah, bl, start=False, stop=False, **flags)
                    last = mm(dst, al, bh, start=False, stop=stop and i == len(terms) - 1, **flags)
                return last

            pe.wait_ge(ld_x, 16)
            for m in range(DK):
                src, dst = batches(xT[:, m, 0:BANK], CB), batches(ps[:, 2 + m, :], CB)
                for delay in range(PTAPS):
                    pe.wait_ge(s_diag, m * PTAPS + delay + 1)
                    last = mm(dst[:, :, delay:SEQ], diag[:, m * PTAPS + delay, :], src[:, :, 0:SEQ - delay],
                              start=(delay == 0), stop=(delay == PTAPS - 1))
                last.then_inc(s_conv_mm, 1)
            def turn_y(t):
                pe.wait_ge(s_yw_ready, DK * (t // CT + 1))
                if t >= 2:
                    pe.wait_ge(s_hid_attn, t - 1)
                for m in range(DK):
                    last = nc.tensor.transpose(ps[:, 7, m * P:(m + 1) * P], yT[:, m, tokens(t)], ident)
                last.then_inc(s_ytok_T, 1)

            def proj(t):
                for k in range(NPROJ):
                    if t == 0:
                        pe.wait_ge(s_piece_lo, k + 1)
                        if k == 2:
                            pe.wait_ge(s_y1, DK)
                    if k >= 4:
                        pe.wait_ge(s_squares, (4 * QK + 1) * t + 1 + 4 * (k - 3))
                    split_mm(ps[:, k % 4, :],
                             [(act_hi[:, m, tokens(t)], act_lo[:, m, tokens(t)], w_hi[:, k, m, :], w_lo[:, k, m, :])
                              for m in range(DK)]).then_inc(s_proj0, 1)

            def turn_qk(t):
                for k in range(QK):
                    f = QK * t + k
                    pe.wait_ge(s_roped, f + 1)
                    if k < 3:
                        pe.wait_ge(s_squares, (4 * QK + 1) * t + 1 + 4 * (k + 3))
                    elif k == 3:
                        pe.wait_ge(s_v0_ready, t + 1)
                    else:
                        pe.wait_ge(s_qkT_copied, QK * t + 1)
                    for h in range(4):
                        last = nc.tensor.transpose(ps[:, QK_BANK[k], h * DH:(h + 1) * DH],
                                                   qr[:, k * BANK + h * DH:k * BANK + (h + 1) * DH], ident)
                    last.then_inc(s_qkT_in_psum, 1)

            def scores0(t):
                pe.wait_ge(s_qkT_copied, QK * (t + 1))
                if t == 0:
                    pe.wait_ge(s_ada_ready, 1)
                if t >= 1:
                    pe.wait_ge(s_s0_taken, t)
                for h in range(HQ):
                    for b in range(BT):
                        q = h * P + b * SEQ
                        k = HQ * P + (h // REP) * P + b * SEQ
                        last = mm(ps[b * SEQ:(b + 1) * SEQ, 4, h * SEQ:(h + 1) * SEQ], qkT[:, q:q + SEQ],
                                  qkT[:, k:k + SEQ], start=True, stop=True)
                last.then_inc(s_s0, 1)

            def pv0(t):
                pe.wait_ge(s_v0_ready, t + 1)
                pe.wait_ge(s_bd0, BT * (t + 1))
                for j in range(HKV):
                    n = 4 * t + j
                    if n >= 2:
                        pe.wait_ge(s_pv0_copied, n - 1)
                    mm(ps[:, 5 + n % 2, :], v0[:, t % 2, j * DH:(j + 1) * DH],
                       bd[:, t % 2, REP * j:REP * (j + 1)].rearrange("p h b q -> p (h b q)"),
                       start=True, stop=True).then_inc(s_pv0, 1)

            def oproj(t):
                if t + 1 < TILES:
                    pe.wait_ge(s_ytok_copied, t + 2)
                    pe.wait_ge(s_squares, (4 * QK + 1) * (t + 1) + 1)
                else:
                    pe.wait_ge(s_hid_attn, t)
                for h in range(HQ):
                    if t == TILES - 1 and h == HQ // 2:
                        for i in range(3, 6):
                            turn_h(i)
                        for i in range(3):
                            logits0(i)
                    if h % REP == 0:
                        pe.wait_ge(s_pv0_copied, 4 * t + h // REP + 1)
                    last = mm(ps[:, 7, 0:D], attnT[:, h * P:(h + 1) * P], wo0[:, h, :], start=(h == 0), stop=(h == HQ - 1))
                last.then_inc(s_o0, 1)

            def turn_h(t):
                pe.wait_ge(s_hn_ready, t + 1)
                if t >= 3:
                    pe.wait_ge(s_h2_f32, DK * (t - 2))
                for m in range(DK):
                    last = nc.tensor.transpose(ps[:, t % 3, m * P:(m + 1) * P], hn[:, t % 3, m * P:(m + 1) * P], ident)
                last.then_inc(s_hnT, 1)

            def logits0(t):
                pe.wait_ge(s_h2_f32, DK * (t + 1))
                for m in range(DK):
                    last = mm(ps[:, 3, t * NE:(t + 1) * NE], h2[:, m, tokens(t)], gate_w[:, m, :],
                              start=(m == 0), stop=(m == DK - 1))
                last.then_inc(s_glog, 1)

            turn_y(0)
            for s in range(TILES + 1):
                if s < TILES:
                    proj(s)
                if s == 0:
                    pe.wait_ge(ld_ada, 32)
                    for n in range(NADA):
                        for m in range(DK):
                            last = mm(ps[:, 4, n * BATCH:(n + 1) * BATCH], wada[:, m, n * P:(n + 1) * P], cond[:, m, :],
                                      start=(m == 0), stop=(m == DK - 1))
                    last.then_inc(s_ada_mm, 1)
                if s == TILES:
                    pe.wait_ge(ld_small, 48)
                    for t in range(3):
                        turn_h(t)
                if s >= 1:
                    if s == 1:
                        pe.wait_ge(ld_o0, 16)
                    pv0(s - 1)
                    oproj(s - 1)
                if s < TILES:
                    turn_qk(s)
                    if s < TILES - 1:
                        turn_y(s + 1)
                    scores0(s)

            for t in range(3, 6):
                logits0(t)
            for t in range(6, TILES):
                turn_h(t)
                logits0(t)

            def halves(slice_parts, part, s):
                hi, lo = slice_parts
                return [(hi[:, part + k, :], lo[:, part + k, :], act_hi[:, k, s], act_lo[:, k, s]) for k in range(DK)]

            def moe_up(n):
                m, c = MOE[n]
                s = slice(c * BANK, (c + 1) * BANK)
                if c == 0:
                    pe.wait_ge(s_slice_lo, m + 1)
                if n < CHUNKS:
                    pe.wait_ge(s_h2_ready, CT * (c + 1))
                if n >= 2:
                    pe.wait_ge(s_sg_ready, n - 1)
                split_mm(ps[:, 4 + 2 * (n % 2), :], halves(parts_of(m, m), 0, s)).then_inc(s_moe_g, 1)
                if n >= 2:
                    pe.wait_ge(s_hu_ready, n - 1)
                split_mm(ps[:, 5 + 2 * (n % 2), :], halves(parts_of(m, m), DK, s)).then_inc(s_moe_u, 1)

            def moe_down(n):
                m, c = MOE[n]
                pe.wait_ge(s_hm_ready, n + 1)
                for t in range(CT):
                    last = split_mm(ps[:, 2 * c + t // 2, (t % 2) * D:(t % 2 + 1) * D],
                                    [(hid_hi[:, n % 2, t * P:(t + 1) * P], hid_lo[:, n % 2, t * P:(t + 1) * P],
                                      down_hi[:, m % SS, :], down_lo[:, m % SS, :])],
                                    start=(m == 0 and t % 2 == 0), stop=(m == MI - 1), skip_group_check=True)
                last.then_inc(s_hm_used, 1)

            pe.wait_ge(s_hid_attn, TILES)
            for n in range(NM + 2):
                if n < NM:
                    moe_up(n)
                if n == 1:
                    pe.wait_ge(s_comb, 1)
                    for t in range(TILES):
                        nc.tensor.transpose(ps[0:NE, 2 + t // CT, (t % CT) * P:(t % CT + 1) * P], rt[:, 9, t, :],
                                            ident).then_inc(s_combT_psum, 1)
                if n == 3:
                    pe.wait_ge(s_combT_ready, CHUNKS)
                    moe_down(0)
                if n >= 3:
                    moe_down(n - 2)

            def turn_z(t):
                pe.wait_ge(s_z_ready, t + 1)
                if t >= 2:
                    pe.wait_ge(s_mod, t - 1)
                    pe.wait_ge(s_xT1_copied, t - 1)
                for m in range(DK):
                    nc.tensor.transpose(ps[:, 4 + t % 2, m * P:(m + 1) * P], z[:, t % 2, m * P:(m + 1) * P], ident)
                for m in range(DK):
                    last = nc.tensor.transpose(ps[:, 6 + t % 2, m * P:(m + 1) * P], xres[:, t, m * P:(m + 1) * P], ident)
                last.then_inc(s_zT, 1)

            def proj1(u):
                j, c = divmod(u, CHUNKS)
                s = slice(c * BANK, (c + 1) * BANK)
                pe.wait_ge(s_xn1_ready, CT * (c + 1))
                for k in range(12):
                    if u == 0 and k in Z_BEHIND:
                        turn_z(CT + Z_BEHIND.index(k))
                    n = 12 * u + k
                    i = 4 * j + k // 4
                    w = i % WSLOTS
                    if k % 4 == 0:
                        pe.wait_ge(s_piece_lo, NPROJ + i + 1)
                    if n >= 2:
                        pe.wait_ge(s_q1_copied, n - 1)
                    if k < 8:
                        h = slice((k % 4) * DH, (k % 4 + 1) * DH)
                        terms = [(w_hi[:, w, m, h], w_lo[:, w, m, h], act_hi[:, m, s], act_lo[:, m, s]) for m in range(DK)]
                    else:
                        t = tokens(c * CT + k - 8)
                        terms = [(act_hi[:, m, t], act_lo[:, m, t], w_hi[:, w, m, :], w_lo[:, w, m, :]) for m in range(DK)]
                    split_mm(ps[:, n % 2, :], terms).then_inc(s_proj1, 1)

            def scores1(u):
                pe.wait_ge(s_q1_copied, 12 * u + 8)
                if u >= 1:
                    pe.wait_ge(s_s1_shifted, u)
                for h in range(4):
                    for t in range(CT):
                        for b in range(BT):
                            q = h * BANK + t * P + b * SEQ
                            k = 4 * h + t
                            last = mm(ps[b * SEQ:(b + 1) * SEQ, 2, k * SEQ:(k + 1) * SEQ], qT1[:, q:q + SEQ],
                                      kT1[:, q:q + SEQ], start=True, stop=True)
                last.then_inc(s_s1, 1)

            def pv1(u, h):
                n = 4 * u + h
                if h == 0:
                    pe.wait_ge(s_q1_copied, 12 * (u + 1))
                    pe.wait_ge(s_bd1, BT * (u + 1))
                if n >= 2:
                    pe.wait_ge(s_pv1_lo, n - 1)
                for t in range(CT):
                    last = mm(ps[:, 4 + n % 2, t * P:(t + 1) * P], v1[:, u % 2, t, h * DH:(h + 1) * DH],
                              bd[:, u % 2, 4 * h + t].rearrange("p b q -> p (b q)"), start=True, stop=True)
                last.then_inc(s_pv1, 1)

            def out1(u, h):
                n = 4 * u + h
                i = 4 * (u // CHUNKS) + 3
                w = i % WSLOTS
                pe.wait_ge(s_pv1_lo, n + 1)
                if h == 0:
                    pe.wait_ge(s_piece_lo, NPROJ + i + 1)
                    if u >= 1:
                        pe.wait_ge(s_acc1, DK * u)
                for m in range(DK):
                    at = (h % 2) * D + m * P
                    last = split_mm(ps[:, 6 + m, :], [(w_hi[:, w, h // 2, at:at + P], w_lo[:, w, h // 2, at:at + P],
                                                       flat(strm_hi[:, n % SS]), flat(strm_lo[:, n % SS]))],
                                    start=(h == 0), stop=(h == 3))
                last.then_inc(s_out1, 1)

            def turn_x2(c):
                pe.wait_ge(s_x2_ready, DK * (c + 1))
                for t in range(c * CT, (c + 1) * CT):
                    if t >= 2:
                        pe.wait_ge(s_x2s_copied, t - 1)
                    if t in (4, 5):
                        pe.wait_ge(s_mod, TILES + t - 1)
                    for m in range(DK):
                        last = nc.tensor.transpose(ps[:, 2 + t % 2, m * P:(m + 1) * P], xT[:, m, tokens(t)], ident)
                    last.then_inc(s_x2T, 1)

            def turn_z2(tiles):
                for t in tiles:
                    pe.wait_ge(s_z2_ready, t + 1)
                    if t < CT:
                        bank = t
                        if t == 2:
                            pe.wait_ge(s_x2s_copied, CT)
                    else:
                        bank = 2 + t % 2
                        if t < 6:
                            pe.wait_ge(s_x2s_copied, TILES)
                        else:
                            pe.wait_ge(s_mod, TILES + t - 1)
                    for m in range(DK):
                        last = nc.tensor.transpose(ps[:, bank, m * P:(m + 1) * P], z2[:, t, m * P:(m + 1) * P], ident)
                    last.then_inc(s_z2T, 1)

            pe.wait_ge(s_x1_ready, 1)
            for t in range(CT):
                turn_z(t)
            pe.wait_ge(s_x1_ready, 2)
            for u in range(U + 1):
                if u < U:
                    proj1(u)
                if u == 1:
                    pe.wait_ge(s_xn1_ready, TILES)
                    pe.wait_ge(s_xT1_copied, TILES)
                if u >= 1:
                    pv1(u - 1, 0)
                    pv1(u - 1, 1)
                if u < U:
                    if u == 0:
                        pe.wait_ge(s_x1_ready, 4)
                    scores1(u)
                if u >= 1:
                    out1(u - 1, 0)
                    pv1(u - 1, 2)
                    out1(u - 1, 1)
                    pv1(u - 1, 3)
                    out1(u - 1, 2)
                    if u == U:
                        pe.wait_ge(s_s1_shifted, U)
                        turn_x2(0)
                    out1(u - 1, 3)
            pe.wait_ge(s_q1_copied, 12 * U)
            turn_z2(range(CT))

            def ffn_up(n):
                m, c = FFN[n]
                s = slice(c * BANK, (c + 1) * BANK)
                if c == 0:
                    pe.wait_ge(s_slice_lo, MI + m + 1)
                pe.wait_ge(s_xn3_ready, CT * (c + 1))
                if n >= 4:
                    pe.wait_ge(s_gelu, n - 3)
                split_mm(ps[:, 4 + n % 4, :], halves(parts_of(MI + m, m), 0, s)).then_inc(s_ffn_up, 1)

            def ffn_down(n):
                m, c = FFN[n]
                pe.wait_ge(s_glo, n + 1)
                hi, lo = parts_of(MI + m, m)
                for d in range(DK):
                    last = split_mm(ps[:, 2 * c + d, :], [(hi[:, DK + d, :], lo[:, DK + d, :],
                                                           w_hi2[:, n % 4, :], w_lo2[:, n % 4, :])],
                                    start=(m == 0), stop=(m == MM - 1))
                last.then_inc(s_ffn_down, 1)

            for n in range(NF + 2):
                if n == 3:
                    ffn_down(1)
                if n == 2:
                    pe.wait_ge(s_acc1, DK * U)
                if n < NF:
                    ffn_up(n)
                if n == 0:
                    turn_x2(1)
                if n == 1:
                    turn_z2((4, 5))
                if n == 2:
                    turn_z2((6, 7))
                if n >= 2 and n != 3:
                    ffn_down(n - 2)

            def logits1(c):
                pe.wait_ge(s_x4_ready, DK * (c + 1))
                for t in range(c * CT, (c + 1) * CT):
                    i = t - c * CT
                    for m in range(DK):
                        last = mm(ps[:, c, i * NE:(i + 1) * NE], xT[:, m, tokens(t)], r_w[:, m, :],
                                  start=(m == 0), stop=(m == DK - 1))
                    last.then_inc(s_rlog, 1)

            def turn_sel(c):
                pe.wait_ge(s_wsel, c + 1)
                for i in range(CT):
                    nc.tensor.transpose(ps[0:NE, c, i * P:(i + 1) * P], rt[:, 9, c * CT + i, :],
                                        ident).then_inc(s_selT_psum, 1)

            def lora_up(n):
                m, c = LORA[n]
                s = slice(c * BANK, (c + 1) * BANK)
                if n == c * MR:
                    pe.wait_ge(s_x4_split, DK * (c + 1))
                if n < MR:
                    pe.wait_ge(s_slice_lo, MI + MM + n + 1)
                else:
                    pe.wait_ge(s_up_copied, n - MR + 1)
                f, part = (MM, DK) if m == MR - 1 else (MM + m, 0)
                split_mm(ps[:, 4 + n % 4, :], halves(parts_of(MI + f, f), part, s)).then_inc(s_lora_up, 1)

            def lora_down(n):
                m, c = LORA[n]
                pe.wait_ge(s_hmk_ready, n + 1)
                rows = raw_t[:, 1, 2 * D:3 * D] if m == MR - 1 else raw_t[:, (MM + m) % SS, D:2 * D]
                for t in range(CT):
                    bank = (2 * c + t // 2 + 2) % 4
                    last = mm(ps[:, bank, (t % 2) * D:(t % 2 + 1) * D], hmk[:, n % 3, t * P:(t + 1) * P], rows,
                              start=(n % MR == 0 and t % 2 == 0), stop=(n % MR == MR - 1), skip_group_check=True)
                last.then_inc(s_hmk_used, 1)

            logits1(0)
            pe.wait_ge(s_gelu, NF)
            for n in range(NL):
                if n == 2:
                    logits1(1)
                if n == 3:
                    turn_sel(0)
                if n == MR + 1:
                    turn_sel(1)
                lora_up(n)
            for n in range(MR):
                lora_down(n)
            pe.wait_ge(s_selT_ready, CHUNKS)
            for n in range(MR, NL):
                lora_down(n)


def _by_row(a, n):
    return np.ascontiguousarray(a.reshape(n, P, -1).transpose(1, 0, 2))


def _columns(a):
    return a.reshape(-1, P).T


def _constants():
    freqs = (1.0 / np.float32(1000000.0) ** (np.arange(0, DH, 2, dtype=np.float32) / np.float32(DH))).astype(np.float32)
    angle = np.outer(np.arange(SEQ, dtype=np.float32), freqs).astype(np.float32)
    cos, sin = np.cos(angle), np.sin(angle)
    causal = np.where(np.tril(np.ones((SEQ, SEQ), bool)), 0.0, NEG)
    return np.concatenate([
        np.eye(P), np.tile(np.concatenate([cos, cos], 1), (BT, 1)), np.tile(np.concatenate([-sin, sin], 1), (BT, 1)),
        np.tile(causal, (BT, 1)), np.tile(np.arange(NE), (P, 1))], axis=1).astype(np.float32)


def kernel(**inputs):
    import concourse.bacc as bacc
    from concourse.bass_utils import run_bass_kernel_spmd

    a = {k: np.asarray(v) for k, v in inputs.items()}
    x = a["x"].reshape(TOK, D)
    qw, kw = a["L0_ffn_q_norm_w"], a["L0_ffn_k_norm_w"]
    turn = np.roll(np.arange(DH), -(DH // 2))
    rope_w = np.stack([qw, qw[turn], kw, kw[turn]])
    qkv_b = a["L1_cond_qkv_b"].reshape(3, HQ * DH)
    cols = np.concatenate([
        _by_row(a["cond_2048"].T, DK).reshape(P, -1), _columns(a["L0_cond_b"]), _columns(a["L0_ffn_attn_norm_w"]),
        _columns(a["L0_ffn_ffn_norm_w"]), _columns(a["L1_cond_ada_b"]), _columns(qkv_b[0]), _columns(qkv_b[1]),
        _columns(qkv_b[2]), _columns(a["L1_cond_out_b"]), _columns(a["L1_cond_ffn_b1"]), _columns(a["L1_cond_ffn_b2"]),
        np.broadcast_to(a["L1_ffn_br"], (P, NE))], axis=1)
    wqkv0 = np.concatenate([a["L0_ffn_q_w"], a["L0_ffn_k_w"], a["L0_ffn_v_w"]]).T
    wqkv1 = a["L1_cond_qkv_w"].reshape(DK, P, 3, GROUPS, BANK).transpose(3, 2, 1, 0, 4).reshape(GROUPS, 3, P, PIECE)
    wo1 = a["L1_cond_out_w"].reshape(GROUPS, 1, 4, P, D).transpose(0, 1, 3, 2, 4).reshape(GROUPS, 1, P, PIECE)

    def up_slices(w, n):
        return w.reshape(DK, P, n, P).transpose(2, 1, 0, 3).reshape(n, P, D)

    arrays = {
        "x_tok": _by_row(x, TILES),
        "x_T": _by_row(x.T, DK),
        "cond_T": _by_row(a["cond_2048"].T, DK),
        "cols": cols,
        "consts": _constants(),
        "rope_w": np.broadcast_to(rope_w, (P, 4, DH)),
        "w_qkv0": wqkv0.reshape(DK, P, NPROJ, BANK).transpose(2, 1, 0, 3).reshape(NPROJ, P, PIECE),
        "w_o0": _by_row(a["L0_ffn_o_w"].T, HQ),
        "w_gate0": _by_row(a["L0_ffn_gate_w"].T, DK),
        "w_moe": np.concatenate([
            up_slices(a["L0_ffn_wg"].reshape(EI, D).T, MI), up_slices(a["L0_ffn_wu"].reshape(EI, D).T, MI),
            a["L0_ffn_wd"].transpose(0, 2, 1).reshape(MI, P, D)], axis=2),
        "w_ada": _by_row(a["L1_cond_ada_w"], DK),
        "w_attn1": np.concatenate([wqkv1, wo1], axis=1).reshape(4 * GROUPS, P, PIECE),
        "w_ffn1": np.concatenate([up_slices(a["L1_cond_ffn_w1"], MM), a["L1_cond_ffn_w2"].reshape(MM, P, D)], axis=2),
        "w_lora": np.concatenate([up_slices(a["L1_ffn_A"].reshape(ER, D).T, MR),
                                  a["L1_ffn_B"].transpose(0, 2, 1).reshape(MR, P, D)], axis=2),
        "w_r": _by_row(a["L1_ffn_Wr"].T, DK),
    }
    arrays = {k: np.ascontiguousarray(v) for k, v in arrays.items()}
    nc = bacc.Bacc("TRN2", target_bir_lowering=False, num_devices=1)
    aps = {k: nc.dram_tensor("in_" + k, v.shape, mybir.dt.from_np(v.dtype), kind="ExternalInput").ap()
           for k, v in arrays.items()}
    out = nc.dram_tensor("out", (P, TILES, D), F32, kind="ExternalOutput").ap()
    build_program(nc, out=out, **aps)
    r = run_bass_kernel_spmd(nc, [{"in_" + k: v for k, v in arrays.items()}], core_ids=[0])
    got = r.results[0]["out"]
    return got.transpose(1, 0, 2).reshape(BATCH, SEQ, D)
```
